# Optimizing a Trainium2 kernel written in Bass

```python
import numpy as np
import jax
import jax.numpy as jnp

def _softmax(x, axis=-1):
    return jax.nn.softmax(x, axis=axis)

def _gelu(x):
    return jax.nn.gelu(x, approximate=True)

def _silu(x):
    return jax.nn.silu(x)

def _sigmoid(x):
    return jax.nn.sigmoid(x)

def _layernorm(x, axis=-1, eps=1e-05):
    m = jnp.mean(x, axis=axis, keepdims=True)
    v = jnp.var(x, axis=axis, keepdims=True)
    return (x - m) / jnp.sqrt(v + eps)

def _scatter_add(tgt, idx, src, axis=0):
    return tgt.at[idx].add(src)

def _segment_sum(src, seg, n):
    return jax.ops.segment_sum(src, seg, n)
kernel_name = 'mk_metaformer_d4_conv_nhwc256_r4_3f35fd'

def setup_inputs(seed: int=0):
    np.random.seed(seed)
    _w = jnp.asarray

    def _rec_inputs():
        import jax
        import jax.numpy as jnp
        _gk = jax.random.key(seed)
        x = -0.0003929 + 0.9999 * jax.random.normal(jax.random.fold_in(_gk, 1), (4, 32, 32, 64), jnp.float32)
        return x
    x = _rec_inputs()

    def _L0_conv_setup():
        import jax, jax.numpy as jnp
        import numpy as np
        D_MODEL = 64
        D_CONV = 4
        EXPAND = 2
        D_INNER = EXPAND * D_MODEL

        def silu(v):
            return v * jax.nn.sigmoid(v)
        key = jax.random.key(seed)
        k0, k1, k2, k3, k4 = jax.random.split(key, 5)
        B, H, W = (4, 32, 32)
        x = jax.random.normal(k0, (B, H, W, D_MODEL), jnp.float32)
        W_in = jax.random.normal(k1, (2 * D_INNER, D_MODEL), jnp.float32) * 0.02
        conv_w = jax.random.normal(k2, (D_INNER, 1, D_CONV), jnp.float32) * 0.1
        conv_b = jax.random.normal(k3, (D_INNER,), jnp.float32) * 0.02
        W_out = jax.random.normal(k4, (D_MODEL, D_INNER), jnp.float32) * 0.02
        return {'x': x, 'W_in': W_in, 'conv_w': conv_w, 'conv_b': conv_b, 'W_out': W_out}
    _L0_conv_all = _L0_conv_setup()
    _L0_conv_in = {k: v for k, v in _L0_conv_all.items() if k in ('W_in', 'conv_w', 'conv_b', 'W_out')}
    del _L0_conv_all

    def _L0_ffn_setup():
        import jax, jax.numpy as jnp
        import numpy as np
        TOP_K = 2
        key = jax.random.key(seed)
        ks = jax.random.split(key, 4)
        B, L, D, H, E = (8, 1024, 64, 256, 8)
        s = 0.02
        return {'x': jax.random.normal(ks[0], (B, L, D), jnp.float32), 'Wg': jax.random.normal(ks[1], (D, E), jnp.float32) * s, 'bg': jnp.zeros((E,), jnp.float32), 'W1': jax.random.normal(ks[2], (E, D, H), jnp.float32) * s, 'b1': jnp.zeros((E, H), jnp.float32), 'W2': jax.random.normal(ks[3], (E, H, D), jnp.float32) * s, 'b2': jnp.zeros((E, D), jnp.float32)}
    _L0_ffn_all = _L0_ffn_setup()
    _L0_ffn_in = {k: v for k, v in _L0_ffn_all.items() if k in ('Wg', 'bg', 'W1', 'b1', 'W2', 'b2')}
    del _L0_ffn_all

    def _L1_conv_setup():
        import jax, jax.numpy as jnp
        import numpy as np
        _QMAX = 127.0

        def _quantize(x, axes):
            amax = jnp.max(jnp.abs(x), axis=axes, keepdims=True)
            scale = jnp.maximum(amax, 1e-06) / _QMAX
            q = jnp.clip(jnp.round(x / scale), -_QMAX, _QMAX)
            return (q, scale)
        key = jax.random.key(seed)
        k1, k2 = jax.random.split(key)
        lhs = jax.random.normal(k1, (32, 56, 56, 64), dtype=jnp.float32)
        rhs = jax.random.normal(k2, (3, 3, 64, 64), dtype=jnp.float32)
        return {'lhs': lhs, 'rhs': rhs}
    _L1_conv_all = _L1_conv_setup()
    _L1_conv_in = {k: v for k, v in _L1_conv_all.items() if k in ('rhs',)}
    del _L1_conv_all

    def _L1_ffn_setup():
        import math
        import jax, jax.numpy as jnp
        import numpy as np
        CAPACITY_FACTOR = 1.25
        TOP_K = 2
        LN_EPS = 1e-05

        def _layer_norm(x, gamma, beta):
            mu = jnp.mean(x, axis=-1, keepdims=True)
            var = jnp.var(x, axis=-1, keepdims=True)
            return (x - mu) * jax.lax.rsqrt(var + LN_EPS) * gamma + beta
        key = jax.random.key(seed)
        ks = jax.random.split(key, 4)
        B, S, D, F, E = (8, 1024, 64, 128, 8)
        x = jax.random.normal(ks[0], (B, S, D), dtype=jnp.float32)
        Wr = jax.random.normal(ks[1], (D, E), dtype=jnp.float32) / np.sqrt(D)
        br = jnp.zeros((E,), jnp.float32)
        W1 = jax.random.normal(ks[2], (E, D, F), dtype=jnp.float32) / np.sqrt(D)
        b1 = jnp.zeros((E, F), jnp.float32)
        W2 = jax.random.normal(ks[3], (E, F, D), dtype=jnp.float32) / np.sqrt(F)
        b2 = jnp.zeros((E, D), jnp.float32)
        gamma = jnp.ones((D,), jnp.float32)
        beta = jnp.zeros((D,), jnp.float32)
        return {'x': x, 'Wr': Wr, 'br': br, 'W1': W1, 'b1': b1, 'W2': W2, 'b2': b2, 'gamma': gamma, 'beta': beta}
    _L1_ffn_all = _L1_ffn_setup()
    _L1_ffn_in = {k: v for k, v in _L1_ffn_all.items() if k in ('Wr', 'br', 'W1', 'b1', 'W2', 'b2', 'gamma', 'beta')}
    del _L1_ffn_all

    def _L2_conv_setup():
        import jax, jax.numpy as jnp
        import numpy as np
        key = jax.random.key(seed)
        k1, k2, k3 = jax.random.split(key, 3)
        B, H, W, C, R = (32, 56, 56, 64, 16)
        x = jax.random.normal(k1, (B, H, W, C), dtype=jnp.float32)
        w1 = jax.random.normal(k2, (C, C // R), dtype=jnp.float32) * (1.0 / np.sqrt(C))
        b1 = jnp.zeros((C // R,), dtype=jnp.float32)
        w2 = jax.random.normal(k3, (C // R, C), dtype=jnp.float32) * (1.0 / np.sqrt(C // R))
        b2 = jnp.zeros((C,), dtype=jnp.float32)
        return {'x': x, 'w1': w1, 'b1': b1, 'w2': w2, 'b2': b2}
    _L2_conv_all = _L2_conv_setup()
    _L2_conv_in = {k: v for k, v in _L2_conv_all.items() if k in ('w1', 'b1', 'w2', 'b2')}
    del _L2_conv_all

    def _L2_ffn_setup():
        import jax, jax.numpy as jnp
        import numpy as np
        B, N, D = (16, 1024, 64)
        NUM_EXPERTS, TOP_K, HEADS = (4, 2, 4)
        N_EDGES = 262144
        LN_EPS = 1e-05

        def _layernorm(x, g, b):
            mu = x.mean(-1, keepdims=True)
            var = ((x - mu) ** 2).mean(-1, keepdims=True)
            return (x - mu) * jax.lax.rsqrt(var + LN_EPS) * g + b

        def _forward(x, edge_index, W_gat, att_src, att_dst, b_gat, ln_gamma, ln_beta, W1, b1, W2, b2):
            Bc, Nc, Dc = x.shape
            M = Bc * Nc
            x_flat = x.reshape(M, Dc)
            h = (x_flat @ W_gat).reshape(M, HEADS, NUM_EXPERTS)
            loops = jnp.arange(M, dtype=edge_index.dtype)
            src = jnp.concatenate([edge_index[0], loops])
            dst = jnp.concatenate([edge_index[1], loops])
            a_src = (h * att_src).sum(-1)
            a_dst = (h * att_dst).sum(-1)
            e = jax.nn.leaky_relu(a_src[src] + a_dst[dst], negative_slope=0.2)
            e_max = jax.ops.segment_max(e, dst, num_segments=M)
            ee = jnp.exp(e - e_max[dst])
            denom = jax.ops.segment_sum(ee, dst, num_segments=M)
            alpha = ee / (denom[dst] + 1e-16)
            msg = h[src] * alpha[:, :, None]
            agg = jax.ops.segment_sum(msg, dst, num_segments=M).reshape(M, HEADS * NUM_EXPERTS) + b_gat
            scores = _layernorm(agg, ln_gamma, ln_beta).reshape(M, HEADS, NUM_EXPERTS).mean(1)
            scores = scores.reshape(Bc, Nc, NUM_EXPERTS)
            topk_s, topk_i = jax.lax.top_k(scores, TOP_K)
            w = jax.nn.softmax(topk_s, axis=-1)
            out = jnp.zeros_like(x)
            for ei in range(NUM_EXPERTS):
                g = jnp.where(topk_i == ei, w, 0.0).sum(-1)
                hh = jax.nn.gelu(x @ W1[ei] + b1[ei], approximate=False)
                out = out + g[..., None] * (hh @ W2[ei] + b2[ei])
            return out
        key = jax.random.key(seed)
        ks = jax.random.split(key, 8)
        s = 0.05
        return {'x': jax.random.normal(ks[0], (B, N, D), jnp.float32), 'W_gat': jax.random.normal(ks[1], (D, HEADS * NUM_EXPERTS), jnp.float32) * s, 'att_src': jax.random.normal(ks[2], (HEADS, NUM_EXPERTS), jnp.float32) * s, 'att_dst': jax.random.normal(ks[3], (HEADS, NUM_EXPERTS), jnp.float32) * s, 'b_gat': jnp.zeros((HEADS * NUM_EXPERTS,), jnp.float32), 'ln_gamma': jnp.ones((HEADS * NUM_EXPERTS,), jnp.float32), 'ln_beta': jnp.zeros((HEADS * NUM_EXPERTS,), jnp.float32), 'W1': jax.random.normal(ks[4], (NUM_EXPERTS, D, 2 * D), jnp.float32) * s, 'b1': jnp.zeros((NUM_EXPERTS, 2 * D), jnp.float32), 'W2': jax.random.normal(ks[5], (NUM_EXPERTS, 2 * D, D), jnp.float32) * s, 'b2': jnp.zeros((NUM_EXPERTS, D), jnp.float32), 'edge_index': jax.random.randint(ks[6], (2, N_EDGES), 0, B * N, jnp.int32)}
    _L2_ffn_all = _L2_ffn_setup()
    _L2_ffn_in = {k: v for k, v in _L2_ffn_all.items() if k in ('W_gat', 'att_src', 'att_dst', 'b_gat', 'ln_gamma', 'ln_beta', 'W1', 'b1', 'W2', 'b2', 'edge_index')}
    del _L2_ffn_all

    def _L3_conv_setup():
        import jax, jax.numpy as jnp
        import numpy as np
        DB4 = np.array([0.23037781330885523, 0.7148465705525415, 0.6308807679295904, -0.02798376941698385, -0.18703481171888114, 0.030841381835986965, 0.032883011666982945, -0.010597401784997278], dtype=np.float32)

        def _corr_valid(u, f):
            L = f.shape[0]
            B = int(np.prod(u.shape[:-1]))
            out = jax.lax.conv_general_dilated(u.reshape(B, 1, u.shape[-1]), f.reshape(1, 1, L), window_strides=(1,), padding='VALID', dimension_numbers=('NCW', 'OIW', 'NCW'))
            return out.reshape(u.shape[:-1] + (out.shape[-1],))

        def _recon_axis(s, w, h0, h1, axis):
            L = h0.shape[0]
            P = (L - 2) // 2 + 1
            x = jnp.stack([s, w])
            x = jnp.moveaxis(x, axis + 1, -1)
            N = x.shape[-1]
            x = jnp.concatenate([x[..., N - P:], x], axis=-1)[..., 1:]
            up = jnp.stack([jnp.zeros_like(x), x], axis=-1).reshape(x.shape[:-1] + (-1,))
            up = jnp.pad(up, [(0, 0)] * (up.ndim - 1) + [(0, 1)])
            y = _corr_valid(up[0], h0) + _corr_valid(up[1], h1)
            return jnp.moveaxis(y, -1, axis)
        key = jax.random.key(seed)
        x = jax.random.normal(key, (4, 64, 64, 64), dtype=jnp.float32)
        h = jnp.asarray(DB4)
        return {'x': x, 'h': h}
    _L3_conv_all = _L3_conv_setup()
    _L3_conv_in = {k: v for k, v in _L3_conv_all.items() if k in ('h',)}
    del _L3_conv_all

    def _L3_ffn_setup():
        import jax, jax.numpy as jnp
        import numpy as np
        N_EXPERTS = 8
        TOP_K = 2
        key = jax.random.key(seed)
        ks = jax.random.split(key, 5)
        B, T, C, E, H = (8, 512, 64, 8, 682)
        scale = 1.0 / np.sqrt(C)
        return {'x': jax.random.normal(ks[0], (B, T, C), dtype=jnp.float32), 'router_w': jax.random.normal(ks[1], (E, C), dtype=jnp.float32) * scale, 'w1': jax.random.normal(ks[2], (E, H, C), dtype=jnp.float32) * scale, 'w2': jax.random.normal(ks[3], (E, C, H), dtype=jnp.float32) * (1.0 / np.sqrt(H)), 'w3': jax.random.normal(ks[4], (E, H, C), dtype=jnp.float32) * scale}
    _L3_ffn_all = _L3_ffn_setup()
    _L3_ffn_in = {k: v for k, v in _L3_ffn_all.items() if k in ('router_w', 'w1', 'w2', 'w3')}
    del _L3_ffn_all
    return {'x': x, 'L0_conv_W_in': _L0_conv_in['W_in'], 'L0_conv_conv_w': _L0_conv_in['conv_w'], 'L0_conv_conv_b': _L0_conv_in['conv_b'], 'L0_conv_W_out': _L0_conv_in['W_out'], 'L0_ffn_Wg': _L0_ffn_in['Wg'], 'L0_ffn_bg': _L0_ffn_in['bg'], 'L0_ffn_W1': _L0_ffn_in['W1'], 'L0_ffn_b1': _L0_ffn_in['b1'], 'L0_ffn_W2': _L0_ffn_in['W2'], 'L0_ffn_b2': _L0_ffn_in['b2'], 'L1_conv_rhs': _L1_conv_in['rhs'], 'L1_ffn_Wr': _L1_ffn_in['Wr'], 'L1_ffn_br': _L1_ffn_in['br'], 'L1_ffn_W1': _L1_ffn_in['W1'], 'L1_ffn_b1': _L1_ffn_in['b1'], 'L1_ffn_W2': _L1_ffn_in['W2'], 'L1_ffn_b2': _L1_ffn_in['b2'], 'L1_ffn_gamma': _L1_ffn_in['gamma'], 'L1_ffn_beta': _L1_ffn_in['beta'], 'L2_conv_w1': _L2_conv_in['w1'], 'L2_conv_b1': _L2_conv_in['b1'], 'L2_conv_w2': _L2_conv_in['w2'], 'L2_conv_b2': _L2_conv_in['b2'], 'L2_ffn_W_gat': _L2_ffn_in['W_gat'], 'L2_ffn_att_src': _L2_ffn_in['att_src'], 'L2_ffn_att_dst': _L2_ffn_in['att_dst'], 'L2_ffn_b_gat': _L2_ffn_in['b_gat'], 'L2_ffn_ln_gamma': _L2_ffn_in['ln_gamma'], 'L2_ffn_ln_beta': _L2_ffn_in['ln_beta'], 'L2_ffn_W1': _L2_ffn_in['W1'], 'L2_ffn_b1': _L2_ffn_in['b1'], 'L2_ffn_W2': _L2_ffn_in['W2'], 'L2_ffn_b2': _L2_ffn_in['b2'], 'L2_ffn_edge_index': _L2_ffn_in['edge_index'], 'L3_conv_h': _L3_conv_in['h'], 'L3_ffn_router_w': _L3_ffn_in['router_w'], 'L3_ffn_w1': _L3_ffn_in['w1'], 'L3_ffn_w2': _L3_ffn_in['w2'], 'L3_ffn_w3': _L3_ffn_in['w3']}

def reference(x, L0_conv_W_in, L0_conv_conv_w, L0_conv_conv_b, L0_conv_W_out, L0_ffn_Wg, L0_ffn_bg, L0_ffn_W1, L0_ffn_b1, L0_ffn_W2, L0_ffn_b2, L1_conv_rhs, L1_ffn_Wr, L1_ffn_br, L1_ffn_W1, L1_ffn_b1, L1_ffn_W2, L1_ffn_b2, L1_ffn_gamma, L1_ffn_beta, L2_conv_w1, L2_conv_b1, L2_conv_w2, L2_conv_b2, L2_ffn_W_gat, L2_ffn_att_src, L2_ffn_att_dst, L2_ffn_b_gat, L2_ffn_ln_gamma, L2_ffn_ln_beta, L2_ffn_W1, L2_ffn_b1, L2_ffn_W2, L2_ffn_b2, L2_ffn_edge_index, L3_conv_h, L3_ffn_router_w, L3_ffn_w1, L3_ffn_w2, L3_ffn_w3):
    import jax
    import jax.numpy as jnp

    def _L0_conv_ref(x, W_in, conv_w, conv_b, W_out):
        import jax, jax.numpy as jnp
        import numpy as np
        D_MODEL = 64
        D_CONV = 4
        EXPAND = 2
        D_INNER = EXPAND * D_MODEL

        def silu(v):
            return v * jax.nn.sigmoid(v)
        B, H, W, C = x.shape
        L = H * W
        x_flat = x.reshape(B, L, C)
        xz = jnp.einsum('blc,dc->bld', x_flat, W_in)
        x_branch, z_branch = jnp.split(xz, 2, axis=-1)
        u = jax.lax.conv_general_dilated(x_branch.transpose(0, 2, 1), conv_w, window_strides=(1,), padding=[(D_CONV - 1, 0)], dimension_numbers=('NCH', 'OIH', 'NCH'), feature_group_count=D_INNER)
        u = (u + conv_b[None, :, None]).transpose(0, 2, 1)
        u = silu(u)
        y1 = u
        y2 = jnp.flip(jnp.flip(u, axis=1), axis=1)
        u_t = u.reshape(B, H, W, -1).transpose(0, 2, 1, 3).reshape(B, L, -1)
        y3 = u_t.reshape(B, W, H, -1).transpose(0, 2, 1, 3).reshape(B, L, -1)
        y4 = jnp.flip(jnp.flip(u_t, axis=1), axis=1).reshape(B, W, H, -1).transpose(0, 2, 1, 3).reshape(B, L, -1)
        y = (y1 + y2 + y3 + y4) * silu(z_branch)
        out = jnp.einsum('bld,cd->blc', y, W_out)
        return out.reshape(B, H, W, C)

    def _L0_ffn_ref(x, Wg, bg, W1, b1, W2, b2):
        import jax, jax.numpy as jnp
        import numpy as np
        TOP_K = 2
        B, L, D = x.shape
        E = W1.shape[0]
        xf = x.reshape(-1, D)
        gate_logits = xf @ Wg + bg
        top_w, top_i = jax.lax.top_k(gate_logits, TOP_K)
        top_w = jax.nn.softmax(top_w, axis=-1)
        w_dense = jnp.sum(jax.nn.one_hot(top_i, E, dtype=xf.dtype) * top_w[..., None], axis=1)
        out = jnp.zeros_like(xf)
        for e in range(E):
            h = jax.nn.gelu(xf @ W1[e] + b1[e], approximate=False)
            out = out + w_dense[:, e:e + 1] * (h @ W2[e] + b2[e])
        return out.reshape(B, L, D)

    def _L1_conv_ref(lhs, rhs):
        import jax, jax.numpy as jnp
        import numpy as np
        _QMAX = 127.0

        def _quantize(x, axes):
            amax = jnp.max(jnp.abs(x), axis=axes, keepdims=True)
            scale = jnp.maximum(amax, 1e-06) / _QMAX
            q = jnp.clip(jnp.round(x / scale), -_QMAX, _QMAX)
            return (q, scale)
        qlhs, s_lhs = _quantize(lhs, axes=(1, 2, 3))
        qrhs, s_rhs = _quantize(rhs, axes=(0, 1, 2))
        dn = jax.lax.conv_dimension_numbers(lhs.shape, rhs.shape, ('NHWC', 'HWIO', 'NHWC'))
        out = jax.lax.conv_general_dilated(qlhs, qrhs, window_strides=(1, 1), padding='SAME', dimension_numbers=dn, feature_group_count=1, batch_group_count=1, preferred_element_type=jnp.float32)
        return out * s_lhs * s_rhs.reshape(1, 1, 1, -1)

    def _L1_ffn_ref(x, Wr, br, W1, b1, W2, b2, gamma, beta):
        import math
        import jax, jax.numpy as jnp
        import numpy as np
        CAPACITY_FACTOR = 1.25
        TOP_K = 2
        LN_EPS = 1e-05

        def _layer_norm(x, gamma, beta):
            mu = jnp.mean(x, axis=-1, keepdims=True)
            var = jnp.var(x, axis=-1, keepdims=True)
            return (x - mu) * jax.lax.rsqrt(var + LN_EPS) * gamma + beta
        B, S, D = x.shape
        E = Wr.shape[1]
        N = B * S
        K = TOP_K
        logits = jnp.mean(x, axis=1) @ Wr + br
        routing_weights = jax.nn.softmax(logits, axis=-1)
        capacity = float(math.ceil(N * CAPACITY_FACTOR / E))
        expected_loads = routing_weights.sum(axis=0) * (N / B)
        scale = jnp.where(expected_loads > capacity, capacity / expected_loads, 1.0)
        routing_weights = jax.nn.softmax(routing_weights * scale, axis=-1)
        rw_tok = jnp.broadcast_to(routing_weights[:, None, :], (B, S, E)).reshape(N, E)
        top_w, top_i = jax.lax.top_k(rw_tok, K)
        top_w = jax.nn.softmax(top_w, axis=-1)
        xf = x.reshape(N, D)
        h = jax.nn.gelu(jnp.einsum('nd,edf->enf', xf, W1) + b1[:, None, :], approximate=False)
        y = jnp.einsum('enf,efd->end', h, W2) + b2[:, None, :]
        w_dense = jnp.zeros((N, E), x.dtype).at[jnp.arange(N)[:, None], top_i].add(top_w)
        out = jnp.einsum('ne,end->nd', w_dense, y).reshape(B, S, D)
        out = _layer_norm(out + x, gamma, beta)
        return out

    def _L2_conv_ref(x, w1, b1, w2, b2):
        import jax, jax.numpy as jnp
        import numpy as np
        s = jnp.mean(x, axis=(1, 2))
        h = jax.nn.relu(s @ w1 + b1)
        g = jax.nn.sigmoid(h @ w2 + b2)
        return x * g[:, None, None, :]

    def _L2_ffn_ref(x, W_gat, att_src, att_dst, b_gat, ln_gamma, ln_beta, W1, b1, W2, b2, edge_index):
        import jax, jax.numpy as jnp
        import numpy as np
        B, N, D = (16, 1024, 64)
        NUM_EXPERTS, TOP_K, HEADS = (4, 2, 4)
        N_EDGES = 262144
        LN_EPS = 1e-05

        def _layernorm(x, g, b):
            mu = x.mean(-1, keepdims=True)
            var = ((x - mu) ** 2).mean(-1, keepdims=True)
            return (x - mu) * jax.lax.rsqrt(var + LN_EPS) * g + b

        def _forward(x, edge_index, W_gat, att_src, att_dst, b_gat, ln_gamma, ln_beta, W1, b1, W2, b2):
            Bc, Nc, Dc = x.shape
            M = Bc * Nc
            x_flat = x.reshape(M, Dc)
            h = (x_flat @ W_gat).reshape(M, HEADS, NUM_EXPERTS)
            loops = jnp.arange(M, dtype=edge_index.dtype)
            src = jnp.concatenate([edge_index[0], loops])
            dst = jnp.concatenate([edge_index[1], loops])
            a_src = (h * att_src).sum(-1)
            a_dst = (h * att_dst).sum(-1)
            e = jax.nn.leaky_relu(a_src[src] + a_dst[dst], negative_slope=0.2)
            e_max = jax.ops.segment_max(e, dst, num_segments=M)
            ee = jnp.exp(e - e_max[dst])
            denom = jax.ops.segment_sum(ee, dst, num_segments=M)
            alpha = ee / (denom[dst] + 1e-16)
            msg = h[src] * alpha[:, :, None]
            agg = jax.ops.segment_sum(msg, dst, num_segments=M).reshape(M, HEADS * NUM_EXPERTS) + b_gat
            scores = _layernorm(agg, ln_gamma, ln_beta).reshape(M, HEADS, NUM_EXPERTS).mean(1)
            scores = scores.reshape(Bc, Nc, NUM_EXPERTS)
            topk_s, topk_i = jax.lax.top_k(scores, TOP_K)
            w = jax.nn.softmax(topk_s, axis=-1)
            out = jnp.zeros_like(x)
            for ei in range(NUM_EXPERTS):
                g = jnp.where(topk_i == ei, w, 0.0).sum(-1)
                hh = jax.nn.gelu(x @ W1[ei] + b1[ei], approximate=False)
                out = out + g[..., None] * (hh @ W2[ei] + b2[ei])
            return out
        return _forward(x, edge_index, W_gat, att_src, att_dst, b_gat, ln_gamma, ln_beta, W1, b1, W2, b2)

    def _L3_conv_ref(x, h):
        import jax, jax.numpy as jnp
        import numpy as np
        DB4 = np.array([0.23037781330885523, 0.7148465705525415, 0.6308807679295904, -0.02798376941698385, -0.18703481171888114, 0.030841381835986965, 0.032883011666982945, -0.010597401784997278], dtype=np.float32)

        def _corr_valid(u, f):
            L = f.shape[0]
            B = int(np.prod(u.shape[:-1]))
            out = jax.lax.conv_general_dilated(u.reshape(B, 1, u.shape[-1]), f.reshape(1, 1, L), window_strides=(1,), padding='VALID', dimension_numbers=('NCW', 'OIW', 'NCW'))
            return out.reshape(u.shape[:-1] + (out.shape[-1],))

        def _recon_axis(s, w, h0, h1, axis):
            L = h0.shape[0]
            P = (L - 2) // 2 + 1
            x = jnp.stack([s, w])
            x = jnp.moveaxis(x, axis + 1, -1)
            N = x.shape[-1]
            x = jnp.concatenate([x[..., N - P:], x], axis=-1)[..., 1:]
            up = jnp.stack([jnp.zeros_like(x), x], axis=-1).reshape(x.shape[:-1] + (-1,))
            up = jnp.pad(up, [(0, 0)] * (up.ndim - 1) + [(0, 1)])
            y = _corr_valid(up[0], h0) + _corr_valid(up[1], h1)
            return jnp.moveaxis(y, -1, axis)
        h0 = h[::-1]
        sign = jnp.where(jnp.arange(h.shape[0]) % 2 == 0, -1.0, 1.0).astype(h.dtype)
        h1 = sign * h
        out = x
        for axis in range(1, x.ndim):
            s, w = jnp.split(out, 2, axis=axis)
            out = _recon_axis(s, w, h0, h1, axis)
        return out

    def _L3_ffn_ref(x, router_w, w1, w2, w3):
        import jax, jax.numpy as jnp
        import numpy as np
        N_EXPERTS = 8
        TOP_K = 2
        B, T, C = x.shape
        flat = x.reshape(-1, C)
        logits = flat @ router_w.T
        probs = jax.nn.softmax(logits, axis=-1)
        topk_probs, topk_idx = jax.lax.top_k(probs, TOP_K)
        topk_probs = topk_probs / (jnp.sum(topk_probs, axis=-1, keepdims=True) + 1e-09)
        onehot = jax.nn.one_hot(topk_idx, N_EXPERTS, dtype=flat.dtype)
        gates = jnp.einsum('nk,nke->ne', topk_probs, onehot)
        h1 = jnp.einsum('nc,ehc->neh', flat, w1)
        h3 = jnp.einsum('nc,ehc->neh', flat, w3)
        h = jax.nn.silu(h1) * h3
        y = jnp.einsum('neh,ech->nec', h, w2)
        out = jnp.einsum('ne,nec->nc', gates, y)
        return out.reshape(B, T, C)

    def _gn(v, G=32, eps=1e-05):
        B_, H_, W_, C_ = v.shape
        g = v.reshape(B_, H_, W_, G, C_ // G)
        m = jnp.mean(g, axis=(1, 2, 4), keepdims=True)
        s = jnp.var(g, axis=(1, 2, 4), keepdims=True)
        return ((g - m) / jnp.sqrt(s + eps)).reshape(v.shape)

    def _ln_c(v, eps=1e-06):
        m = jnp.mean(v, axis=-1, keepdims=True)
        s = jnp.var(v, axis=-1, keepdims=True)
        return (v - m) / jnp.sqrt(s + eps)

    def _ln_t(v, eps=1e-05):
        m = jnp.mean(v, axis=-1, keepdims=True)
        s = jnp.var(v, axis=-1, keepdims=True)
        return (v - m) / jnp.sqrt(s + eps)

    def _to_tokens(v):
        B_, H_, W_, C_ = v.shape
        return v.reshape(B_, H_ * W_, C_)

    def _from_tokens(t, like):
        return t.reshape(like.shape)
    x = x + _L0_conv_ref(_ln_c(x), L0_conv_W_in, L0_conv_conv_w, L0_conv_conv_b, L0_conv_W_out)
    t = _to_tokens(x)
    t = t + _L0_ffn_ref(_ln_t(t), L0_ffn_Wg, L0_ffn_bg, L0_ffn_W1, L0_ffn_b1, L0_ffn_W2, L0_ffn_b2)
    x = _from_tokens(t, x)
    x = x + _L1_conv_ref(_ln_c(x), L1_conv_rhs)
    t = _to_tokens(x)
    t = t + _L1_ffn_ref(_ln_t(t), L1_ffn_Wr, L1_ffn_br, L1_ffn_W1, L1_ffn_b1, L1_ffn_W2, L1_ffn_b2, L1_ffn_gamma, L1_ffn_beta)
    x = _from_tokens(t, x)
    x = x + _L2_conv_ref(_ln_c(x), L2_conv_w1, L2_conv_b1, L2_conv_w2, L2_conv_b2)
    t = _to_tokens(x)
    t = t + _L2_ffn_ref(_ln_t(t), L2_ffn_W_gat, L2_ffn_att_src, L2_ffn_att_dst, L2_ffn_b_gat, L2_ffn_ln_gamma, L2_ffn_ln_beta, L2_ffn_W1, L2_ffn_b1, L2_ffn_W2, L2_ffn_b2, L2_ffn_edge_index)
    x = _from_tokens(t, x)
    x = x + _L3_conv_ref(_ln_c(x), L3_conv_h)
    t = _to_tokens(x)
    t = t + _L3_ffn_ref(_ln_t(t), L3_ffn_router_w, L3_ffn_w1, L3_ffn_w2, L3_ffn_w3)
    x = _from_tokens(t, x)
    return x

_drawn_inputs = setup_inputs


def setup_inputs(seed=0):
    import zlib

    import numpy as np

    out = dict(_drawn_inputs(seed))
    spreads = {'L0_ffn_bg': (0.0, 0.1),
     'L0_ffn_b1': (0.0, 0.411),
     'L0_ffn_b2': (0.0, 0.1),
     'L1_ffn_br': (0.0, 0.489),
     'L1_ffn_b1': (0.0, 0.8),
     'L1_ffn_b2': (0.0, 2.0),
     'L1_ffn_gamma': (1.0, 0.6),
     'L1_ffn_beta': (0.0, 0.8),
     'L2_conv_b1': (0.0, 0.8),
     'L2_conv_b2': (0.0, 2.0),
     'L2_ffn_b_gat': (0.0, 0.8),
     'L2_ffn_ln_gamma': (1.0, 0.6),
     'L2_ffn_ln_beta': (0.0, 0.8),
     'L2_ffn_b1': (0.0, 0.8),
     'L2_ffn_b2': (0.0, 0.8)}
    factors = {'L0_conv_W_in': 8.0,
     'L0_conv_conv_w': 8.0,
     'L0_conv_conv_b': 8.0,
     'L0_conv_W_out': 8.0,
     'L0_ffn_W1': 2.685,
     'L1_ffn_Wr': 4.01,
     'L1_ffn_W1': 3.876,
     'L1_ffn_W2': 3.435,
     'L2_conv_w1': 8.0,
     'L2_conv_w2': 8.0,
     'L2_ffn_W_gat': 8.0,
     'L2_ffn_att_src': 8.0,
     'L2_ffn_att_dst': 8.0,
     'L2_ffn_W1': 8.0,
     'L2_ffn_W2': 8.0,
     'L3_ffn_router_w': 3.627,
     'L3_ffn_w1': 3.387,
     'L3_ffn_w2': 3.186,
     'L3_ffn_w3': 3.176}
    for name, (base, spread) in spreads.items():
        noise = np.random.default_rng([zlib.crc32(name.encode()), seed]).standard_normal(out[name].shape)
        drawn = base * np.exp(spread * noise) if base else spread * noise
        out[name] = jnp.asarray(drawn.astype(out[name].dtype))
    for name, factor in factors.items():
        out[name] = (out[name] * factor).astype(out[name].dtype)
    return out
```

```python
from contextlib import ExitStack

import concourse.bass as bass
from concourse import mybir

F32 = mybir.dt.float32
BF16 = mybir.dt.bfloat16
F16 = mybir.dt.float16
I32 = mybir.dt.int32
U32 = mybir.dt.uint32
ALU = mybir.AluOpType
ACT = mybir.ActivationFunctionType
AX = mybir.AxisListType
RMAX = bass.bass_isa.ReduceOp.max

P = 128
B, H, W, C = 4, 32, 32, 64
NT = W
GT = 4
NG = NT // GT
L = H * W
GN = GT * P

DI = 2 * C
TAPS = 4
XW = (NT + TAPS - 1) * P

L0F = (8, 128, 2)
L1F = (8, 128, 1)
L2F = (4, 128, 1)
L3F = (8, 114, 6)
MOES = [L0F, L1F, L2F, L3F]
CHUNK0 = [NG * sum(e * f for e, _, f in MOES[:m]) for m in range(5)]
UNIT0 = [NG * sum(e for e, _, _ in MOES[:m]) for m in range(5)]

HEADS, HK = 4, 4
N_EDGES = 262144
NODES = B * H * W
EPP = N_EDGES // P
SEG = 512
NSEG = EPP // SEG
TOP = 8
MAXR = SEG // TOP
COMMON_ROUNDS = 24
UNROLL = 8
BLK = TOP
NBLK = EPP // BLK
SUPER = 16
EDGE_STEPS = 2 * 14
SRCW = 2 * HEADS + HEADS * HK
DSTW = 2 * HEADS
MSG = HEADS * HK + HEADS
PAD = W + 2
CAPACITY = -(-NODES * 5 // (4 * 8))
QMAX = 127.0
ROUND = 1.5 * 2.0 ** 23
FT = 8
X_SCALE, W_SCALE = 32.0, 64.0
UNSCALE = 1.0 / (X_SCALE * W_SCALE)
UP3 = 2 * 8 * 684
PIECES = 6
PIECE = UP3 // PIECES


class Steps:

    def __init__(self, eng, sem):
        self.eng, self.sem, self.at, self.i, self.per, self.first = eng, sem, 0, None, 0, 0

    def __call__(self, ins):
        ins.then_inc(self.sem, 1)
        self.at += 1
        self.eng.wait_ge(self.sem, self.at if self.i is None else self.i * self.per + self.at)

    def enter(self, i, per):
        self.i, self.per, self.first = i, per, self.at

    def leave(self, times):
        assert self.at - self.first == self.per, (self.at - self.first, self.per)
        self.at = self.first + times * self.per
        self.i = None


def settle(eng, sem):
    eng.sem_inc(sem, 1)


def build_program(nc, a, out):
    ctx = ExitStack()

    def sb(name, shape, dt=F32):
        return ctx.enter_context(nc.sbuf_tensor(name, shape, dt))

    def sem(name):
        return ctx.enter_context(nc.semaphore(name))

    with ctx:
        X = sb("X", [P, NT, C])
        XC = sb("XC", [P, NT, C])
        Y = sb("Y", [P, NT, C])
        SQ = sb("SQ", [P, NT, C])
        ACC = sb("ACC", [P, NT, C])
        yT = sb("yT", [P, NT * P], F16)
        yg = sb("yg", [P, 2, GT, 2, C], F16)
        ygf = sb("ygf", [P, 2, GT, C])
        hS = sb("hS", [P, 12, GN])
        arena = sb("arena", [P, 12288])
        keys = sb("keys", [P, EPP + TOP * UNROLL])
        sil = sb("sil", [P, 2, GN])
        comb = sb("comb", [P, 2, GT, C])
        ident = sb("ident", [P, P])
        identb = sb("identb", [P, P], BF16)
        identh = sb("identh", [P, P], F16)
        ones = sb("ones", [P, P])
        blk32 = sb("blk32", [P, B])
        iotaP = sb("iotaP", [P, P])
        iotaW = sb("iotaW", [P, W])
        lnsum = sb("lnsum", [P, NT])
        lnneg = sb("lnneg", [P, NT])
        lnvar = sb("lnvar", [P, NT])
        lnsd = sb("lnsd", [P, NT])
        rstd = sb("rstd", [P, NT])
        logit = sb("logit", [P, NT, 16])
        gate = sb("gate", [P, NT, 8])
        gex = sb("gex", [P, NT, 8])
        gsum = sb("gsum", [P, 4, NT])
        gst = sb("gst", [P, GT * 8])
        gTs = sb("gTs", [GT * 8, P])
        small = sb("small", [P, 256])
        w0in = sb("w0in", [P, 2, 2 * DI], F16)
        w0out = sb("w0out", [DI, C])
        c0w = sb("c0w", [DI, TAPS])
        c0b = sb("c0b", [DI, 1])
        gw1 = sb("gw1", [C, 8])
        gwp = {m: sb(f"gwp{m}", [P, 2, n], F16) for m, n in ((0, 8), (2, 16), (3, 8))}
        gb = [sb(f"gb{m}", [P, 16]) for m in range(4)]
        up = [sb(f"up{m}", [P, 2, e * f * k], F16) for m, (e, k, f) in enumerate(MOES[:3])]
        ub = [sb(f"ub{m}", [P, e * f]) for m, (e, k, f) in enumerate(MOES[:3])]
        dn = [sb(f"dn{m}", [k, e * f, C]) for m, (e, k, f) in enumerate(MOES)]
        db = [sb(f"db{m}", [GT * 8, GT, C]) for m in range(3)]
        rhsq = sb("rhsq", [P, 6, C], BF16)
        srow = sb("srow", [P, C])
        gam1 = sb("gam1", [P, C])
        bet1 = sb("bet1", [P, C])
        se1 = sb("se1", [C, 4])
        se1b = sb("se1b", [4, 1])
        se2 = sb("se2", [4, C])
        se2b = sb("se2b", [P, C])
        att = sb("att", [P, 2, 16])
        gatv = sb("gatv", [P, 3, 16])
        hb = sb("hb", [P, 2, FT])
        rc = sb("rc", [P, C])
        rcp = sb("rcp", [P, 2, C], F16)
        rh = sb("rh", [P, P])
        counts = sb("counts", [P, 8])
        rounds = sb("rounds", [P, 8], I32)

        esrc = arena[:, 0:EPP].bitcast(I32)
        edst = arena[:, EPP:2 * EPP].bitcast(I32)
        ekey = arena[:, 2 * EPP:3 * EPP]
        etmp = arena[:, 3 * EPP:4 * EPP]
        xbuf = arena[:, 0:XW]
        zs = arena[:, XW:XW + NT * P]
        spread = arena[:, 0:2 * BLK * W * MSG].rearrange("p (s c w m) -> p s c w m", s=2, c=BLK, w=W)
        onehot = arena[:, 10240:10240 + 2 * BLK * P].rearrange("p (s c q) -> p s c q", s=2, c=BLK)
        up3 = arena[:, 0:UP3].bitcast(F16).rearrange("p (k n) -> p k n", k=2)
        stage_up, at = [], XW + NT * P
        for e, k, f in MOES[:3]:
            stage_up.append(arena[:, at:at + e * k * f])
            at += e * k * f
        assert at <= 12288
        sil_flat = sil[:].rearrange("p a n -> p (a n)")
        stage_w0 = sil_flat[:, 0:2 * DI]
        stage_gw = {m: sil_flat[:, o:o + n] for m, o, n in ((0, 256, 8), (2, 264, 16), (3, 280, 8))}
        cu = hS[:, 0:2, :]
        csu = hS[:, 2:4, :]
        cy = hS[:, 4:6, :]
        qg = hS[:, 0:1, :].rearrange("p a n -> p (a n)").bitcast(BF16).rearrange("p (s t d c) -> p s t d c", s=2, t=GT, d=2)
        qf = hS[:, 1, :].rearrange("p (s t c) -> p s t c", s=2, t=GT)
        wqf = hS[0:C, 2:4, :].rearrange("p a n -> p (a n)")[:, 0:576]
        wqb = hS[0:C, 9:12, :].rearrange("p a n -> p (a n)")[:, 600:600 + 288].bitcast(BF16)
        qpad = hS[:, 2:11, :].rearrange("p a n -> p (a n)").bitcast(BF16)[:, 0:2 * PAD * P].rearrange(
            "p (k x n) -> p k x n", k=2, x=PAD)
        rq = hS[0:C, 9:12, :].rearrange("p a n -> p (a n)")
        maskH = hS[:, 0:2, :].rearrange("p a n -> p (a n)").rearrange("p (t q) -> p t q", t=FT)
        maskC = hS[:, 2:3, :].rearrange("p a n -> p (a n)").rearrange("p (t q) -> p t q", t=FT)
        piece = hS[:, 3:12, :].rearrange("p a n -> p (a n)")[:, 0:2 * PIECE].rearrange("p (s n) -> p s n", s=2)
        hn = hS[:, 0, :].rearrange("p (t k) -> p t k", t=NT)
        stab = hS[:, 1:3, :].rearrange("p a n -> p (a n)")[:, 0:NT * SRCW].rearrange("p (t k) -> p t k", t=NT)
        dtab = hS[:, 3, 0:NT * DSTW].rearrange("p (t k) -> p t k", t=NT)
        gsrc = hS[:, 4, 0:2 * BLK * SRCW].rearrange("p (s c k) -> p s c k", s=2, c=BLK)
        gdst = hS[:, 5, 0:2 * BLK * DSTW].rearrange("p (s c k) -> p s c k", s=2, c=BLK)
        em = hS[:, 6, 0:2 * BLK * MSG].rearrange("p (s c k) -> p s c k", s=2, c=BLK)
        ei = hS[:, 7, 0:2 * 3 * BLK].bitcast(I32).rearrange("p (s k c) -> p s k c", s=2, k=3)
        epart = hS[:, 7, 128:128 + 3 * BLK].bitcast(I32).rearrange("p (k c) -> p k c", k=3)
        ef = hS[:, 8, 0:3 * BLK].rearrange("p (k c) -> p k c", k=3)
        ew = hS[:, 8, 64:64 + BLK * HEADS].rearrange("p (c k) -> p c k", c=BLK)
        av = hS[:, 11, 0:4 * NT * HEADS].rearrange("p (k t h) -> p k t h", k=4, t=NT)
        aggr = hS[:, 9:11, :].rearrange("p a n -> p (a n)")[:, 0:NT * MSG].rearrange("p (t k) -> p t k", t=NT)

        ps = [ctx.enter_context(nc.psum_tensor(f"ps{n}", [P, 512], F32)) for n in range(8)]
        src_rows = nc.dram_tensor("src_rows", [NODES, SRCW], F32, kind="Internal").ap()
        dst_rows = nc.dram_tensor("dst_rows", [NODES, DSTW], F32, kind="Internal").ap()

        x_in = sem("x_in")
        edges_in = sem("edges_in")
        w_in = sem("w_in")
        masks_in = sem("masks_in")
        piece_in = [sem(f"piece_in{h}") for h in range(2)]
        piece_cut = sem("piece_cut")
        weights_cut = sem("weights_cut")
        edges_left = sem("edges_left")
        tables_out = sem("tables_out")
        stored = sem("stored")
        pool_const = sem("pool_const")
        carried = sem("carried")
        dve_step = sem("dve_step")
        act_step = sem("act_step")
        pool_step = sem("pool_step")
        ask_act, act_done = sem("ask_act"), sem("act_done")
        ask_pe, pe_done = sem("ask_pe"), sem("pe_done")
        ask_pool, pool_done = sem("ask_pool"), sem("pool_done")
        group_made = sem("group_made")
        group_turned = sem("group_turned")
        turned_copied = sem("turned_copied")
        turned_used = sem("turned_used")
        product_read = sem("product_read")
        xz_copied = sem("xz_copied")
        conv_made = sem("conv_made")
        conv_silu = sem("conv_silu")
        conv_gated = sem("conv_gated")
        conv_out = sem("conv_out")
        conv_added = sem("conv_added")
        hid_full = sem("hid_full")
        hid_act = sem("hid_act")
        sil_done = sem("sil_done")
        down_done = sem("down_done")
        comb_done = sem("comb_done")
        gate_staged = sem("gate_staged")
        gate_turned = sem("gate_turned")
        gate_copied = sem("gate_copied")
        bias_done = sem("bias_done")
        bias_read = sem("bias_read")
        q_turned = sem("q_turned")
        q_low = sem("q_low")
        q_high = sem("q_high")
        taps_done = sem("taps_done")
        taps_read = sem("taps_read")
        sorted_seg = [sem(f"sorted_seg{s}") for s in range(NSEG)]
        idx_ready = sem("idx_ready")
        rows_used = sem("rows_used")
        src_in = [sem(f"src_in{h}") for h in range(2)]
        dst_in = [sem(f"dst_in{h}") for h in range(2)]
        edge_step = sem("edge_step")
        spread_made = sem("spread_made")
        block_added = sem("block_added")

        RING2 = [group_turned, turned_copied, turned_used, product_read, conv_silu,
                 conv_gated, conv_out, conv_added, hid_full, hid_act, sil_done, down_done, comb_done,
                 q_turned, q_low, q_high, taps_done, taps_read, block_added, rows_used]
        RING1 = [gate_turned, gate_copied, bias_done, bias_read] + sorted_seg

        W_LOADS = 52
        POOL_CONSTS = 10
        PE_EDGES = 12

        block = ctx.enter_context(nc.Block())

        T_L0C, T_L0F, T_L1F, T_L2F, T_WAV, T_L3F = range(6)
        READ0 = {T_L0F: 0, T_L2F: NG, T_WAV: 2 * NG, T_L3F: 3 * NG}

        @block.sync
        def _(sp):
            sp.dma_start(X[:], a["x"]).then_inc(x_in, 16)
            sp.dma_start(esrc, a["src"]).then_inc(edges_in, 16)
            sp.dma_start(edst, a["dst"]).then_inc(edges_in, 16)
            n_w = [0]

            def load(dst, src):
                n_w[0] += 16
                sp.dma_start(dst, src).then_inc(w_in, 16)

            def rows(v):
                return v.partition_broadcast(P)

            def load_twice(dst, src):
                load(dst[0:C], src)
                load(dst[C:P], src)

            load_twice(stage_w0, a["w0in"])
            load(w0out[:], a["w0out"])
            load(c0w[:], a["c0w"])
            load(c0b[:], a["c0b"])
            for m, (e, k, f) in enumerate(MOES):
                if m < 3:
                    load_twice(stage_up[m], a[f"up{m}"])
                    load(ub[m][0:k, :], a[f"ub{m}"])
                load(dn[m][:], a[f"dn{m}"])
                if m == 1:
                    load(gw1[:], a["gw1"])
                else:
                    load_twice(stage_gw[m], a[f"gw{m}"])
            for m in range(2):
                load(gb[m][:, 0:8], rows(a[f"gb{m}"]))
            sp.wait_ge(pool_const, 1)
            for m in range(3):
                e = MOES[m][0]
                for j in range(GT):
                    load(db[m][j * 8:j * 8 + e, j, :], a[f"db{m}"])
            load(rq[:, 0:576], a["rhs"])
            load(gam1[:], rows(a["gam1"]))
            load(bet1[:], rows(a["bet1"]))
            load(se1[:], a["se1"])
            load(se1b[:], a["se1b"])
            load(se2[:], a["se2"])
            load(se2b[:], rows(a["se2b"]))
            load(att[:, 0, :], rows(a["att_src"]))
            load(att[:, 1, :], rows(a["att_dst"]))
            load(gatv[:, 0, :], rows(a["b_gat"]))
            load(gatv[:, 1, :], rows(a["gat_g"]))
            load(gatv[:, 2, :], rows(a["gat_b"]))
            load(hb[:, 0, :], rows(a["wavelet"]))
            assert n_w[0] == W_LOADS * 16, n_w[0] // 16
            sp.wait_ge(tables_out, 1)
            sp.dma_start(src_rows.rearrange("(p t) k -> p (t k)", p=P), stab.rearrange("p t k -> p (t k)")).then_inc(tables_out, 16)
            sp.dma_start(dst_rows.rearrange("(p t) k -> p (t k)", p=P), dtab.rearrange("p t k -> p (t k)")).then_inc(tables_out, 16)
            sp.wait_ge(pe_done, PE_EDGES)
            sp.wait_ge(edges_left, 1)
            for n in range(PIECES):
                if n >= 2:
                    sp.wait_ge(piece_cut, n - 1)
                for half in range(2):
                    sp.dma_start(piece[half * C:(half + 1) * C, n % 2], a["up3"][:, n * PIECE:(n + 1) * PIECE]).then_inc(piece_in[n % 2], 16)
            sp.wait_ge(masks_in, 1)
            sp.dma_start(maskH, a["maskH"]).then_inc(masks_in, 16)
            for half in range(2):
                sp.dma_start(maskC[half * C:(half + 1) * C], a["maskC"]).then_inc(masks_in, 16)
            sp.wait_ge(stored, 1)
            sp.dma_start(out, X[:]).then_inc(stored, 16)
            sp.wait_ge(stored, 17)

        @block.vector
        def _(v):
            st = Steps(v, dve_step)
            asked = {"act": 0, "pe": 0, "pool": 0}
            asks = {"act": (ask_act, act_done), "pe": (ask_pe, pe_done), "pool": (ask_pool, pool_done)}

            def ask(who, ins):
                ins.then_inc(asks[who][0], 1)
                asked[who] += 1

            def answer(who):
                v.wait_ge(asks[who][1], asked[who])

            def bc(ap, shape):
                return ap.to_broadcast(shape)

            for s in RING2:
                v.sem_inc(s, 2)
            for s in RING1:
                v.sem_inc(s, 1)
            v.sem_inc(xz_copied, 4)

            v.wait_ge(edges_in, 32)
            st(v.memset(keys[:], 0.0))
            st(v.tensor_scalar(etmp, esrc, float(NODES - 1), 1.0, ALU.min, ALU.add))
            st(v.scalar_tensor_tensor(etmp, edst, float(NODES), etmp, ALU.mult, ALU.add))
            st(v.tensor_scalar(ekey, edst, float(NODES), None, ALU.is_lt))
            for s in range(NSEG):
                st(v.tensor_reduce(counts[:, s:s + 1], ekey[:, s * SEG:(s + 1) * SEG], AX.X, ALU.add))
            st(v.tensor_tensor(ekey, ekey, etmp, ALU.mult))
            ask("pool", v.tensor_copy(counts[:, 4:4 + NSEG], counts[:, 0:NSEG]))
            answer("pool")
            st(v.tensor_scalar(rounds[:, 0:NSEG], counts[:, 0:NSEG], float(TOP - 1), None, ALU.add))
            st(v.tensor_scalar(rounds[:, 0:NSEG], rounds[:, 0:NSEG], 3, None, ALU.logical_shift_right))
            st(v.tensor_scalar(rounds[:, 4:5], rounds[:, 0:1], 0.0, None, ALU.add))
            for s in range(1, NSEG):
                st(v.tensor_tensor(rounds[:, 4 + s:5 + s], rounds[:, 3 + s:4 + s], rounds[:, s:s + 1], ALU.add))
            for s in range(NSEG):
                n_rounds = v.value_load(rounds[0:1, s:s + 1], min_val=0, max_val=MAXR)
                first = 0 if s == 0 else v.value_load(rounds[0:1, 3 + s:4 + s], min_val=0, max_val=MAXR * s)
                seg = ekey[:, s * SEG:(s + 1) * SEG]

                def sort_rounds(r0):
                    for k in range(UNROLL):
                        r = r0 + k
                        v.wait_ge(sorted_seg[s], r * 3 + 1)
                        settle(v, carried)
                        v.max(small[:, 0:8], seg).then_inc(sorted_seg[s], 1)
                        v.wait_ge(sorted_seg[s], r * 3 + 2)
                        v.tensor_copy(keys[:, bass.ds((r + first) * TOP, TOP)], small[:, 0:8]).then_inc(sorted_seg[s], 1)
                        v.match_replace(seg, small[:, 0:8], seg, 0.0).then_inc(sorted_seg[s], 1)
                with v.Fori(0, COMMON_ROUNDS, UNROLL) as r:
                    sort_rounds(r)
                v.wait_ge(sorted_seg[s], 3 * COMMON_ROUNDS + 1)
                with v.If(n_rounds > COMMON_ROUNDS):
                    with v.Fori(COMMON_ROUNDS, MAXR, UNROLL) as r:
                        sort_rounds(r)
                    v.wait_ge(sorted_seg[s], 3 * MAXR + 1)

            v.wait_ge(x_in, 16)
            v.wait_ge(pool_const, POOL_CONSTS)
            v.wait_ge(w_in, W_LOADS * 16)
            v.wait_ge(weights_cut, 1)

            def layer_norm(src, eps):
                st(v.tensor_reduce(lnsum[:], src[:], AX.X, ALU.add))
                st(v.tensor_scalar(lnneg[:], lnsum[:], -1.0 / C, None, ALU.mult))
                ask("act", v.tensor_tensor(XC[:], src[:], bc(lnneg[:].unsqueeze(2), [P, NT, C]), ALU.add))
                answer("act")
                st(v.tensor_reduce(lnvar[:], SQ[:], AX.X, ALU.add))
                ask("act", v.tensor_scalar(lnvar[:], lnvar[:], 1.0 / C, eps, ALU.mult, ALU.add))
                answer("act")
                st(v.reciprocal(rstd[:], lnsd[:]))

            def normalised(dst):
                st(v.tensor_tensor(dst[:], XC[:], bc(rstd[:].unsqueeze(2), [P, NT, C]), ALU.mult))

            def turn_groups(stage, made, read=None):
                per = (made[1] + (read[1] if read else 0)) * 2
                with v.Fori(0, NG // 2) as it:
                    st.enter(it, per)
                    for half in range(2):
                        n = it * 2 + half + NG * stage
                        v.wait_ge(group_turned, n + 1)
                        made[0](it * 2 + half, half)
                    if read:
                        for half in range(2):
                            n = it * 2 + half + NG * stage
                            v.wait_ge(turned_used, n + 3)
                            read[0](it * 2 + half, half, n)
                    st.leave(NG // 2)

            def group_norm(g, half):
                st(v.scalar_tensor_tensor(ygf[:, half], XC[:, bass.ds(g * GT, GT), :], X_SCALE,
                                          bc(rstd[:, bass.ds(g * GT, GT)].unsqueeze(2), [P, GT, C]), ALU.mult, ALU.mult))
                cut_group(half)

            def cut_group(half):
                st(v.tensor_copy(yg[:, half, :, 0], ygf[:, half]))
                v.tensor_tensor(yg[:, half, :, 1], ygf[:, half], yg[:, half, :, 0], ALU.subtract).then_inc(group_made, 1)

            def read_logits(width, bias, dst):
                def read(g, half, n):
                    o = ps[2 + half][:, 0:GT * width].rearrange("p (t k) -> p t k", t=GT)
                    d = dst[:, bass.ds(g * GT, GT), 0:width]
                    if bias is None:
                        v.tensor_scalar(d, o, UNSCALE, None, ALU.mult).then_inc(product_read, 1)
                    else:
                        v.scalar_tensor_tensor(d, o, UNSCALE, bc(bias.unsqueeze(1), [P, GT, width]), ALU.mult, ALU.add).then_inc(product_read, 1)
                return read, 0

            def top2_gates(n_tiles, E, eps=None):
                lg, gx, gt = (z[:, 0:n_tiles, 0:E] for z in (logit, gex, gate))
                beats = SQ[:].rearrange("p t c -> p (t c)")[:, 0:n_tiles * E * E].rearrange("p (t e f) -> p t e f", t=n_tiles, e=E)
                mx, sm, z, rec = (gsum[:, k, 0:n_tiles] for k in range(4))
                st(v.tensor_reduce(mx, lg, AX.X, ALU.max))
                ask("act", v.tensor_tensor(gx, lg, bc(mx.unsqueeze(2), [P, n_tiles, E]), ALU.subtract))
                for e in range(E):
                    if e:
                        st(v.tensor_tensor(beats[:, :, e, 0:e], lg[:, :, 0:e], bc(lg[:, :, e:e + 1], [P, n_tiles, e]), ALU.is_ge))
                    st(v.tensor_tensor(beats[:, :, e, e:E], lg[:, :, e:E], bc(lg[:, :, e:e + 1], [P, n_tiles, E - e]), ALU.is_gt))
                st(v.tensor_reduce(gt, beats, AX.X, ALU.add))
                st(v.tensor_scalar(gt, gt, 1.5, None, ALU.is_lt))
                answer("act")
                st(v.tensor_tensor(gt, gt, gx, ALU.mult))
                st(v.tensor_reduce(sm, gt, AX.X, ALU.add))
                if eps is not None:
                    st(v.tensor_reduce(z, gx, AX.X, ALU.add))
                    st(v.scalar_tensor_tensor(sm, z, eps, sm, ALU.mult, ALU.add))
                st(v.reciprocal(rec, sm))
                st(v.tensor_tensor(gt, gt, bc(rec.unsqueeze(2), [P, n_tiles, E]), ALU.mult))

            def softmax_row():
                lg, mx, sm, rec = logit[:, 0, 0:8], gsum[:, 0, 0:1], gsum[:, 1, 0:1], gsum[:, 2, 0:1]
                st(v.tensor_reduce(mx, lg, AX.X, ALU.max))
                ask("act", v.tensor_scalar(gex[:, 0, 0:8], lg, mx, None, ALU.subtract))
                answer("act")
                st(v.tensor_reduce(sm, gex[:, 0, 0:8], AX.X, ALU.add))
                st(v.reciprocal(rec, sm))
                st(v.tensor_scalar(lg, gex[:, 0, 0:8], rec, None, ALU.mult))

            def image_means():
                ask("pe", v.tensor_reduce(SQ[:, 0, :], Y[:].rearrange("p t c -> p c t"), AX.X, ALU.add))
                answer("pe")

            def round_clip(dst, src, scale, tmp):
                st(v.tensor_scalar(tmp, src, scale, ROUND, ALU.mult, ALU.add))
                st(v.tensor_scalar(tmp, tmp, ROUND, QMAX, ALU.subtract, ALU.min))
                return v.tensor_scalar(dst, tmp if len(dst.shape) == len(tmp.shape) else
                                       bc(tmp.unsqueeze(2), list(dst.shape)), -QMAX, None, ALU.max)

            def experts(m, T):
                E, KH, FC = MOES[m]
                bias = m < 3
                with v.Fori(0, NG) as g:
                    st.enter(g, E + (2 if bias else 1))
                    if bias:
                        v.wait_ge(gate_turned, g + NG * m + 1)
                    st(v.tensor_copy(gst[:].rearrange("p (t e) -> p t e", t=GT), gate[:, bass.ds(g * GT, GT), :]))
                    tg = T[:, bass.ds(g * GT, GT), :]
                    if bias:
                        v.sem_inc(gate_staged, 1)
                        v.wait_ge(bias_done, g + NG * m + 2)
                        st(v.tensor_tensor(tg, tg, ps[7][:, 0:GT * C].rearrange("p (t c) -> p t c", t=GT), ALU.add))
                        v.sem_inc(bias_read, 1)

                    def gated_hidden(e):
                        for f in range(FC):
                            k = e * FC + f
                            n = g * (E * FC) + (k + CHUNK0[m])
                            v.wait_ge(sil_done, g * (E * FC) + (k + 3))
                            if f == 0:
                                v.wait_ge(down_done, g * E + (e + UNIT0[m] + 1))
                            v.scalar_tensor_tensor(hS[0:KH, (e % 2) * FC + f, :], ps[2 + k % 2][0:KH, :], UNSCALE,
                                                   sil[0:KH, k % 2, :], ALU.mult, ALU.mult).then_inc(hid_act, 1)

                    def combine(e):
                        u = g * E + (e + UNIT0[m])
                        v.wait_ge(down_done, u + 3)
                        v.tensor_tensor(comb[:, e % 2], ps[4 + e % 2][:, 0:GT * C].rearrange("p (t c) -> p t c", t=GT),
                                        bc(gst[:].rearrange("p (t e) -> p t e", t=GT)[:, :, e:e + 1], [P, GT, C]),
                                        ALU.mult).then_inc(comb_done, 1)
                        v.wait_ge(comb_done, u + 3)
                        st(v.tensor_tensor(tg, tg, comb[:, e % 2], ALU.add))

                    for e in range(E):
                        if m == 3:
                            gated_hidden(e)
                            if e:
                                combine(e - 1)
                        else:
                            combine(e)
                    if m == 3:
                        combine(E - 1)
                    st.leave(NG)

            layer_norm(X, 1e-6)

            def read_nothing(g, half, n):
                pass
            turn_groups(T_L0C, (group_norm, 2))
            v.wait_ge(xz_copied, 4 + 2 * NG)
            st(v.memset(xbuf[:, 0:(TAPS - 1) * P], 0.0))
            prev = xbuf[:, NT * P:XW].rearrange("p (t b h) -> p t b h", t=TAPS - 1, b=B)
            head = xbuf[:, 0:(TAPS - 1) * P].rearrange("p (t b h) -> p t b h", t=TAPS - 1, b=B)
            for t in range(TAPS - 1):
                st(v.tensor_copy(head[:, t, :, 1:H], prev[:, t, :, 0:H - 1]))
            with v.Fori(0, NG // 2) as it:
                st.enter(it, 2 * (TAPS - 1) + 2)
                for half in range(2):
                    g = it * 2 + half
                    v.wait_ge(conv_silu, g + 1)
                    st(v.tensor_scalar(cu[:, half], xbuf[:, bass.ds(g * GN, GN)], c0w[:, 0:1], None, ALU.mult))
                    for k in range(1, TAPS):
                        ins = v.scalar_tensor_tensor(cu[:, half], xbuf[:, bass.ds(g * GN + k * P, GN)], c0w[:, k:k + 1],
                                                     cu[:, half], ALU.mult, ALU.add)
                        if k == TAPS - 1:
                            ins.then_inc(conv_made, 1)
                        else:
                            st(ins)
                for half in range(2):
                    g = it * 2 + half
                    v.wait_ge(conv_silu, g + 3)
                    v.wait_ge(conv_out, g + 1)
                    v.scalar_tensor_tensor(cy[:, half], csu[:, half], 4.0, zs[:, bass.ds(g * GN, GN)], ALU.mult,
                                           ALU.mult).then_inc(conv_gated, 1)
                for half in range(2):
                    g = it * 2 + half
                    v.wait_ge(conv_out, g + 3)
                    xg = X[:, bass.ds(g * GT, GT), :]
                    st(v.tensor_tensor(xg, xg, ps[half][:, 0:GT * C].rearrange("p (t c) -> p t c", t=GT), ALU.add))
                    v.sem_inc(conv_added, 1)
                st.leave(NG // 2)

            layer_norm(X, 1e-5)
            turn_groups(T_L0F, (group_norm, 2), read_logits(8, gb[0][:, 0:8], logit))
            v.wait_ge(product_read, 2 + NG)
            top2_gates(NT, 8)
            experts(0, X)

            amax, scale, inv = small[0:C, 8:9], small[0:C, 9:10], small[0:C, 10:11]
            st(v.tensor_reduce(amax, rq[:, 0:576], AX.X, ALU.max, apply_absolute_value=True))
            st(v.tensor_scalar(scale, amax, 1e-6, 1.0 / QMAX, ALU.max, ALU.mult))
            st(v.reciprocal(inv, scale))
            ask("pe", round_clip(wqb, rq[:, 0:576], inv, wqf))
            answer("pe")
            st(v.memset(rhsq[:], 0.0))
            wt = ps[6][:, 0:3 * C].bitcast(BF16).rearrange("p (k o) -> p k o", k=6)
            st(v.tensor_copy(rhsq[:, 0:6:2, :], wt[:, 0:6:2, :]))
            st(v.tensor_copy(rhsq[0:C, 1:6:2, :], wt[0:C, 1:6:2, :]))
            ask("pe", v.tensor_copy(SQ[0:C, 0:2, :].rearrange("p a c -> p (a c)"), bc(scale, [C, P])))
            answer("pe")
            st(v.tensor_copy(srow[:], ps[7][:, 0:C]))
            st(v.memset(qpad, 0.0))
            layer_norm(X, 1e-6)
            normalised(Y)
            ask("pe", v.tensor_reduce(small[:, 11:12], Y[:].rearrange("p t c -> p (t c)"), AX.X, ALU.max,
                                      apply_absolute_value=True))
            answer("pe")
            st(v.tensor_reduce(small[0:1, 12:16], ps[6][0:1, 0:P].rearrange("p (b h) -> p b h", b=B), AX.X, ALU.max))
            ask("pe", v.tensor_copy(SQ[0:1, 0:2, :].rearrange("p a c -> p (a c)").rearrange("p (b h) -> p b h", b=B),
                                    bc(small[0:1, 12:16].unsqueeze(2), [1, B, H])))
            answer("pe")
            st(v.tensor_scalar(small[:, 16:17], ps[7][:, 0:1], 1e-6, 1.0 / QMAX, ALU.max, ALU.mult))
            st(v.reciprocal(small[:, 17:18], small[:, 16:17]))
            with v.Fori(0, NG // 2) as it:
                st.enter(it, 4)
                for half in range(2):
                    g = it * 2 + half
                    v.wait_ge(q_turned, g + 1)
                    round_clip(qg[:, half], Y[:, bass.ds(g * GT, GT), :], small[:, 17:18], qf[:, half]).then_inc(group_made, 1)
                for half in range(2):
                    g = it * 2 + half
                    v.wait_ge(q_turned, g + 3)
                    v.tensor_copy(qpad[C:P, 0, bass.ds(g * GT + 1, GT), :].rearrange("p x n -> p (x n)"),
                                  ps[half][C:P, 0:GT * C].bitcast(BF16)).then_inc(q_high, 1)
                st.leave(NG // 2)
            with v.Fori(0, NG // 2) as it:
                st.enter(it, 4)
                for half in range(2):
                    g = it * 2 + half
                    v.wait_ge(taps_done, g + 3)
                    xg = X[:, bass.ds(g * GT, GT), :]
                    st(v.scalar_tensor_tensor(comb[:, half], ps[4 + half][:, 0:GT * C].rearrange("p (t c) -> p t c", t=GT),
                                              small[:, 16:17], bc(srow[:].unsqueeze(1), [P, GT, C]), ALU.mult, ALU.mult))
                    v.sem_inc(taps_read, 1)
                    st(v.tensor_tensor(xg, xg, comb[:, half], ALU.add))
                st.leave(NG // 2)

            layer_norm(X, 1e-5)
            turn_groups(T_L1F, (group_norm, 2))
            normalised(Y)
            image_means()
            ask("pe", v.tensor_scalar(SQ[0:C, 1:3, :].rearrange("p a c -> p (a c)").rearrange("p (b h) -> p b h", b=B),
                                      bc(ps[6][0:C, 0:B].unsqueeze(2), [C, B, H]), 1.0 / L, None, ALU.mult))
            answer("pe")
            st(v.tensor_tensor(logit[:, 0, 0:8], ps[7][:, 0:8], gb[1][:, 0:8], ALU.add))
            softmax_row()
            ask("pe", v.tensor_copy(SQ[:, 3, 0:8], logit[:, 0, 0:8]))
            answer("pe")
            load = SQ[:, 4, 0:8]
            st(v.tensor_scalar(load, ps[6][:, 0:8], float(L // H), None, ALU.mult))
            st(v.reciprocal(load, load))
            st(v.tensor_scalar(load, load, float(CAPACITY), 1.0, ALU.mult, ALU.min))
            st(v.tensor_tensor(logit[:, 0, 0:8], logit[:, 0, 0:8], load, ALU.mult))
            softmax_row()
            top2_gates(1, 8)
            st(v.tensor_copy(gate[:, 1:NT, :], bc(gate[:, 0:1, :], [P, NT - 1, 8])))
            experts(1, Y)
            layer_norm(Y, 1e-5)
            normalised(Y)
            st(v.tensor_tensor(Y[:], Y[:], bc(gam1[:].unsqueeze(1), [P, NT, C]), ALU.mult))
            st(v.tensor_tensor(Y[:], Y[:], bc(bet1[:].unsqueeze(1), [P, NT, C]), ALU.add))
            st(v.tensor_tensor(X[:], X[:], Y[:], ALU.add))

            layer_norm(X, 1e-6)
            normalised(Y)
            image_means()
            ask("pe", v.tensor_scalar(SQ[0:C, 1, 0:B], ps[6][0:C, 0:B], 1.0 / L, None, ALU.mult))
            answer("pe")
            st(v.tensor_scalar(small[0:4, 20:24], ps[7][0:4, 0:B], se1b[:, 0:1], 0.0, ALU.add, ALU.max))
            ask("pe", v.tensor_copy(SQ[0:4, 2:4, :].rearrange("p a c -> p (a c)").rearrange("p (b h) -> p b h", b=B),
                                    bc(small[0:4, 20:24].unsqueeze(2), [4, B, H])))
            answer("pe")
            ask("act", v.tensor_tensor(SQ[:, 4, :], ps[6][:, 0:C], se2b[:], ALU.add))
            answer("act")
            st(v.tensor_tensor(Y[:], Y[:], bc(SQ[:, 4:5, :], [P, NT, C]), ALU.mult))
            st(v.tensor_tensor(X[:], X[:], Y[:], ALU.add))

            layer_norm(X, 1e-5)
            turn_groups(T_L2F, (group_norm, 2), read_logits(16, None, hn))
            v.wait_ge(product_read, 2 + READ0[T_WAV])
            hk = SQ[:].rearrange("p t c -> p (t c)")[:, 0:NT * 16].rearrange("p (t k) -> p t k", t=NT)
            hk4 = hk.rearrange("p t (h k) -> p t h k", h=HEADS)
            sa, da, sw, sv = (av[:, k] for k in range(4))
            for k, dst in ((0, sa), (1, da)):
                st(v.tensor_tensor(hk, hn, bc(att[:, k:k + 1, :], [P, NT, 16]), ALU.mult))
                st(v.tensor_reduce(dst, hk4, AX.X, ALU.add))
            ask("pool", v.tensor_reduce(small[:, 24:28], sa.rearrange("p t h -> p h t"), AX.X, ALU.max))
            answer("pool")
            top = bc(small[:, 28:32].unsqueeze(1), [P, NT, HEADS])
            sp_, sq_, sh_ = stab[:, :, 0:4], stab[:, :, 4:8], stab[:, :, 8:SRCW]
            du_, dv_ = dtab[:, :, 0:4], dtab[:, :, 4:8]
            st(v.tensor_tensor(sp_, sa, top, ALU.subtract))
            st(v.tensor_scalar(sq_, sp_, 0.2, None, ALU.mult))
            st(v.tensor_tensor(da, da, top, ALU.add))
            st(v.scalar_tensor_tensor(sw, da, 0.2, da, ALU.mult, ALU.max))
            st(v.tensor_tensor(du_, da, sw, ALU.subtract))
            ask("act", v.scalar_tensor_tensor(dv_, da, 0.2, sw, ALU.mult, ALU.subtract))
            st(v.tensor_copy(sh_, hn))
            answer("act")
            v.sem_inc(tables_out, 1)
            st(v.tensor_tensor(sw, sp_, du_, ALU.mult))
            st(v.tensor_tensor(sv, sq_, dv_, ALU.mult))
            st(v.tensor_tensor(aggr[:, :, 16:MSG], sw, sv, ALU.max))
            a4 = aggr[:, :, 0:16].rearrange("p t (h k) -> p t h k", h=HEADS)
            for h in range(HEADS):
                ins = v.tensor_tensor(a4[:, :, h, :], hn[:, :, h * HK:(h + 1) * HK],
                                      bc(aggr[:, :, 16 + h:17 + h], [P, NT, HK]), ALU.mult)
                if h < HEADS - 1:
                    st(ins)
                else:
                    ask("pe", ins)
            answer("pe")

            def cut_keys(b, half, es):
                kb = keys[:, bass.ds(b * BLK, BLK)]
                es(v.tensor_scalar(ei[:, half, 0], kb, -1.0, 0.0, ALU.add, ALU.max))
                es(v.tensor_scalar(ei[:, half, 1], ei[:, half, 0], NODES - 1, None, ALU.bitwise_and))
                v.tensor_scalar(ei[:, half, 2], ei[:, half, 0], 12, None, ALU.logical_shift_right).then_inc(idx_ready, 1)

            es = Steps(v, edge_step)
            for half in range(2):
                cut_keys(half, half, es)
            total = v.value_load(rounds[0:1, 7:8], min_val=0, max_val=NBLK)
            with v.Fori(0, NBLK // SUPER) as o:
                with v.If(o * SUPER < total):
                    with v.Fori(0, SUPER // 2) as n:
                        pair = o * (SUPER // 2) + n
                        with v.If(pair * 2 < total):
                            es.enter(pair, EDGE_STEPS)
                            for half in range(2):
                                b = pair * 2 + half
                                gs, gd, m, kb = gsrc[:, half], gdst[:, half], em[:, half], keys[:, bass.ds(b * BLK, BLK)]
                                v.wait_ge(src_in[half], (pair + 1) * (16 * BLK))
                                v.wait_ge(dst_in[half], (pair + 1) * (16 * BLK))
                                cut_keys(b + 2, half, es)
                                es(v.tensor_scalar(epart[:, 0], kb, -1.0, 0.0, ALU.add, ALU.max))
                                es(v.tensor_scalar(epart[:, 1], epart[:, 0], 12, W - 1, ALU.logical_shift_right, ALU.bitwise_and))
                                es(v.tensor_scalar(epart[:, 2], epart[:, 0], 17, None, ALU.logical_shift_right))
                                es(v.tensor_copy(ef[:, 0], epart[:, 1]))
                                es(v.tensor_scalar(ef[:, 1], kb, 0.5, -1000.0, ALU.is_lt, ALU.mult))
                                es(v.tensor_tensor(ef[:, 1], ef[:, 1], epart[:, 2], ALU.add))
                                es(v.tensor_tensor(m[:, :, 16:MSG], gs[:, :, 0:4], gd[:, :, 0:4], ALU.mult))
                                es(v.tensor_tensor(ew, gs[:, :, 4:8], gd[:, :, 4:8], ALU.mult))
                                es(v.tensor_tensor(m[:, :, 16:MSG], m[:, :, 16:MSG], ew, ALU.max))
                                for h in range(HEADS):
                                    ins = v.tensor_tensor(m[:, :, h * HK:(h + 1) * HK], gs[:, :, 8 + h * HK:8 + (h + 1) * HK],
                                                          bc(m[:, :, 16 + h:17 + h], [P, BLK, HK]), ALU.mult)
                                    if h < HEADS - 1:
                                        es(ins)
                                ins.then_inc(rows_used, 1)
                                v.wait_ge(rows_used, b + 3)
                                v.wait_ge(block_added, b + 1)
                                for c in range(BLK):
                                    v.tensor_scalar(onehot[:, half, c], iotaP[:], ef[:, 1, c:c + 1], None,
                                                    ALU.is_equal).then_inc(spread_made, 1)
                                    v.scalar_tensor_tensor(spread[:, half, c], bc(iotaW[:].unsqueeze(2), [P, W, MSG]),
                                                           ef[:, 0, c:c + 1], bc(m[:, c:c + 1, :], [P, W, MSG]),
                                                           ALU.is_equal, ALU.mult).then_inc(spread_made, 1)
                                v.wait_ge(spread_made, (b + 1) * (2 * BLK))
                                settle(v, carried)
                            es.at = es.first
                            es.i = None
            ask("pe", v.drain())
            answer("pe")
            for k in range(2):
                st(v.tensor_copy(aggr[:, k * 16:(k + 1) * 16, :].rearrange("p t k -> p (t k)"), ps[6 + k][:, 0:16 * MSG]))
            den = av[:, 0]
            st(v.tensor_scalar(den, aggr[:, :, 16:MSG], 1e-16, None, ALU.add))
            st(v.reciprocal(den, den))
            for h in range(HEADS):
                st(v.tensor_tensor(hk4[:, :, h, :], aggr[:, :, h * HK:(h + 1) * HK], bc(den[:, :, h:h + 1], [P, NT, HK]), ALU.mult))
            v.sem_inc(edges_left, 1)
            vec = lambda k: bc(gatv[:, k:k + 1, :], [P, NT, 16])
            st(v.tensor_tensor(hk, hk, vec(0), ALU.add))
            st(v.tensor_reduce(lnsum[:], hk, AX.X, ALU.add))
            st(v.tensor_scalar(lnneg[:], lnsum[:], -1.0 / 16, None, ALU.mult))
            st(v.tensor_tensor(hk, hk, bc(lnneg[:].unsqueeze(2), [P, NT, 16]), ALU.add))
            sq16 = SQ[:].rearrange("p t c -> p (t c)")[:, NT * 16:NT * 32].rearrange("p (t k) -> p t k", t=NT)
            st(v.tensor_tensor(sq16, hk, hk, ALU.mult))
            st(v.tensor_reduce(lnvar[:], sq16, AX.X, ALU.add))
            ask("act", v.tensor_scalar(lnvar[:], lnvar[:], 1.0 / 16, 1e-5, ALU.mult, ALU.add))
            answer("act")
            st(v.reciprocal(rstd[:], lnsd[:]))
            st(v.tensor_tensor(hk, hk, bc(rstd[:].unsqueeze(2), [P, NT, 16]), ALU.mult))
            st(v.tensor_tensor(hk, hk, vec(1), ALU.mult))
            st(v.tensor_tensor(hk, hk, vec(2), ALU.add))
            st(v.tensor_reduce(logit[:, :, 0:4], hk.rearrange("p t (h k) -> p t k h", h=HEADS), AX.X, ALU.add))
            st(v.tensor_scalar(logit[:, :, 0:4], logit[:, :, 0:4], 1.0 / HEADS, None, ALU.mult))
            st(v.memset(gate[:], 0.0))
            top2_gates(NT, 4)
            experts(2, X)

            v.sem_inc(masks_in, 1)
            layer_norm(X, 1e-6)
            normalised(Y)
            v.wait_ge(masks_in, 49)
            st(v.tensor_copy(hb[:, 1, 1:FT:2], hb[:, 0, 1:FT:2]))
            st(v.tensor_scalar(hb[:, 1, 0:FT:2], hb[:, 0, 0:FT:2], -1.0, None, ALU.mult))
            for mat, mask in ((rc, maskC), (rh, maskH)):
                st(v.tensor_scalar(mat[:], mask[:, 0], hb[:, 0, 0:1], None, ALU.mult))
                for k in range(1, FT):
                    ins = v.scalar_tensor_tensor(mat[:], mask[:, k], hb[:, 0, k:k + 1], mat[:], ALU.mult, ALU.add)
                    if k == FT - 1 and mat is rh:
                        ask("pe", ins)
                    else:
                        st(ins)
            st(v.tensor_scalar(rc[:], rc[:], W_SCALE, None, ALU.mult))
            st(v.tensor_copy(rcp[:, 0], rc[:]))
            st(v.tensor_tensor(rcp[:, 1], rc[:], rcp[:, 0], ALU.subtract))
            answer("pe")
            ask("act", v.drain())
            answer("act")
            for par in range(2):
                rows_out = ACC[:].rearrange("p (m two) c -> p m two c", two=2)[:, :, par]
                first = True
                for k in range(1 - par, FT, 2):
                    off = ((par + k - 1) // 2 - (FT // 2 - 1)) % (W // 2)
                    for wide, filt in ((0, hb[:, 0, FT - 1 - k:FT - k]), (1, hb[:, 1, k:k + 1])):
                        for m0, m1, s0 in ((0, W // 2 - off, off), (W // 2 - off, W // 2, 0)):
                            if m0 == m1:
                                continue
                            srcs = XC[:, wide * (W // 2) + s0:wide * (W // 2) + s0 + m1 - m0, :]
                            o = rows_out[:, m0:m1, :]
                            if first:
                                st(v.tensor_scalar(o, srcs, filt, None, ALU.mult))
                            else:
                                st(v.scalar_tensor_tensor(o, srcs, filt, o, ALU.mult, ALU.add))
                        first = False

            def copy_group(g, half):
                st(v.tensor_scalar(ygf[:, half], ACC[:, bass.ds(g * GT, GT), :], X_SCALE, None, ALU.mult))
                cut_group(half)

            def add_group(g, half, n):
                xg = X[:, bass.ds(g * GT, GT), :]
                v.scalar_tensor_tensor(xg, ps[2 + half][:, 0:GT * C].rearrange("p (t c) -> p t c", t=GT), UNSCALE, xg,
                                       ALU.mult, ALU.add).then_inc(product_read, 1)
            turn_groups(T_WAV, (copy_group, 2), (add_group, 0))
            v.wait_ge(product_read, 2 + READ0[T_L3F])

            layer_norm(X, 1e-5)
            turn_groups(T_L3F, (group_norm, 2), read_logits(8, None, logit))
            v.wait_ge(product_read, 2 + READ0[T_L3F] + NG)
            top2_gates(NT, 8, 1e-9)
            experts(3, X)
            v.drain().then_inc(stored, 1)

        @block.scalar
        def _(s):
            done = [0]

            def asked():
                done[0] += 1
                s.wait_ge(ask_act, done[0])

            def layer_norm():
                asked()
                s.activation(SQ[:], XC[:], ACT.Square).then_inc(act_done, 1)
                asked()
                s.activation(lnsd[:], lnvar[:], ACT.Sqrt).then_inc(act_done, 1)

            def exp_gates(n_tiles, E):
                asked()
                s.activation(gex[:, 0:n_tiles, 0:E], gex[:, 0:n_tiles, 0:E], ACT.Exp).then_inc(act_done, 1)

            def turn_groups(stage, after=None):
                with s.Fori(0, NG // 2) as it:
                    for half in range(2):
                        n = it * 2 + half + NG * stage
                        s.wait_ge(group_turned, n + 3)
                        s.activation(yT[:, bass.ds((it * 2 + half) * GN, GN)], ps[half][:, 0:GN // 2].bitcast(F16),
                                     ACT.Copy).then_inc(turned_copied, 1)
                        if after:
                            after(it * 2 + half, half)

            def experts(m):
                E, KH, FC = MOES[m]
                with s.Fori(0, NG) as g:
                    for e in range(E):
                        for f in range(FC):
                            k = e * FC + f
                            n = g * (E * FC) + (k + CHUNK0[m])
                            s.wait_ge(hid_full, n + 3)
                            if m == 3:
                                s.wait_ge(hid_act, n + 1)
                                s.activation(sil[0:KH, k % 2], ps[k % 2][0:KH, :], ACT.Silu, scale=UNSCALE).then_inc(sil_done, 1)
                                continue
                            if f == 0:
                                s.wait_ge(down_done, g * E + (e + UNIT0[m] + 1))
                            s.activation(hS[0:KH, (e % 2) * FC + f, :], ps[k % 2][0:KH, :], ACT.Gelu,
                                         bias=ub[m][0:KH, k:k + 1], scale=UNSCALE).then_inc(hid_act, 1)
                        if e == 0 and m < 3:
                            s.wait_ge(gate_turned, g + NG * m + 2)
                            s.wait_ge(bias_done, g + NG * m + 1)
                            s.activation(gTs[:], ps[6][0:GT * 8, 0:P], ACT.Copy).then_inc(gate_copied, 1)

            s.wait_ge(w_in, W_LOADS * 16)
            layer_norm()

            def copy_xz(g, half):
                s.wait_ge(turned_used, g + 3)
                s.activation(xbuf[:, bass.ds(g * GN + (TAPS - 1) * P, GN)], ps[4 + half][:, :], ACT.Copy, scale=UNSCALE).then_inc(xz_copied, 1)
                s.activation(zs[:, bass.ds(g * GN, GN)], ps[6 + half][:, :], ACT.Silu, scale=UNSCALE).then_inc(xz_copied, 1)
            turn_groups(T_L0C, copy_xz)
            with s.Fori(0, NG // 2) as it:
                for half in range(2):
                    g = it * 2 + half
                    s.wait_ge(conv_made, g + 1)
                    s.wait_ge(conv_gated, g + 1)
                    s.activation(csu[:, half], cu[:, half], ACT.Silu, bias=c0b[:, 0:1]).then_inc(conv_silu, 1)
            layer_norm()
            turn_groups(T_L0F)
            exp_gates(NT, 8)
            experts(0)
            layer_norm()
            with s.Fori(0, NG // 2) as it:
                for half in range(2):
                    g = it * 2 + half
                    s.wait_ge(q_turned, g + 3)
                    for k, o0, i0 in ((0, 1, 0), (1, 0, 1)):
                        ins = s.activation(
                            qpad[0:C, k, bass.ds(g * GT + 1, GT), :].rearrange("p x (b h) -> p x b h", b=B)[:, :, :, o0:o0 + H - 1],
                            ps[half][0:C, 0:GT * C].bitcast(BF16).rearrange("p (t b h) -> p t b h", t=GT, b=B)[:, :, :, i0:i0 + H - 1],
                            ACT.Copy)
                    ins.then_inc(q_low, 1)
            layer_norm()
            turn_groups(T_L1F)
            exp_gates(1, 8)
            exp_gates(1, 8)
            exp_gates(1, 8)
            experts(1)
            layer_norm()
            layer_norm()
            asked()
            s.activation(SQ[:, 4, :], SQ[:, 4, :], ACT.Sigmoid).then_inc(act_done, 1)
            layer_norm()
            turn_groups(T_L2F)
            asked()
            s.activation(dtab, dtab, ACT.Exp).then_inc(act_step, 1)
            s.activation(stab[:, :, 0:8], stab[:, :, 0:8], ACT.Exp).then_inc(act_done, 1)
            asked()
            s.activation(lnsd[:], lnvar[:], ACT.Sqrt).then_inc(act_done, 1)
            exp_gates(NT, 4)
            experts(2)
            layer_norm()
            asked()
            for k in range(4):
                ins = s.activation(XC[:].rearrange("p t c -> p (t c)")[:, k * 512:(k + 1) * 512], ps[k][:, :], ACT.Copy)
            ins.then_inc(act_done, 1)
            turn_groups(T_WAV)
            layer_norm()
            turn_groups(T_L3F)
            exp_gates(NT, 8)
            experts(3)

        @block.tensor
        def _(t):
            def turn_groups(stage, product):
                with t.Fori(0, NG // 2) as it:
                    for half in range(2):
                        n = it * 2 + half + NG * stage
                        t.wait_ge(group_made, n + (1 + (NG if stage >= T_L1F else 0)))
                        t.wait_ge(turned_copied, n + 1)
                        settle(t, carried)
                        for j in range(GT):
                            ins = t.transpose(ps[half][:, j * C:(j + 1) * C].bitcast(F16),
                                              yg[:, half, j].rearrange("p d c -> p (d c)"), identh[:])
                        ins.then_inc(group_turned, 1)
                        t.wait_ge(turned_copied, n + 3)
                        product(it * 2 + half, half, n)

            def logits(w, width, base):
                def product(g, half, n):
                    t.wait_ge(product_read, g + (base + 1))
                    settle(t, carried)
                    for j in range(GT):
                        for k in range(2):
                            ins = t.matmul(ps[2 + half][:, j * width:(j + 1) * width], yT[:, bass.ds(g * GN + j * P, P)],
                                           w[:, k], start=(k == 0), stop=(k == 1))
                    ins.then_inc(turned_used, 1)
                return product

            def experts(m, stage, reads, ups):
                E, KH, FC = MOES[m]
                t.wait_ge(turned_copied, 2 + NG * (stage + 1))
                t.wait_ge(product_read, 2 + reads)
                with t.Fori(0, NG) as g:
                    x = yT[:, bass.ds(g * GN, GN)]

                    def project_up(e):
                        for f in range(FC):
                            k = e * FC + f
                            n = g * (E * FC) + (k + CHUNK0[m])
                            t.wait_ge(hid_act, n + 1)
                            settle(t, carried)
                            for q, w in enumerate(ups):
                                for part in range(2):
                                    ins = t.matmul(ps[2 * q + k % 2][0:KH, :], w[:, part, k * KH:(k + 1) * KH], x,
                                                   start=(part == 0), stop=(part == 1))
                            ins.then_inc(hid_full, 1)

                    def project_down(e):
                        u = g * E + (e + UNIT0[m])
                        t.wait_ge(hid_act, g * (E * FC) + ((e + 1) * FC + CHUNK0[m] + 2))
                        t.wait_ge(comb_done, u + 1)
                        for j in range(GT):
                            for f in range(FC):
                                ins = t.matmul(ps[4 + e % 2][:, j * C:(j + 1) * C],
                                               hS[0:KH, (e % 2) * FC + f, j * P:(j + 1) * P],
                                               dn[m][:, e * FC + f, :], start=(f == 0), stop=(f == FC - 1))
                        ins.then_inc(down_done, 1)

                    def turn_gates():
                        t.wait_ge(gate_staged, g + NG * m + 1)
                        t.wait_ge(gate_copied, g + NG * m + 1)
                        t.transpose(ps[6][0:GT * 8, 0:P], gst[:], ident[:]).then_inc(gate_turned, 1)

                    def bias():
                        t.wait_ge(gate_copied, g + NG * m + 2)
                        t.wait_ge(bias_read, g + NG * m + 1)
                        t.matmul(ps[7][:, 0:GT * C], gTs[:], db[m][:].rearrange("p t c -> p (t c)"), start=True,
                                 stop=True).then_inc(bias_done, 1)

                    for e in range(E):
                        project_up(e)
                        if e == 0 and m < 3:
                            turn_gates()
                        if e == 1 and m < 3:
                            bias()
                        if e:
                            project_down(e - 1)
                    project_down(E - 1)

            t.wait_ge(w_in, W_LOADS * 16)
            t.wait_ge(pool_const, POOL_CONSTS)
            t.wait_ge(weights_cut, 1)

            def project_xz(g, half, n):
                t.wait_ge(xz_copied, g * 2 + 2)
                for bank in range(2):
                    for part in range(2):
                        ins = t.matmul(ps[4 + 2 * bank + half][:, :], w0in[:, part, bank * DI:(bank + 1) * DI],
                                       yT[:, bass.ds(g * GN, GN)], start=(part == 0), stop=(part == 1))
                ins.then_inc(turned_used, 1)

            turn_groups(T_L0C, project_xz)
            with t.Fori(0, NG // 2) as it:
                for half in range(2):
                    g = it * 2 + half
                    t.wait_ge(conv_gated, g + 3)
                    t.wait_ge(conv_added, g + 1)
                    for j in range(GT):
                        ins = t.matmul(ps[half][:, j * C:(j + 1) * C], cy[:, half, j * P:(j + 1) * P], w0out[:],
                                       start=True, stop=True)
                    ins.then_inc(conv_out, 1)
            turn_groups(T_L0F, logits(gwp[0], 8, 0))
            experts(0, T_L0F, NG, [up[0]])

            asked = [0]

            def ask():
                asked[0] += 1
                t.wait_ge(ask_pe, asked[0])

            def no_product(g, half, n):
                t.sem_inc(turned_used, 1)

            ask()
            wt = ps[6][:, 0:3 * C].bitcast(BF16).rearrange("p (k o) -> p k o", k=6)
            for dx in range(3):
                t.transpose(wt[:, 2 * dx], wqb[:, dx * 3 * C:dx * 3 * C + 2 * C], identb[0:C, 0:C])
                ins = t.transpose(wt[0:C, 2 * dx + 1], wqb[:, dx * 3 * C + 2 * C:(dx + 1) * 3 * C], identb[0:C, 0:C])
            ins.then_inc(pe_done, 1)
            ask()
            t.matmul(ps[7][:, 0:C], SQ[0:C, 0:2, :].rearrange("p a c -> p (a c)"), ident[0:C, 0:C], start=True, stop=True).then_inc(pe_done, 1)
            ask()
            t.transpose(ps[6][0:1, 0:P], small[:, 11:12], ident[:]).then_inc(pe_done, 1)
            ask()
            t.matmul(ps[7][:, 0:1], SQ[0:1, 0:2, :].rearrange("p a c -> p (a c)"), ones[0:1, 0:1], start=True, stop=True).then_inc(pe_done, 1)
            with t.Fori(0, NG // 2) as it:
                for half in range(2):
                    g = it * 2 + half
                    t.wait_ge(group_made, g + (2 * NG + 1))
                    t.wait_ge(q_low, g + 1)
                    t.wait_ge(q_high, g + 1)
                    for j in range(GT):
                        ins = t.transpose(ps[half][:, j * C:(j + 1) * C].bitcast(BF16),
                                          qg[:, half, j].rearrange("p d c -> p (d c)"), identb[:])
                    ins.then_inc(q_turned, 1)
            t.wait_ge(q_low, 2 + NG)
            t.wait_ge(q_high, 2 + NG)
            with t.Fori(0, NG // 2) as it:
                for half in range(2):
                    g = it * 2 + half
                    t.wait_ge(taps_read, g + 1)
                    for j in range(GT):
                        for k in range(6):
                            ins = t.matmul(ps[4 + half][:, j * C:(j + 1) * C],
                                           qpad[:, k % 2, bass.ds(g * GT + (j + k // 2), 1), :].rearrange("p x n -> p (x n)"),
                                           rhsq[:, k, :], start=(k == 0), stop=(k == 5))
                    ins.then_inc(taps_done, 1)
            turn_groups(T_L1F, no_product)
            ask()
            t.matmul(ps[6][0:C, 0:B], SQ[:, 0, :], blk32[:], start=True, stop=True).then_inc(pe_done, 1)
            ask()
            t.matmul(ps[7][:, 0:8], SQ[0:C, 1:3, :].rearrange("p a c -> p (a c)"), gw1[:], start=True, stop=True).then_inc(pe_done, 1)
            ask()
            t.matmul(ps[6][:, 0:8], ones[:], SQ[:, 3, 0:8], start=True, stop=True).then_inc(pe_done, 1)
            experts(1, T_L1F, READ0[T_L2F], [up[1]])
            ask()
            t.matmul(ps[6][0:C, 0:B], SQ[:, 0, :], blk32[:], start=True, stop=True).then_inc(pe_done, 1)
            ask()
            t.matmul(ps[7][0:4, 0:B], se1[:], SQ[0:C, 1, 0:B], start=True, stop=True).then_inc(pe_done, 1)
            ask()
            t.matmul(ps[6][:, 0:C], SQ[0:4, 2:4, :].rearrange("p a c -> p (a c)"), se2[:], start=True, stop=True).then_inc(pe_done, 1)
            turn_groups(T_L2F, logits(gwp[2], 16, READ0[T_L2F]))
            ask()
            flat = aggr.rearrange("p t k -> p (t k)")
            for k in range(2):
                ins = t.matmul(ps[6 + k][:, 0:16 * MSG], ident[:], flat[:, k * 16 * MSG:(k + 1) * 16 * MSG],
                               start=True, stop=False, skip_group_check=True)
            ins.then_inc(pe_done, 1)
            total = t.value_load(rounds[0:1, 7:8], min_val=0, max_val=NBLK)
            with t.Fori(0, NBLK // SUPER) as o:
                with t.If(o * SUPER < total):
                    with t.Fori(0, SUPER // 2) as n:
                        pair = o * (SUPER // 2) + n
                        with t.If(pair * 2 < total):
                            for half in range(2):
                                b = pair * 2 + half
                                for c in range(BLK):
                                    t.wait_ge(spread_made, b * (2 * BLK) + 2 * (c + 1))
                                    for k in range(2):
                                        ins = t.matmul(ps[6 + k][:, 0:16 * MSG], onehot[:, half, c],
                                                       spread[:, half, c, k * 16:(k + 1) * 16, :].rearrange("p w m -> p (w m)"),
                                                       start=False, stop=False, skip_group_check=True)
                                ins.then_inc(block_added, 1)
            ask()
            t.drain().then_inc(pe_done, 1)
            assert asked[0] == PE_EDGES
            experts(2, T_L2F, READ0[T_WAV], [up[2]])
            ask()
            for k in range(4):
                ins = t.matmul(ps[k][:, :], rh[:], Y[:].rearrange("p t c -> p (t c)")[:, k * 512:(k + 1) * 512],
                               start=True, stop=True)
            ins.then_inc(pe_done, 1)
            turn_groups(T_WAV, logits(rcp, C, READ0[T_WAV]))
            turn_groups(T_L3F, logits(gwp[3], 8, READ0[T_L3F]))
            t.wait_ge(piece_cut, PIECES)
            experts(3, T_L3F, READ0[T_L3F] + NG, [up3[:, :, 0:UP3 // 2], up3[:, :, UP3 // 2:UP3]])

        @block.gpsimd
        def _(q):
            for m in range(3):
                q.memset(db[m][:], 0.0)
            q.engine_nop().then_inc(pool_const, 1)
            cst = [1]

            def const(ins):
                ins.then_inc(pool_const, 1)
                cst[0] += 1
                q.wait_ge(pool_const, cst[0])
            const(q.memset(ident[:], 0.0))
            const(q.memset(ones[:], 1.0))
            const(q.affine_select(out=ident[:], in_=ident[:], compare_op=ALU.not_equal, fill=1.0, base=0,
                                  pattern=[[-1, P]], channel_multiplier=1))
            const(q.tensor_copy(identb[:], ident[:]))
            const(q.tensor_copy(identh[:], ident[:]))
            const(q.affine_select(out=blk32[:], in_=ones[:, 0:B], compare_op=ALU.is_ge, fill=0.0, base=0,
                                  pattern=[[-H, B]], channel_multiplier=1))
            const(q.affine_select(out=blk32[:], in_=blk32[:], compare_op=ALU.is_ge, fill=0.0, base=H - 1,
                                  pattern=[[H, B]], channel_multiplier=-1))
            const(q.iota(iotaP[:], [[1, P]], base=0, channel_multiplier=0, allow_small_or_imprecise_dtypes=True))
            const(q.iota(iotaW[:], [[1, W]], base=0, channel_multiplier=0, allow_small_or_imprecise_dtypes=True))
            assert cst[0] == POOL_CONSTS
            q.wait_ge(ask_pool, 1)
            q.partition_all_reduce(counts[:, 0:NSEG], counts[:, 4:4 + NSEG], P, RMAX).then_inc(pool_done, 1)

            cuts = [0]

            def cut(parts, whole):
                for ins in (lambda: q.tensor_scalar(whole, whole, W_SCALE, None, ALU.mult),
                            lambda: q.tensor_copy(parts[:, 0], whole),
                            lambda: q.tensor_tensor(parts[:, 1], whole, parts[:, 0], ALU.subtract)):
                    ins().then_inc(pool_step, 1)
                    cuts[0] += 1
                    q.wait_ge(pool_step, cuts[0])

            q.wait_ge(w_in, W_LOADS * 16)
            cut(w0in, stage_w0)
            for m in (0, 2, 3):
                cut(gwp[m], stage_gw[m])
            for m in range(3):
                cut(up[m], stage_up[m])
            q.sem_inc(weights_cut, 1)

            q.wait_ge(ask_pool, 2)
            q.partition_all_reduce(small[:, 28:32], small[:, 24:28], P, RMAX).then_inc(pool_done, 1)
            q.wait_ge(tables_out, 33)
            total = q.value_load(rounds[0:1, 7:8], min_val=0, max_val=NBLK)
            with q.Fori(0, NBLK // SUPER) as o:
                with q.If(o * SUPER < total):
                    with q.Fori(0, SUPER // 2) as n:
                        pair = o * (SUPER // 2) + n
                        with q.If(pair * 2 < total):
                            for half in range(2):
                                b = pair * 2 + half
                                q.wait_ge(idx_ready, b + 1)
                                q.wait_ge(rows_used, b + 1)
                                settle(q, carried)
                                for c in range(BLK):
                                    q.indirect_dma_start(gsrc[:, half, c], None, src_rows,
                                                         bass.IndirectOffsetOnAxis(ap=ei[:, half, 1, c:c + 1].bitcast(U32), axis=0)).then_inc(src_in[half], 16)
                                    q.indirect_dma_start(gdst[:, half, c], None, dst_rows,
                                                         bass.IndirectOffsetOnAxis(ap=ei[:, half, 2, c:c + 1].bitcast(U32), axis=0)).then_inc(dst_in[half], 16)
            for n in range(PIECES):
                q.wait_ge(piece_in[n % 2], 32 * (n // 2 + 1))
                cut(up3[:, :, n * PIECE:(n + 1) * PIECE], piece[:, n % 2])
                q.sem_inc(piece_cut, 1)


def kernel(**inputs):
    import numpy as np
    import concourse.bacc as bacc
    from concourse.bass_utils import run_bass_kernel_spmd as run

    nc = bacc.Bacc("TRN2", target_bir_lowering=False, num_devices=1)
    arrays, aps = {}, {}

    def give(name, v):
        v = np.ascontiguousarray(v)
        arrays[f"in_{name}"] = v
        aps[name] = nc.dram_tensor(f"in_{name}", v.shape, mybir.dt.from_np(v.dtype), kind="ExternalInput").ap()

    i = {k: np.asarray(v) for k, v in inputs.items()}
    give("x", i["x"].reshape(P, NT, C))
    give("src", i["L2_ffn_edge_index"][0].reshape(P, EPP))
    give("dst", i["L2_ffn_edge_index"][1].reshape(P, EPP))
    give("w0in", i["L0_conv_W_in"].T)
    give("w0out", i["L0_conv_W_out"].T)
    give("c0w", i["L0_conv_conv_w"].reshape(DI, TAPS))
    give("c0b", i["L0_conv_conv_b"].reshape(DI, 1))

    def ups(w, k, f):
        e, c, h = w.shape
        r = np.zeros((c, e, k * f), w.dtype)
        r[:, :, 0:h] = w.transpose(1, 0, 2)
        return r.reshape(c, e * k * f)

    def downs(w, k, f):
        e, h, c = w.shape
        r = np.zeros((e, k * f, c), w.dtype)
        r[:, 0:h, :] = w
        return r.reshape(e * f, k, c).transpose(1, 0, 2)

    for m in range(3):
        e, k, f = MOES[m]
        give(f"up{m}", ups(i[f"L{m}_ffn_W1"], k, f))
        give(f"ub{m}", i[f"L{m}_ffn_b1"].reshape(e * f, k).T)
        give(f"dn{m}", downs(i[f"L{m}_ffn_W2"], k, f))
        give(f"db{m}", i[f"L{m}_ffn_b2"])
    e, k, f = L3F
    give("up3", np.concatenate([ups(i[f"L3_ffn_{w}"].transpose(0, 2, 1), k, f) for w in ("w1", "w3")], 1))
    give("dn3", downs(i["L3_ffn_w2"].transpose(0, 2, 1), k, f))
    give("gw0", i["L0_ffn_Wg"])
    give("gw1", i["L1_ffn_Wr"])
    give("gw2", i["L2_ffn_W_gat"])
    give("gw3", i["L3_ffn_router_w"].T)
    give("gb0", i["L0_ffn_bg"])
    give("gb1", i["L1_ffn_br"])
    give("rhs", i["L1_conv_rhs"].transpose(3, 1, 0, 2).reshape(C, 9 * C))
    give("gam1", i["L1_ffn_gamma"])
    give("bet1", i["L1_ffn_beta"])
    give("se1", i["L2_conv_w1"])
    give("se1b", i["L2_conv_b1"].reshape(4, 1))
    give("se2", i["L2_conv_w2"])
    give("se2b", i["L2_conv_b2"])
    give("att_src", i["L2_ffn_att_src"].reshape(16))
    give("att_dst", i["L2_ffn_att_dst"].reshape(16))
    give("b_gat", i["L2_ffn_b_gat"])
    give("gat_g", i["L2_ffn_ln_gamma"])
    give("gat_b", i["L2_ffn_ln_beta"])
    give("wavelet", i["L3_conv_h"])

    def masks(n, copies):
        half = n // 2
        m = np.zeros((n, FT, n), np.float32)
        for o in range(n):
            for k in range(FT):
                if (o + k) % 2:
                    at = ((o + k - 1) // 2 - (FT // 2 - 1)) % half
                    m[at, FT - 1 - k, o] = 1.0
                    m[half + at, k, o] = 1.0 if k % 2 else -1.0
        r = np.zeros((copies, n, FT, copies, n), np.float32)
        for c in range(copies):
            r[c, :, :, c, :] = m
        return r.reshape(copies * n, FT, copies * n)

    give("maskH", masks(H, B))
    give("maskC", masks(C, 1))
    out = nc.dram_tensor("out_x", (P, NT, C), F32, kind="ExternalOutput").ap()
    build_program(nc, aps, out)
    r = run(nc, [arrays], core_ids=[0])
    return np.asarray(r.results[0]["out_x"]).reshape(B, H, W, C)
```

```python
from contextlib import ExitStack

import concourse.bass as bass
from concourse import mybir

F32 = mybir.dt.float32
BF16 = mybir.dt.bfloat16
F16 = mybir.dt.float16
I32 = mybir.dt.int32
U32 = mybir.dt.uint32
ALU = mybir.AluOpType
ACT = mybir.ActivationFunctionType
AX = mybir.AxisListType
RMAX = bass.bass_isa.ReduceOp.max

P = 128
B, H, W, C = 4, 32, 32, 64
NT = W
GT = 4
TURNS = 4
NG = NT // GT
L = H * W
GN = GT * P

DI = 2 * C
TAPS = 4
XW = (NT + TAPS - 1) * P

L0F = (8, 128, 2)
L1F = (8, 128, 1)
L2F = (4, 128, 1)
L3F = (8, 114, 6)
MOES = [L0F, L1F, L2F, L3F]
CHUNK0 = [NG * sum(e * f for e, _, f in MOES[:m]) for m in range(5)]
UNIT0 = [NG * sum(e for e, _, _ in MOES[:m]) for m in range(5)]

HEADS, HK = 4, 4
N_EDGES = 262144
NODES = B * H * W
EPP = N_EDGES // P
TOP = 8
SEG = 256
NSEG = EPP // SEG
NEAR_ROUNDS = 5
NEAR_LIST = NSEG * NEAR_ROUNDS * TOP
BLK = TOP
NBLK = EPP // BLK
SHORT_BLOCKS = 24
SURE_BLOCKS = 20
SHORT_ROUNDS = SHORT_BLOCKS // NG
FQ = 64
FARB = 16
FAR_STEPS = EPP // FARB
FAR_PER_BLOCK = 2 * (FAR_STEPS // (2 * SURE_BLOCKS))
FAR_FIRST = FAR_STEPS - SURE_BLOCKS * FAR_PER_BLOCK
TABLE = (SHORT_BLOCKS + 2) * BLK
SRCW = 2 * HEADS + HEADS * HK
DSTW = 2 * HEADS
MSG = HEADS * HK + HEADS
PAD = W + 2
CAPACITY = -(-NODES * 5 // (4 * 8))
QMAX = 127.0
ROUND = 1.5 * 2.0 ** 23
FT = 8
X_SCALE, W_SCALE = 32.0, 64.0
UNSCALE = 1.0 / (X_SCALE * W_SCALE)
UP3H = 8 * 684
UP3 = 2 * UP3H + 36
DN3 = 8 * 6 * C
UP_PIECES, DN_PIECES = 6, 2
PIECE, DN_PIECE = UP3 // UP_PIECES, DN3 // DN_PIECES
PIECES = UP_PIECES + DN_PIECES
LAG = 4
KEEP_AT, TURN_AT = 10, 11
H_SCALE = 1.0 / 8
DN_UNSCALE = 1.0 / (H_SCALE * W_SCALE)


class Steps:

    def __init__(self, eng, sem):
        self.eng, self.sem, self.at, self.i, self.per, self.first = eng, sem, 0, None, 0, 0

    def __call__(self, ins):
        ins.then_inc(self.sem, 1)
        self.at += 1
        self.eng.wait_ge(self.sem, self.at if self.i is None else self.i * self.per + self.at)

    def enter(self, i, per):
        self.i, self.per, self.first = i, per, self.at

    def leave(self, times):
        assert self.at - self.first == self.per, (self.at - self.first, self.per)
        self.at = self.first + times * self.per
        self.i = None


def settle(eng, sem):
    eng.sem_inc(sem, 1)


def run_blocks(eng, total, block):
    with eng.Fori(0, SURE_BLOCKS // 2) as pair:
        for half in range(2):
            block(pair * 2 + half, pair, half, 0)
    for b in range(SURE_BLOCKS, SHORT_BLOCKS):
        with eng.If(total > b):
            block(b, b // 2, b % 2, 1)
    with eng.If(total > SHORT_BLOCKS):
        with eng.Fori(SHORT_BLOCKS // 2, NBLK // 2) as pair:
            for half in range(2):
                block(pair * 2 + half, pair, half, 2)


def build_program(nc, a, out):
    ctx = ExitStack()

    def sb(name, shape, dt=F32):
        return ctx.enter_context(nc.sbuf_tensor(name, shape, dt))

    def sem(name):
        return ctx.enter_context(nc.semaphore(name))

    with ctx:
        X = sb("X", [P, NT, C])
        XC = sb("XC", [P, NT, C])
        Y = sb("Y", [P, NT, C])
        SQ = sb("SQ", [P, NT, C])
        ACC = sb("ACC", [P, NT, C])
        yT = sb("yT", [P, NT * P], F16)
        yg = sb("yg", [P, 2, GT, 2, C], F16)
        ygf = sb("ygf", [P, 2, GT, C])
        hS = sb("hS", [P, 12, GN])
        arena = sb("arena", [P, 12288])
        keys = sb("keys", [P, EPP + 2 * BLK])
        sil = sb("sil", [P, 2, GN])
        comb = sb("comb", [P, 2, GT, C])
        ident = sb("ident", [P, P])
        identb = sb("identb", [P, P], BF16)
        identh = sb("identh", [P, P], F16)
        ones = sb("ones", [P, P])
        blk32 = sb("blk32", [P, B])
        iotaP = sb("iotaP", [P, P])
        iotaW = sb("iotaW", [P, W])
        lnsum = sb("lnsum", [P, NT])
        lnneg = sb("lnneg", [P, NT])
        lnvar = sb("lnvar", [P, NT])
        lnsd = sb("lnsd", [P, NT])
        rstd = sb("rstd", [P, NT])
        logit = sb("logit", [P, NT, 16])
        gate = sb("gate", [P, NT, 8])
        gex = sb("gex", [P, NT, 8])
        gsum = sb("gsum", [P, 4, NT])
        gst = sb("gst", [P, GT * 8])
        gTs = sb("gTs", [GT * 8, P])
        small = sb("small", [P, 256])
        w0in = sb("w0in", [P, 2, 2 * DI], F16)
        w0out = sb("w0out", [DI, C])
        c0w = sb("c0w", [DI, TAPS])
        c0b = sb("c0b", [DI, 1])
        gw1 = sb("gw1", [C, 8])
        gwp = {m: sb(f"gwp{m}", [P, 2, n], F16) for m, n in ((0, 8), (2, 16), (3, 8))}
        gb = [sb(f"gb{m}", [P, 16]) for m in range(4)]
        up = [sb(f"up{m}", [P, 2, e * f * k], F16) for m, (e, k, f) in enumerate(MOES[:3])]
        ub = [sb(f"ub{m}", [P, e * f]) for m, (e, k, f) in enumerate(MOES[:3])]
        dn = [sb(f"dn{m}", [k, e * f, C]) for m, (e, k, f) in enumerate(MOES[:3])]
        dn3 = sb("dn3", [P, DN3 // C, 2 * C], F16)
        db = [sb(f"db{m}", [GT * 8, GT, C]) for m in range(3)]
        rhsq = sb("rhsq", [P, 6, C], BF16)
        seg = sb("seg", [P, SEG])
        best = sb("best", [P, NEAR_ROUNDS * TOP])
        srow = sb("srow", [P, C])
        gam1 = sb("gam1", [P, C])
        bet1 = sb("bet1", [P, C])
        se1 = sb("se1", [C, 4])
        se1b = sb("se1b", [4, 1])
        se2 = sb("se2", [4, C])
        se2b = sb("se2b", [P, C])
        att = sb("att", [P, 2, 16])
        gatv = sb("gatv", [P, 3, 16])
        hb = sb("hb", [P, 2, FT])
        rc = sb("rc", [P, C])
        rcp = sb("rcp", [P, 2, C], F16)
        rh = sb("rh", [P, P])
        twoid = sb("twoid", [P, C])
        lastsel = sb("lastsel", [P, P])
        halfsel = sb("halfsel", [FQ, 2, P])
        zerob = sb("zerob", [P, P], BF16)
        iotaQ = sb("iotaQ", [P, FQ, FARB], BF16)
        farhi = sb("farhi", [P, EPP], BF16)
        farlo = sb("farlo", [P, EPP], BF16)
        segcnt = sb("segcnt", [P, NSEG])
        counts = sb("counts", [P, 2, 2])
        plan = sb("plan", [P, 4], I32)
        fardst = sb("fardst", [P, NT])

        esrc = arena[:, 0:EPP].bitcast(I32)
        edst = arena[:, EPP:2 * EPP].bitcast(I32)
        isnear, nodebits = Y[:].rearrange("p t c -> p (t c)"), SQ[:].rearrange("p t c -> p (t c)").bitcast(I32)
        farhot = Y[:].rearrange("p t c -> p (t c)").bitcast(BF16).rearrange("p (s k q c) -> p s k q c", s=2, k=2, q=FQ)
        farcnt = Y[0:FQ].rearrange("p t c -> p (t c)")[:, 0:FQ]
        xbuf = arena[:, 0:XW]
        zs = arena[:, XW:XW + NT * P]
        spread = arena[:, 0:2 * BLK * W * MSG].rearrange("p (s c w m) -> p s c w m", s=2, c=BLK, w=W)
        onehot = arena[:, 10240:10240 + 2 * BLK * P].rearrange("p (s c q) -> p s c q", s=2, c=BLK)
        up3 = arena[:, 0:UP3].bitcast(F16).rearrange("p (k n) -> p k n", k=2)
        nearlist = sil[:].rearrange("p a n -> p (a n)")[:, 512:512 + NEAR_LIST]
        shortlist = sil[:].rearrange("p a n -> p (a n)")[:, 832:832 + SHORT_BLOCKS * BLK]
        outs = farlo[:].bitcast(F32).rearrange("p (s n) -> p s n", s=2)
        hid = farhi[:].bitcast(F32).rearrange("p (s n) -> p s n", s=2)
        hidp = hS[:].rearrange("p a n -> p (a n)").bitcast(F16).rearrange("p (a k n) -> p a k n", a=12, k=2)
        stage_up, at = [], XW + NT * P
        for e, k, f in MOES[:3]:
            stage_up.append(arena[:, at:at + e * k * f])
            at += e * k * f
        assert at <= 12288
        sil_flat = sil[:].rearrange("p a n -> p (a n)")
        stage_w0 = sil_flat[:, 0:2 * DI]
        stage_gw = {m: sil_flat[:, o:o + n] for m, o, n in ((0, 256, 8), (2, 264, 16), (3, 280, 8))}
        cu = hS[:, 0:2, :]
        csu = hS[:, 2:4, :]
        cy = hS[:, 4:6, :]
        qg = hS[:, 0:1, :].rearrange("p a n -> p (a n)").bitcast(BF16).rearrange("p (s t d c) -> p s t d c", s=2, t=GT, d=2)
        qf = hS[:, 1, :].rearrange("p (s t c) -> p s t c", s=2, t=GT)
        wqf = hS[0:C, 2:4, :].rearrange("p a n -> p (a n)")[:, 0:576]
        wqb = hS[0:C, 9:12, :].rearrange("p a n -> p (a n)")[:, 600:600 + 288].bitcast(BF16)
        qpad = hS[:, 2:11, :].rearrange("p a n -> p (a n)").bitcast(BF16)[:, 0:2 * PAD * P].rearrange(
            "p (k x n) -> p k x n", k=2, x=PAD)
        rq = hS[0:C, 9:12, :].rearrange("p a n -> p (a n)")
        maskH = hS[:, 0:2, :].rearrange("p a n -> p (a n)").rearrange("p (t q) -> p t q", t=FT)
        maskC = hS[:, 2:3, :].rearrange("p a n -> p (a n)").rearrange("p (t q) -> p t q", t=FT)
        piece = hS[:, 3:12, :].rearrange("p a n -> p (a n)")[:, 0:2 * PIECE].rearrange("p (s n) -> p s n", s=2)
        hn = hS[:, 0, :].rearrange("p (t k) -> p t k", t=NT)
        stab = hS[:, 1:3, :].rearrange("p a n -> p (a n)")[:, 0:NT * SRCW].rearrange("p (t k) -> p t k", t=NT)
        dtab = hS[:, 3, 0:NT * DSTW].rearrange("p (t k) -> p t k", t=NT)
        gsrc = hS[:, 4, 0:2 * BLK * SRCW].rearrange("p (s c k) -> p s c k", s=2, c=BLK)
        gdst = hS[:, 5, 0:2 * BLK * DSTW].rearrange("p (s c k) -> p s c k", s=2, c=BLK)
        em = hS[:, 6, 0:2 * BLK * MSG].rearrange("p (s c k) -> p s c k", s=2, c=BLK)
        ei = hS[:, 7, 0:2 * 2 * BLK].bitcast(I32).rearrange("p (s k c) -> p s k c", s=2, k=2)
        epart = hS[:, 7, 128:128 + 2 * BLK].bitcast(I32).rearrange("p (k c) -> p k c", k=2)
        ef = hS[:, 8, 0:2 * 2 * BLK].rearrange("p (s k c) -> p s k c", s=2, k=2)
        ew = hS[:, 8, 64:64 + BLK * 2 * HEADS].rearrange("p (c k) -> p c k", c=BLK)
        offset = XC[:].rearrange("p t c -> p (t c)")[:, 1024:1024 + BLK * P].rearrange("p (c q) -> p c q", c=BLK)
        nodes = XC[:].rearrange("p t c -> p (t c)")[:, 0:2 * TABLE].bitcast(I32).rearrange("p (k c) -> p k c", k=2)
        places = XC[:].rearrange("p t c -> p (t c)")[:, 2 * TABLE:4 * TABLE].rearrange("p (k c) -> p k c", k=2)
        spare = SQ[:].rearrange("p t c -> p (t c)")[:, 0:2 * TABLE].bitcast(I32).rearrange("p (k c) -> p k c", k=2)
        av = hS[:, 11, 0:4 * NT * HEADS].rearrange("p (k t h) -> p k t h", k=4, t=NT)
        aggr = hS[:, 9:11, :].rearrange("p a n -> p (a n)")[:, 0:NT * MSG].rearrange("p (t k) -> p t k", t=NT)

        ps = [ctx.enter_context(nc.psum_tensor(f"ps{n}", [P, 512], F32)) for n in range(8)]
        src_rows = nc.dram_tensor("src_rows", [NODES, SRCW], F32, kind="Internal").ap()
        dst_rows = nc.dram_tensor("dst_rows", [NODES, DSTW], F32, kind="Internal").ap()

        x_in = sem("x_in")
        edges_in = sem("edges_in")
        w0_in = sem("w0_in")
        w_in = sem("w_in")
        masks_in = sem("masks_in")
        piece_in = [sem(f"piece_in{h}") for h in range(2)]
        piece_cut = sem("piece_cut")
        weights_cut = sem("weights_cut")
        edges_left = sem("edges_left")
        tables_out = sem("tables_out")
        stored = sem("stored")
        pool_const = sem("pool_const")
        carried = sem("carried")
        dve_step = sem("dve_step")
        act_step = sem("act_step")
        pool_step = sem("pool_step")
        ask_act, act_done = sem("ask_act"), sem("act_done")
        ask_pe, pe_done = sem("ask_pe"), sem("pe_done")
        ask_pool, pool_done = sem("ask_pool"), sem("pool_done")
        group_made = sem("group_made")
        group_turned = sem("group_turned")
        turned_copied = sem("turned_copied")
        turned_used = sem("turned_used")
        product_read = sem("product_read")
        xz_copied = sem("xz_copied")
        conv_made = sem("conv_made")
        conv_silu = sem("conv_silu")
        conv_gated = sem("conv_gated")
        conv_out = sem("conv_out")
        conv_added = sem("conv_added")
        hid_full = sem("hid_full")
        hid_act = sem("hid_act")
        hid_made = sem("hid_made")
        high_done = sem("high_done")
        low_done = [sem(f"low_done{h}") for h in range(2)]
        out_kept = sem("out_kept")
        out_turned = sem("out_turned")
        sil_done = sem("sil_done")
        down_done = sem("down_done")
        comb_done = sem("comb_done")
        gate_staged = sem("gate_staged")
        gate_turned = sem("gate_turned")
        gate_copied = sem("gate_copied")
        bias_done = sem("bias_done")
        bias_read = sem("bias_read")
        q_turned = sem("q_turned")
        q_low = sem("q_low")
        q_high = sem("q_high")
        taps_done = sem("taps_done")
        taps_read = sem("taps_read")
        list_kept = sem("list_kept")
        far_made = sem("far_made")
        far_counted = sem("far_counted")
        idx_ready = sem("idx_ready")
        rows_used = sem("rows_used")
        src_in = [sem(f"src_in{h}") for h in range(2)]
        dst_in = [sem(f"dst_in{h}") for h in range(2)]
        edge_step = sem("edge_step")
        rest_step = sem("rest_step")
        places_cut = sem("places_cut")
        hot_made = sem("hot_made")
        offset_made = sem("offset_made")
        spread_made = sem("spread_made")
        block_added = sem("block_added")

        RING2 = [group_turned, turned_copied, turned_used, product_read, conv_silu,
                 conv_gated, conv_out, conv_added, hid_full, hid_act, hid_made, high_done, out_kept, out_turned,
                 sil_done, down_done, comb_done,
                 q_turned, q_low, q_high, taps_done, taps_read, block_added, rows_used,
                 far_counted, hot_made]
        RING1 = [gate_turned, gate_copied, bias_done, bias_read] + low_done

        W_LOADS = 46
        POOL_CONSTS = 17
        PE_EDGES = 14

        block = ctx.enter_context(nc.Block())

        T_L0C, T_L0F, T_L1F, T_L2F, T_WAV, T_L3F = range(6)
        READ0 = {T_L0F: 0, T_L2F: NG, T_WAV: 2 * NG, T_L3F: 3 * NG}

        @block.sync
        def _(sp):
            sp.dma_start(X[:], a["x"]).then_inc(x_in, 16)
            for half in range(2):
                sp.dma_start(stage_w0[half * C:(half + 1) * C], a["w0in"]).then_inc(w0_in, 16)
            sp.dma_start(edst, a["dst"]).then_inc(edges_in, 16)
            sp.dma_start(esrc, a["src"]).then_inc(edges_in, 16)
            sp.dma_start(w0out[:], a["w0out"]).then_inc(w0_in, 16)
            sp.dma_start(c0w[:], a["c0w"]).then_inc(w0_in, 16)
            sp.dma_start(c0b[:], a["c0b"]).then_inc(w0_in, 16)
            n_w = [0]

            def load(dst, src):
                n_w[0] += 16
                sp.dma_start(dst, src).then_inc(w_in, 16)

            def rows(v):
                return v.partition_broadcast(P)

            def load_twice(dst, src):
                load(dst[0:C], src)
                load(dst[C:P], src)

            for m, (e, k, f) in enumerate(MOES):
                if m < 3:
                    load_twice(stage_up[m], a[f"up{m}"])
                    load(ub[m][0:k, :], a[f"ub{m}"])
                    load(dn[m][:], a[f"dn{m}"])
                if m == 1:
                    load(gw1[:], a["gw1"])
                else:
                    load_twice(stage_gw[m], a[f"gw{m}"])
            for m in range(2):
                load(gb[m][:, 0:8], rows(a[f"gb{m}"]))
            sp.wait_ge(pool_const, 1)
            for m in range(3):
                e = MOES[m][0]
                for j in range(GT):
                    load(db[m][j * 8:j * 8 + e, j, :], a[f"db{m}"])
            load(rq[:, 0:576], a["rhs"])
            load(gam1[:], rows(a["gam1"]))
            load(bet1[:], rows(a["bet1"]))
            load(se1[:], a["se1"])
            load(se1b[:], a["se1b"])
            load(se2[:], a["se2"])
            load(se2b[:], rows(a["se2b"]))
            load(att[:, 0, :], rows(a["att_src"]))
            load(att[:, 1, :], rows(a["att_dst"]))
            load(gatv[:, 0, :], rows(a["b_gat"]))
            load(gatv[:, 1, :], rows(a["gat_g"]))
            load(gatv[:, 2, :], rows(a["gat_b"]))
            load(hb[:, 0, :], rows(a["wavelet"]))
            assert n_w[0] == W_LOADS * 16, n_w[0] // 16
            sp.wait_ge(tables_out, 1)
            sp.dma_start(src_rows.rearrange("(p t) k -> p (t k)", p=P), stab.rearrange("p t k -> p (t k)")).then_inc(tables_out, 16)
            sp.dma_start(dst_rows.rearrange("(p t) k -> p (t k)", p=P), dtab.rearrange("p t k -> p (t k)")).then_inc(tables_out, 16)
            sp.wait_ge(pe_done, PE_EDGES)
            sp.wait_ge(edges_left, 1)
            for n in range(PIECES):
                if n >= 2:
                    sp.wait_ge(piece_cut, n - 1)
                if n < UP_PIECES:
                    for half in range(2):
                        sp.dma_start(piece[half * C:(half + 1) * C, n % 2], a["up3"][:, n * PIECE:(n + 1) * PIECE]).then_inc(piece_in[n % 2], 16)
                else:
                    k = n - UP_PIECES
                    sp.dma_start(piece[:, n % 2, 0:DN_PIECE], a["dn3"][:, k * DN_PIECE:(k + 1) * DN_PIECE]).then_inc(piece_in[n % 2], 32)
            sp.wait_ge(masks_in, 1)
            sp.dma_start(maskH, a["maskH"]).then_inc(masks_in, 16)
            for half in range(2):
                sp.dma_start(maskC[half * C:(half + 1) * C], a["maskC"]).then_inc(masks_in, 16)
            sp.wait_ge(stored, 1)
            sp.dma_start(out, X[:]).then_inc(stored, 16)
            sp.wait_ge(stored, 17)

        @block.vector
        def _(v):
            st = Steps(v, dve_step)
            asked = {"act": 0, "pe": 0, "pool": 0}
            asks = {"act": (ask_act, act_done), "pe": (ask_pe, pe_done), "pool": (ask_pool, pool_done)}

            def ask(who, ins):
                ins.then_inc(asks[who][0], 1)
                asked[who] += 1

            def answer(who):
                v.wait_ge(asks[who][1], asked[who])

            def bc(ap, shape):
                return ap.to_broadcast(shape)

            for s in RING2:
                v.sem_inc(s, 2)
            for s in RING1:
                v.sem_inc(s, 1)
            v.sem_inc(xz_copied, 4)

            v.wait_ge(x_in, 16)

            def layer_norm(src, eps):
                st(v.tensor_reduce(lnsum[:], src[:], AX.X, ALU.add))
                st(v.tensor_scalar(lnneg[:], lnsum[:], -1.0 / C, None, ALU.mult))
                ask("act", v.tensor_tensor(XC[:], src[:], bc(lnneg[:].unsqueeze(2), [P, NT, C]), ALU.add))
                answer("act")
                st(v.tensor_reduce(lnvar[:], SQ[:], AX.X, ALU.add))
                ask("act", v.tensor_scalar(lnvar[:], lnvar[:], 1.0 / C, eps, ALU.mult, ALU.add))
                answer("act")
                st(v.reciprocal(rstd[:], lnsd[:]))

            def normalised(dst):
                st(v.tensor_tensor(dst[:], XC[:], bc(rstd[:].unsqueeze(2), [P, NT, C]), ALU.mult))

            def turn_groups(stage, made, read=None):
                per = made[1] * TURNS
                with v.Fori(0, NG // TURNS) as it:
                    st.enter(it, per)

                    def make(k):
                        v.wait_ge(group_turned, it * TURNS + (k + NG * stage + 1))
                        made[0](it * TURNS + k, k % 2)

                    def take(k):
                        v.wait_ge(turned_used, it * TURNS + (k + NG * stage + 3))
                        read(it * TURNS + k, k % 2)
                    for k in range(2):
                        make(k)
                    for k in range(TURNS):
                        if k + 2 < TURNS:
                            make(k + 2)
                        if read:
                            take(k)
                    st.leave(NG // TURNS)

            def group_norm(g, half):
                st(v.scalar_tensor_tensor(ygf[:, half], XC[:, bass.ds(g * GT, GT), :], X_SCALE,
                                          bc(rstd[:, bass.ds(g * GT, GT)].unsqueeze(2), [P, GT, C]), ALU.mult, ALU.mult))
                cut_group(half)

            def cut_group(half):
                st(v.tensor_copy(yg[:, half, :, 0], ygf[:, half]))
                v.tensor_tensor(yg[:, half, :, 1], ygf[:, half], yg[:, half, :, 0], ALU.subtract).then_inc(group_made, 1)

            def read_logits(width, bias, dst):
                def read(g, half):
                    o = ps[2 + half][:, 0:GT * width].rearrange("p (t k) -> p t k", t=GT)
                    d = dst[:, bass.ds(g * GT, GT), 0:width]
                    if bias is None:
                        v.tensor_scalar(d, o, UNSCALE, None, ALU.mult).then_inc(product_read, 1)
                    else:
                        v.scalar_tensor_tensor(d, o, UNSCALE, bc(bias.unsqueeze(1), [P, GT, width]), ALU.mult, ALU.add).then_inc(product_read, 1)
                return read

            def top2_gates(n_tiles, E, eps=None):
                lg, gx, gt = (z[:, 0:n_tiles, 0:E] for z in (logit, gex, gate))
                beats = SQ[:].rearrange("p t c -> p (t c)")[:, 0:n_tiles * E * E].rearrange("p (t e f) -> p t e f", t=n_tiles, e=E)
                mx, sm, z, rec = (gsum[:, k, 0:n_tiles] for k in range(4))
                st(v.tensor_reduce(mx, lg, AX.X, ALU.max))
                ask("act", v.tensor_tensor(gx, lg, bc(mx.unsqueeze(2), [P, n_tiles, E]), ALU.subtract))
                for e in range(E):
                    if e:
                        st(v.tensor_tensor(beats[:, :, e, 0:e], lg[:, :, 0:e], bc(lg[:, :, e:e + 1], [P, n_tiles, e]), ALU.is_ge))
                    st(v.tensor_tensor(beats[:, :, e, e:E], lg[:, :, e:E], bc(lg[:, :, e:e + 1], [P, n_tiles, E - e]), ALU.is_gt))
                st(v.tensor_reduce(gt, beats, AX.X, ALU.add))
                st(v.tensor_scalar(gt, gt, 1.5, None, ALU.is_lt))
                answer("act")
                st(v.tensor_tensor(gt, gt, gx, ALU.mult))
                st(v.tensor_reduce(sm, gt, AX.X, ALU.add))
                if eps is not None:
                    st(v.tensor_reduce(z, gx, AX.X, ALU.add))
                    st(v.scalar_tensor_tensor(sm, z, eps, sm, ALU.mult, ALU.add))
                st(v.reciprocal(rec, sm))
                st(v.tensor_tensor(gt, gt, bc(rec.unsqueeze(2), [P, n_tiles, E]), ALU.mult))

            def softmax_row():
                lg, mx, sm, rec = logit[:, 0, 0:8], gsum[:, 0, 0:1], gsum[:, 1, 0:1], gsum[:, 2, 0:1]
                st(v.tensor_reduce(mx, lg, AX.X, ALU.max))
                ask("act", v.tensor_scalar(gex[:, 0, 0:8], lg, mx, None, ALU.subtract))
                answer("act")
                st(v.tensor_reduce(sm, gex[:, 0, 0:8], AX.X, ALU.add))
                st(v.reciprocal(rec, sm))
                st(v.tensor_scalar(lg, gex[:, 0, 0:8], rec, None, ALU.mult))

            def image_means():
                ask("pe", v.tensor_reduce(SQ[:, 0, :], Y[:].rearrange("p t c -> p c t"), AX.X, ALU.add))
                answer("pe")

            def round_clip(dst, src, scale, tmp):
                st(v.tensor_scalar(tmp, src, scale, ROUND, ALU.mult, ALU.add))
                st(v.tensor_scalar(tmp, tmp, ROUND, QMAX, ALU.subtract, ALU.min))
                return v.tensor_scalar(dst, tmp if len(dst.shape) == len(tmp.shape) else
                                       bc(tmp.unsqueeze(2), list(dst.shape)), -QMAX, None, ALU.max)

            def sort_round(source, r):
                b = best[:, r * TOP:(r + 1) * TOP]
                settle(v, carried)
                st(v.max(b, source))
                settle(v, carried)
                st(v.match_replace(source, b, source, 0.0))

            def sort_segment(g, e):
                if e == 0:
                    st(v.tensor_copy(seg[:], keys[:, bass.ds(g * SEG, SEG)]))
                if e < NEAR_ROUNDS:
                    sort_round(seg[:], e)
                if e == NEAR_ROUNDS:
                    st(v.tensor_copy(nearlist[:, bass.ds(g * (NEAR_ROUNDS * TOP), NEAR_ROUNDS * TOP)], best[:]))

            def sort_list(g, e):
                if e < SHORT_ROUNDS:
                    sort_round(nearlist, e)
                if e == SHORT_ROUNDS:
                    st(v.tensor_copy(shortlist[:, bass.ds(g * (SHORT_ROUNDS * TOP), SHORT_ROUNDS * TOP)],
                                     best[:, 0:SHORT_ROUNDS * TOP]))

            def experts(m, T, beside=None, beside_steps=0):
                E, KH, FC = MOES[m]
                bias = m < 3
                with v.Fori(0, NG) as g:
                    st.enter(g, E + (2 if bias else 1) + beside_steps)
                    if bias:
                        v.wait_ge(gate_turned, g + NG * m + 1)
                    st(v.tensor_copy(gst[:].rearrange("p (t e) -> p t e", t=GT), gate[:, bass.ds(g * GT, GT), :]))
                    tg = T[:, bass.ds(g * GT, GT), :]
                    if bias:
                        v.sem_inc(gate_staged, 1)
                        v.wait_ge(bias_done, g + NG * m + 2)
                        st(v.tensor_tensor(tg, tg, ps[7][:, 0:GT * C].rearrange("p (t c) -> p t c", t=GT), ALU.add))
                        v.sem_inc(bias_read, 1)

                    def combine(e):
                        u = g * E + (e + UNIT0[m])
                        v.wait_ge(down_done, u + 3)
                        v.tensor_tensor(comb[:, e % 2], ps[4 + e % 2][:, 0:GT * C].rearrange("p (t c) -> p t c", t=GT),
                                        bc(gst[:].rearrange("p (t e) -> p t e", t=GT)[:, :, e:e + 1], [P, GT, C]),
                                        ALU.mult).then_inc(comb_done, 1)
                        v.wait_ge(comb_done, u + 3)
                        st(v.tensor_tensor(tg, tg, comb[:, e % 2], ALU.add))

                    for e in range(E):
                        if beside:
                            beside(g, e)
                        combine(e)
                    st.leave(NG)

            def experts3():
                E, KH, FC = L3F
                st(v.tensor_scalar(gate[:], gate[:], DN_UNSCALE, None, ALU.mult))

                def whole(g, k):
                    v.wait_ge(sil_done, g * (E * FC) + (k + 3))
                    v.wait_ge(low_done[k % 2], g * (E * FC // 2) + (k // 2 + 1))
                    v.scalar_tensor_tensor(hid[:, k % 2], ps[2 + k % 2][:, :], UNSCALE * H_SCALE,
                                           sil[:, k % 2, :], ALU.mult, ALU.mult).then_inc(hid_made, 1)
                    if k % 2:
                        slot = hidp[:, (k - 1) % (2 * FC)]
                        v.wait_ge(high_done, g * (E * FC) + (k + 2))
                        v.tensor_tensor(slot[:, 1], hid[:, 0], slot[:, 0], ALU.subtract).then_inc(low_done[0], 1)

                def combine(g, e):
                    xg = X[:, bass.ds(g * GT, GT), :]
                    v.wait_ge(out_turned, g * E + (e + 3))
                    v.tensor_tensor(comb[:, e % 2], ps[6 + e % 2][:, 0:GT * C].rearrange("p (t c) -> p t c", t=GT),
                                    bc(gst[:].rearrange("p (t e) -> p t e", t=GT)[:, :, e:e + 1], [P, GT, C]),
                                    ALU.mult).then_inc(comb_done, 1)
                    v.wait_ge(comb_done, g * E + (e + UNIT0[3] + 3))
                    st(v.tensor_tensor(xg, xg, comb[:, e % 2], ALU.add))

                def rest_of_group(g, last):
                    st(v.tensor_copy(gst[:].rearrange("p (t e) -> p t e", t=GT), gate[:, bass.ds(g * GT, GT), :]))
                    for k in range(LAG, E * FC):
                        whole(g, k)
                        if k % FC == 0 and k >= 2 * FC:
                            combine(g, k // FC - 2)
                    for k in range(LAG):
                        if not last:
                            whole(g + 1, k)
                        if k == 0:
                            combine(g, E - 2)
                    combine(g, E - 1)

                for k in range(LAG):
                    whole(0, k)
                with v.Fori(0, NG - 1) as g:
                    st.enter(g, 1 + E)
                    rest_of_group(g, False)
                    st.leave(NG - 1)
                rest_of_group(NG - 1, True)

            layer_norm(X, 1e-6)

            v.wait_ge(edges_in, 32)
            st(v.tensor_scalar(isnear, edst, float(NODES), None, ALU.is_lt))
            st(v.scalar_tensor_tensor(isnear, esrc, float(NODES - 1), isnear, ALU.is_lt, ALU.mult))
            st(v.tensor_reduce(segcnt[:], isnear.rearrange("p (s c) -> p s c", s=NSEG), AX.X, ALU.add))
            st(v.tensor_reduce(counts[:, 0, 0:1], segcnt[:], AX.X, ALU.max))
            ask("pool", v.tensor_reduce(counts[:, 0, 1:2], segcnt[:], AX.X, ALU.add))
            near = keys[:, 0:EPP]
            st(v.scalar_tensor_tensor(near, edst, float(NODES), esrc, ALU.mult, ALU.add))
            st(v.scalar_tensor_tensor(near, near, 1.0, isnear, ALU.add, ALU.mult))
            st(v.memset(keys[:, EPP:EPP + 2 * BLK], 0.0))
            st(v.tensor_scalar(nodebits, edst, 6, None, ALU.logical_shift_right))
            st(v.scalar_tensor_tensor(farhi[:], isnear, 1024.0, nodebits, ALU.mult, ALU.add))
            st(v.tensor_scalar(nodebits, edst, FQ - 1, None, ALU.bitwise_and))
            st(v.tensor_copy(farlo[:], nodebits))
            answer("pool")
            st(v.tensor_scalar(segcnt[:, 0:1], counts[:, 1, 0:1], float(NEAR_ROUNDS * TOP), None, ALU.is_gt))
            st(v.tensor_scalar(segcnt[:, 1:2], counts[:, 1, 1:2], float(SHORT_BLOCKS * BLK), None, ALU.is_gt))
            st(v.tensor_tensor(plan[:, 1:2], segcnt[:, 0:1], segcnt[:, 1:2], ALU.max))
            st(v.tensor_scalar(plan[:, 0:1], counts[:, 1, 1:2], float(BLK - 1), None, ALU.add))
            st(v.tensor_scalar(plan[:, 0:1], plan[:, 0:1], 3, None, ALU.logical_shift_right))
            st(v.tensor_scalar(plan[:, 2:3], plan[:, 1:2], NBLK, None, ALU.mult))
            st(v.tensor_tensor(plan[:, 0:1], plan[:, 0:1], plan[:, 2:3], ALU.max))
            v.wait_ge(w0_in, 80)
            v.wait_ge(pool_const, POOL_CONSTS)
            v.wait_ge(weights_cut, 1)

            turn_groups(T_L0C, (group_norm, 2))
            v.wait_ge(xz_copied, 4 + 2 * NG)
            st(v.memset(xbuf[:, 0:(TAPS - 1) * P], 0.0))
            prev = xbuf[:, NT * P:XW].rearrange("p (t b h) -> p t b h", t=TAPS - 1, b=B)
            head = xbuf[:, 0:(TAPS - 1) * P].rearrange("p (t b h) -> p t b h", t=TAPS - 1, b=B)
            for t in range(TAPS - 1):
                st(v.tensor_copy(head[:, t, :, 1:H], prev[:, t, :, 0:H - 1]))
            with v.Fori(0, NG // 2) as it:
                st.enter(it, 2 * (TAPS - 1) + 2)
                for half in range(2):
                    g = it * 2 + half
                    v.wait_ge(conv_silu, g + 1)
                    st(v.tensor_scalar(cu[:, half], xbuf[:, bass.ds(g * GN, GN)], c0w[:, 0:1], None, ALU.mult))
                    for k in range(1, TAPS):
                        ins = v.scalar_tensor_tensor(cu[:, half], xbuf[:, bass.ds(g * GN + k * P, GN)], c0w[:, k:k + 1],
                                                     cu[:, half], ALU.mult, ALU.add)
                        if k == TAPS - 1:
                            ins.then_inc(conv_made, 1)
                        else:
                            st(ins)
                for half in range(2):
                    g = it * 2 + half
                    v.wait_ge(conv_silu, g + 3)
                    v.wait_ge(conv_out, g + 1)
                    v.scalar_tensor_tensor(cy[:, half], csu[:, half], 4.0, zs[:, bass.ds(g * GN, GN)], ALU.mult,
                                           ALU.mult).then_inc(conv_gated, 1)
                for half in range(2):
                    g = it * 2 + half
                    v.wait_ge(conv_out, g + 3)
                    xg = X[:, bass.ds(g * GT, GT), :]
                    st(v.tensor_tensor(xg, xg, ps[half][:, 0:GT * C].rearrange("p (t c) -> p t c", t=GT), ALU.add))
                    v.sem_inc(conv_added, 1)
                st.leave(NG // 2)

            layer_norm(X, 1e-5)
            v.wait_ge(w_in, W_LOADS * 16)
            turn_groups(T_L0F, (group_norm, 2), read_logits(8, gb[0][:, 0:8], logit))
            v.wait_ge(product_read, 2 + NG)
            top2_gates(NT, 8)
            experts(0, X, sort_segment, 2 * NEAR_ROUNDS + 2)

            amax, scale, inv = small[0:C, 8:9], small[0:C, 9:10], small[0:C, 10:11]
            st(v.tensor_reduce(amax, rq[:, 0:576], AX.X, ALU.max, apply_absolute_value=True))
            st(v.tensor_scalar(scale, amax, 1e-6, 1.0 / QMAX, ALU.max, ALU.mult))
            st(v.reciprocal(inv, scale))
            ask("pe", round_clip(wqb, rq[:, 0:576], inv, wqf))
            answer("pe")
            st(v.memset(rhsq[:], 0.0))
            wt = ps[6][:, 0:3 * C].bitcast(BF16).rearrange("p (k o) -> p k o", k=6)
            st(v.tensor_copy(rhsq[:, 0:6:2, :], wt[:, 0:6:2, :]))
            st(v.tensor_copy(rhsq[0:C, 1:6:2, :], wt[0:C, 1:6:2, :]))
            ask("pe", v.tensor_copy(SQ[0:C, 0:2, :].rearrange("p a c -> p (a c)"), bc(scale, [C, P])))
            answer("pe")
            st(v.tensor_copy(srow[:], ps[7][:, 0:C]))
            st(v.memset(qpad, 0.0))
            layer_norm(X, 1e-6)
            normalised(Y)
            ask("pe", v.tensor_reduce(small[:, 11:12], Y[:].rearrange("p t c -> p (t c)"), AX.X, ALU.max,
                                      apply_absolute_value=True))
            answer("pe")
            st(v.tensor_reduce(small[0:1, 12:16], ps[6][0:1, 0:P].rearrange("p (b h) -> p b h", b=B), AX.X, ALU.max))
            ask("pe", v.tensor_copy(SQ[0:1, 0:2, :].rearrange("p a c -> p (a c)").rearrange("p (b h) -> p b h", b=B),
                                    bc(small[0:1, 12:16].unsqueeze(2), [1, B, H])))
            answer("pe")
            st(v.tensor_scalar(small[:, 16:17], ps[7][:, 0:1], 1e-6, 1.0 / QMAX, ALU.max, ALU.mult))
            st(v.reciprocal(small[:, 17:18], small[:, 16:17]))
            with v.Fori(0, NG // 2) as it:
                st.enter(it, 4)
                for half in range(2):
                    g = it * 2 + half
                    v.wait_ge(q_turned, g + 1)
                    round_clip(qg[:, half], Y[:, bass.ds(g * GT, GT), :], small[:, 17:18], qf[:, half]).then_inc(group_made, 1)
                for half in range(2):
                    g = it * 2 + half
                    v.wait_ge(q_turned, g + 3)
                    v.tensor_copy(qpad[C:P, 0, bass.ds(g * GT + 1, GT), :].rearrange("p x n -> p (x n)"),
                                  ps[half][C:P, 0:GT * C].bitcast(BF16)).then_inc(q_high, 1)
                st.leave(NG // 2)
            with v.Fori(0, NG // 2) as it:
                st.enter(it, 4)
                for half in range(2):
                    g = it * 2 + half
                    v.wait_ge(taps_done, g + 3)
                    xg = X[:, bass.ds(g * GT, GT), :]
                    st(v.scalar_tensor_tensor(comb[:, half], ps[4 + half][:, 0:GT * C].rearrange("p (t c) -> p t c", t=GT),
                                              small[:, 16:17], bc(srow[:].unsqueeze(1), [P, GT, C]), ALU.mult, ALU.mult))
                    v.sem_inc(taps_read, 1)
                    st(v.tensor_tensor(xg, xg, comb[:, half], ALU.add))
                st.leave(NG // 2)

            layer_norm(X, 1e-5)
            turn_groups(T_L1F, (group_norm, 2))
            normalised(Y)
            image_means()
            ask("pe", v.tensor_scalar(SQ[0:C, 1:3, :].rearrange("p a c -> p (a c)").rearrange("p (b h) -> p b h", b=B),
                                      bc(ps[6][0:C, 0:B].unsqueeze(2), [C, B, H]), 1.0 / L, None, ALU.mult))
            answer("pe")
            st(v.tensor_tensor(logit[:, 0, 0:8], ps[7][:, 0:8], gb[1][:, 0:8], ALU.add))
            softmax_row()
            ask("pe", v.tensor_copy(SQ[:, 3, 0:8], logit[:, 0, 0:8]))
            answer("pe")
            load = SQ[:, 4, 0:8]
            st(v.tensor_scalar(load, ps[6][:, 0:8], float(L // H), None, ALU.mult))
            st(v.reciprocal(load, load))
            st(v.tensor_scalar(load, load, float(CAPACITY), 1.0, ALU.mult, ALU.min))
            st(v.tensor_tensor(logit[:, 0, 0:8], logit[:, 0, 0:8], load, ALU.mult))
            softmax_row()
            top2_gates(1, 8)
            st(v.tensor_copy(gate[:, 1:NT, :], bc(gate[:, 0:1, :], [P, NT - 1, 8])))
            experts(1, Y, sort_list, 2 * SHORT_ROUNDS + 1)
            unsorted = v.value_load(plan[0:1, 1:2], min_val=0, max_val=1)
            with v.If(unsorted < 1):
                v.tensor_copy(keys[:, 0:SHORT_BLOCKS * BLK], shortlist).then_inc(list_kept, 1)
                v.wait_ge(list_kept, 1)
                settle(v, carried)
            layer_norm(Y, 1e-5)
            normalised(Y)
            st(v.tensor_tensor(Y[:], Y[:], bc(gam1[:].unsqueeze(1), [P, NT, C]), ALU.mult))
            st(v.tensor_tensor(Y[:], Y[:], bc(bet1[:].unsqueeze(1), [P, NT, C]), ALU.add))
            st(v.tensor_tensor(X[:], X[:], Y[:], ALU.add))

            layer_norm(X, 1e-6)
            normalised(Y)
            image_means()
            ask("pe", v.tensor_scalar(SQ[0:C, 1, 0:B], ps[6][0:C, 0:B], 1.0 / L, None, ALU.mult))
            answer("pe")
            st(v.tensor_scalar(small[0:4, 20:24], ps[7][0:4, 0:B], se1b[:, 0:1], 0.0, ALU.add, ALU.max))
            ask("pe", v.tensor_copy(SQ[0:4, 2:4, :].rearrange("p a c -> p (a c)").rearrange("p (b h) -> p b h", b=B),
                                    bc(small[0:4, 20:24].unsqueeze(2), [4, B, H])))
            answer("pe")
            ask("act", v.tensor_tensor(SQ[:, 4, :], ps[6][:, 0:C], se2b[:], ALU.add))
            answer("act")
            st(v.tensor_tensor(Y[:], Y[:], bc(SQ[:, 4:5, :], [P, NT, C]), ALU.mult))
            st(v.tensor_tensor(X[:], X[:], Y[:], ALU.add))

            layer_norm(X, 1e-5)
            turn_groups(T_L2F, (group_norm, 2), read_logits(16, None, hn))
            v.wait_ge(product_read, 2 + READ0[T_WAV])
            hk = SQ[:].rearrange("p t c -> p (t c)")[:, 0:NT * 16].rearrange("p (t k) -> p t k", t=NT)
            hk4 = hk.rearrange("p t (h k) -> p t h k", h=HEADS)
            sa, da, sw, sv = (av[:, k] for k in range(4))
            for k, dst in ((0, sa), (1, da)):
                st(v.tensor_tensor(hk, hn, bc(att[:, k:k + 1, :], [P, NT, 16]), ALU.mult))
                st(v.tensor_reduce(dst, hk4, AX.X, ALU.add))
            ask("pool", v.tensor_reduce(small[:, 24:28], sa.rearrange("p t h -> p h t"), AX.X, ALU.max))
            answer("pool")
            top = bc(small[:, 28:32].unsqueeze(1), [P, NT, HEADS])
            sp_, sq_, sh_ = stab[:, :, 0:4], stab[:, :, 4:8], stab[:, :, 8:SRCW]
            du_, dv_ = dtab[:, :, 0:4], dtab[:, :, 4:8]
            st(v.tensor_tensor(sp_, sa, top, ALU.subtract))
            st(v.tensor_scalar(sq_, sp_, 0.2, None, ALU.mult))
            st(v.tensor_tensor(da, da, top, ALU.add))
            st(v.scalar_tensor_tensor(sw, da, 0.2, da, ALU.mult, ALU.max))
            st(v.tensor_tensor(du_, da, sw, ALU.subtract))
            ask("act", v.scalar_tensor_tensor(dv_, da, 0.2, sw, ALU.mult, ALU.subtract))
            st(v.tensor_copy(sh_, hn))
            answer("act")
            v.sem_inc(tables_out, 1)
            st(v.tensor_tensor(sw, sp_, du_, ALU.mult))
            st(v.tensor_tensor(sv, sq_, dv_, ALU.mult))
            st(v.tensor_tensor(aggr[:, :, 16:MSG], sw, sv, ALU.max))
            ask("pe", v.drain())
            answer("pe")
            last = av[:, 1].rearrange("p t h -> p (t h)")[:, 0:SRCW].unsqueeze(1)
            st(v.tensor_copy(last, ps[4][:, 0:SRCW].unsqueeze(1)))
            a4 = aggr[:, :, 0:16].rearrange("p t (h k) -> p t h k", h=HEADS)
            for h in range(HEADS):
                ins = v.tensor_tensor(a4[:, :, h, :], hn[:, :, h * HK:(h + 1) * HK],
                                      bc(aggr[:, :, 16 + h:17 + h], [P, NT, HK]), ALU.mult)
                if h < HEADS - 1:
                    st(ins)
                else:
                    ask("pe", ins)
            answer("pe")

            def cut_nodes(kb, t, to, sc):
                sc(v.tensor_scalar(t, kb, -1.0, 0.0, ALU.add, ALU.max))
                sc(v.tensor_scalar(to[:, 0], t, NODES - 1, None, ALU.bitwise_and))
                return v.tensor_scalar(to[:, 1], t, 12, None, ALU.logical_shift_right)

            def cut_places(kb, t, part, to, sc):
                sc(v.tensor_scalar(t, kb, -1.0, 0.0, ALU.add, ALU.max))
                sc(v.tensor_scalar(part, t, 12, W - 1, ALU.logical_shift_right, ALU.bitwise_and))
                sc(v.tensor_copy(to[:, 1], part))
                sc(v.tensor_scalar(part, t, 17, None, ALU.logical_shift_right))
                sc(v.tensor_scalar(to[:, 0], kb, 0.5, 1000.0, ALU.is_lt, ALU.mult))
                return v.tensor_tensor(to[:, 0], to[:, 0], part, ALU.subtract)

            def count_far(i, n):
                v.wait_ge(far_counted, i + (n + 1))
                for k, part in enumerate((farhi, farlo)):
                    v.tensor_tensor(farhot[:, n % 2, k], iotaQ[:],
                                    bc(part[:, bass.ds(i * FARB + n * FARB, FARB)].unsqueeze(1), [P, FQ, FARB]),
                                    ALU.is_equal).then_inc(far_made, 1)

            table_keys = keys[:, 0:TABLE]
            st(cut_nodes(table_keys, spare[:, 0], nodes, st))
            for half in range(2):
                v.tensor_copy(ei[:, half], nodes[:, :, half * BLK:(half + 1) * BLK]).then_inc(idx_ready, 1)
            st(cut_places(table_keys, spare[:, 0], spare[:, 1], places, st))
            for n in range(FAR_FIRST):
                count_far(0, n)

            def add_block(b, pair, half, phase):
                es = Steps(v, edge_step)
                es.i, es.per = b, 2
                gs, gd, m, kb = gsrc[:, half], gdst[:, half], em[:, half], keys[:, bass.ds(b * BLK, BLK)]
                v.wait_ge(hot_made, b + 1)
                if phase < 2:
                    v.tensor_copy(ef[:, half], places[:, :, bass.ds(b * BLK, BLK)]).then_inc(places_cut, 1)
                else:
                    rs = Steps(v, rest_step)
                    rs.i, rs.per = b - SHORT_BLOCKS, 7
                    cut_places(kb, epart[:, 0], epart[:, 1], ef[:, half], rs).then_inc(places_cut, 1)
                v.wait_ge(src_in[half], pair * (16 * BLK) + 16 * BLK)
                v.wait_ge(dst_in[half], pair * (16 * BLK) + 16 * BLK)
                if phase < 2:
                    v.tensor_copy(ei[:, half], nodes[:, :, bass.ds((b + 2) * BLK, BLK)]).then_inc(idx_ready, 1)
                else:
                    cut_nodes(keys[:, bass.ds((b + 2) * BLK, BLK)], epart[:, 0], ei[:, half], rs).then_inc(idx_ready, 1)
                es(v.tensor_tensor(ew, gs[:, :, 0:8], gd, ALU.mult))
                es(v.tensor_tensor(m[:, :, 16:MSG], ew[:, :, 0:4], ew[:, :, 4:8], ALU.max))
                v.tensor_tensor(m[:, :, 0:16].rearrange("p c (h k) -> p c h k", h=HEADS),
                                gs[:, :, 8:SRCW].rearrange("p c (h k) -> p c h k", h=HEADS),
                                bc(m[:, :, 16:MSG].unsqueeze(3), [P, BLK, HEADS, HK]), ALU.mult).then_inc(rows_used, 1)
                v.wait_ge(rows_used, b + 3)
                v.wait_ge(places_cut, b + 1)
                v.wait_ge(block_added, b + 1)
                for c in range(BLK):
                    v.scalar_tensor_tensor(spread[:, half, c], bc(iotaW[:].unsqueeze(2), [P, W, MSG]),
                                           ef[:, half, 1, c:c + 1], bc(m[:, c:c + 1, :], [P, W, MSG]),
                                           ALU.is_equal, ALU.mult).then_inc(spread_made, 1)
                    if phase == 0 and c < FAR_PER_BLOCK:
                        count_far(b * FAR_PER_BLOCK, FAR_FIRST + c)
                v.wait_ge(spread_made, (b + 1) * BLK)
                settle(v, carried)

            total = v.value_load(plan[0:1, 0:1], min_val=0, max_val=NBLK)
            run_blocks(v, total, add_block)
            ask("pe", v.drain())
            answer("pe")
            for k in range(2):
                st(v.tensor_copy(aggr[:, k * 16:(k + 1) * 16, :].rearrange("p t k -> p (t k)"), ps[6 + k][:, 0:16 * MSG]))
            st(v.tensor_copy(farcnt, ps[5][0:FQ, 0:FQ]))
            ask("pe", v.drain())
            answer("pe")
            st(v.tensor_copy(fardst[:], ps[4][:, 0:NT]))
            farw = av[:, 0]
            st(v.tensor_tensor(sw, du_, bc(last[:, :, 0:4], [P, NT, HEADS]), ALU.mult))
            st(v.tensor_tensor(sv, dv_, bc(last[:, :, 4:8], [P, NT, HEADS]), ALU.mult))
            st(v.tensor_tensor(farw, sw, sv, ALU.max))
            st(v.tensor_tensor(farw, farw, bc(fardst[:].unsqueeze(2), [P, NT, HEADS]), ALU.mult))
            for h in range(HEADS):
                st(v.tensor_tensor(hk4[:, :, h, :], bc(last[:, :, 8 + h * HK:8 + (h + 1) * HK], [P, NT, HK]),
                                   bc(farw[:, :, h:h + 1], [P, NT, HK]), ALU.mult))
            st(v.tensor_tensor(aggr[:, :, 0:16], aggr[:, :, 0:16], hk, ALU.add))
            st(v.tensor_tensor(aggr[:, :, 16:MSG], aggr[:, :, 16:MSG], farw, ALU.add))
            den = av[:, 0]
            st(v.tensor_scalar(den, aggr[:, :, 16:MSG], 1e-16, None, ALU.add))
            st(v.reciprocal(den, den))
            for h in range(HEADS):
                st(v.tensor_tensor(hk4[:, :, h, :], aggr[:, :, h * HK:(h + 1) * HK], bc(den[:, :, h:h + 1], [P, NT, HK]), ALU.mult))
            v.sem_inc(edges_left, 1)
            vec = lambda k: bc(gatv[:, k:k + 1, :], [P, NT, 16])
            st(v.tensor_tensor(hk, hk, vec(0), ALU.add))
            st(v.tensor_reduce(lnsum[:], hk, AX.X, ALU.add))
            st(v.tensor_scalar(lnneg[:], lnsum[:], -1.0 / 16, None, ALU.mult))
            st(v.tensor_tensor(hk, hk, bc(lnneg[:].unsqueeze(2), [P, NT, 16]), ALU.add))
            sq16 = SQ[:].rearrange("p t c -> p (t c)")[:, NT * 16:NT * 32].rearrange("p (t k) -> p t k", t=NT)
            st(v.tensor_tensor(sq16, hk, hk, ALU.mult))
            st(v.tensor_reduce(lnvar[:], sq16, AX.X, ALU.add))
            ask("act", v.tensor_scalar(lnvar[:], lnvar[:], 1.0 / 16, 1e-5, ALU.mult, ALU.add))
            answer("act")
            st(v.reciprocal(rstd[:], lnsd[:]))
            st(v.tensor_tensor(hk, hk, bc(rstd[:].unsqueeze(2), [P, NT, 16]), ALU.mult))
            st(v.tensor_tensor(hk, hk, vec(1), ALU.mult))
            st(v.tensor_tensor(hk, hk, vec(2), ALU.add))
            st(v.tensor_reduce(logit[:, :, 0:4], hk.rearrange("p t (h k) -> p t k h", h=HEADS), AX.X, ALU.add))
            st(v.tensor_scalar(logit[:, :, 0:4], logit[:, :, 0:4], 1.0 / HEADS, None, ALU.mult))
            st(v.memset(gate[:], 0.0))
            top2_gates(NT, 4)
            experts(2, X)

            v.sem_inc(masks_in, 1)
            layer_norm(X, 1e-6)
            normalised(Y)
            v.wait_ge(masks_in, 49)
            st(v.tensor_copy(hb[:, 1, 1:FT:2], hb[:, 0, 1:FT:2]))
            st(v.tensor_scalar(hb[:, 1, 0:FT:2], hb[:, 0, 0:FT:2], -1.0, None, ALU.mult))
            for mat, mask in ((rc, maskC), (rh, maskH)):
                st(v.tensor_scalar(mat[:], mask[:, 0], hb[:, 0, 0:1], None, ALU.mult))
                for k in range(1, FT):
                    ins = v.scalar_tensor_tensor(mat[:], mask[:, k], hb[:, 0, k:k + 1], mat[:], ALU.mult, ALU.add)
                    if k == FT - 1 and mat is rh:
                        ask("pe", ins)
                    else:
                        st(ins)
            st(v.tensor_scalar(rc[:], rc[:], W_SCALE, None, ALU.mult))
            st(v.tensor_copy(rcp[:, 0], rc[:]))
            st(v.tensor_tensor(rcp[:, 1], rc[:], rcp[:, 0], ALU.subtract))
            answer("pe")
            ask("act", v.drain())
            answer("act")
            for par in range(2):
                rows_out = ACC[:].rearrange("p (m two) c -> p m two c", two=2)[:, :, par]
                first = True
                for k in range(1 - par, FT, 2):
                    off = ((par + k - 1) // 2 - (FT // 2 - 1)) % (W // 2)
                    for wide, filt in ((0, hb[:, 0, FT - 1 - k:FT - k]), (1, hb[:, 1, k:k + 1])):
                        for m0, m1, s0 in ((0, W // 2 - off, off), (W // 2 - off, W // 2, 0)):
                            if m0 == m1:
                                continue
                            srcs = XC[:, wide * (W // 2) + s0:wide * (W // 2) + s0 + m1 - m0, :]
                            o = rows_out[:, m0:m1, :]
                            if first:
                                st(v.tensor_scalar(o, srcs, filt, None, ALU.mult))
                            else:
                                st(v.scalar_tensor_tensor(o, srcs, filt, o, ALU.mult, ALU.add))
                        first = False

            def copy_group(g, half):
                st(v.tensor_scalar(ygf[:, half], ACC[:, bass.ds(g * GT, GT), :], X_SCALE, None, ALU.mult))
                cut_group(half)

            def add_group(g, half):
                xg = X[:, bass.ds(g * GT, GT), :]
                v.scalar_tensor_tensor(xg, ps[2 + half][:, 0:GT * C].rearrange("p (t c) -> p t c", t=GT), UNSCALE, xg,
                                       ALU.mult, ALU.add).then_inc(product_read, 1)
            turn_groups(T_WAV, (copy_group, 2), add_group)
            v.wait_ge(product_read, 2 + READ0[T_L3F])

            layer_norm(X, 1e-5)
            turn_groups(T_L3F, (group_norm, 2), read_logits(8, None, logit))
            v.wait_ge(product_read, 2 + READ0[T_L3F] + NG)
            top2_gates(NT, 8, 1e-9)
            experts3()
            v.drain().then_inc(stored, 1)

        @block.scalar
        def _(s):
            done = [0]

            def asked():
                done[0] += 1
                s.wait_ge(ask_act, done[0])

            def layer_norm():
                asked()
                s.activation(SQ[:], XC[:], ACT.Square).then_inc(act_done, 1)
                asked()
                s.activation(lnsd[:], lnvar[:], ACT.Sqrt).then_inc(act_done, 1)

            def exp_gates(n_tiles, E):
                asked()
                s.activation(gex[:, 0:n_tiles, 0:E], gex[:, 0:n_tiles, 0:E], ACT.Exp).then_inc(act_done, 1)

            def turn_groups(stage, after=None):
                with s.Fori(0, NG // TURNS) as it:
                    for k in range(TURNS + 1):
                        if k < TURNS:
                            s.wait_ge(group_turned, it * TURNS + (k + NG * stage + 3))
                            s.activation(yT[:, bass.ds((it * TURNS + k) * GN, GN)], ps[k % 2][:, 0:GN // 2].bitcast(F16),
                                         ACT.Copy).then_inc(turned_copied, 1)
                        if after and k:
                            after(it * TURNS + (k - 1), (k - 1) % 2)

            def experts(m):
                E, KH, FC = MOES[m]
                with s.Fori(0, NG) as g:
                    for e in range(E):
                        for f in range(FC):
                            k = e * FC + f
                            n = g * (E * FC) + (k + CHUNK0[m])
                            s.wait_ge(hid_full, n + 3)
                            if f == 0:
                                s.wait_ge(down_done, g * E + (e + UNIT0[m] + 1))
                            s.activation(hS[0:KH, (e % 2) * FC + f, :], ps[k % 2][0:KH, :], ACT.Gelu,
                                         bias=ub[m][0:KH, k:k + 1], scale=UNSCALE).then_inc(hid_act, 1)
                        if e == 0:
                            s.wait_ge(gate_turned, g + NG * m + 2)
                            s.wait_ge(bias_done, g + NG * m + 1)
                            s.activation(gTs[:], ps[6][0:GT * 8, 0:P], ACT.Copy).then_inc(gate_copied, 1)

            def experts3():
                E, KH, FC = L3F

                def high(g, k):
                    e = k // FC
                    s.wait_ge(hid_made, g * (E * FC) + (k + 3))
                    if k % FC == 0:
                        s.wait_ge(down_done, g * E + (e + UNIT0[3] + 1))
                    s.activation(hidp[:, k % (2 * FC), 0], hid[:, k % 2], ACT.Copy).then_inc(high_done, 1)

                def keep(g, e):
                    s.wait_ge(down_done, g * E + (e + UNIT0[3] + 3))
                    s.wait_ge(out_turned, g * E + (e + 1))
                    s.activation(outs[:, e % 2], ps[4 + e % 2][:, :], ACT.Copy).then_inc(out_kept, 1)

                def gated(g, k):
                    n = g * (E * FC) + k
                    s.wait_ge(hid_full, n + (CHUNK0[3] + 3))
                    s.wait_ge(hid_made, n + 1)
                    s.activation(sil[:, k % 2], ps[k % 2][:, :], ACT.Silu, scale=UNSCALE).then_inc(sil_done, 1)

                def rest_of_group(g, last):
                    for k in range(LAG, E * FC):
                        gated(g, k)
                        high(g, k - 1)
                        if k >= KEEP_AT and (k - KEEP_AT) % FC == 0:
                            keep(g, (k - KEEP_AT) // FC)
                    if last:
                        high(g, E * FC - 1)
                    else:
                        for k in range(LAG):
                            gated(g + 1, k)
                            high(*((g + 1, k - 1) if k else (g, E * FC - 1)))
                    keep(g, E - 1)

                for k in range(LAG):
                    gated(0, k)
                    if k:
                        high(0, k - 1)
                with s.Fori(0, NG - 1) as g:
                    rest_of_group(g, False)
                rest_of_group(NG - 1, True)

            layer_norm()
            s.wait_ge(w0_in, 80)

            def copy_xz(g, half):
                s.wait_ge(turned_used, g + 3)
                s.activation(xbuf[:, bass.ds(g * GN + (TAPS - 1) * P, GN)], ps[4 + half][:, :], ACT.Copy, scale=UNSCALE).then_inc(xz_copied, 1)
                s.activation(zs[:, bass.ds(g * GN, GN)], ps[6 + half][:, :], ACT.Silu, scale=UNSCALE).then_inc(xz_copied, 1)
            turn_groups(T_L0C, copy_xz)
            with s.Fori(0, NG // 2) as it:
                for half in range(2):
                    g = it * 2 + half
                    s.wait_ge(conv_made, g + 1)
                    s.wait_ge(conv_gated, g + 1)
                    s.activation(csu[:, half], cu[:, half], ACT.Silu, bias=c0b[:, 0:1]).then_inc(conv_silu, 1)
            layer_norm()
            s.wait_ge(w_in, W_LOADS * 16)
            turn_groups(T_L0F)
            exp_gates(NT, 8)
            experts(0)
            layer_norm()
            with s.Fori(0, NG // 2) as it:
                for half in range(2):
                    g = it * 2 + half
                    s.wait_ge(q_turned, g + 3)
                    for k, o0, i0 in ((0, 1, 0), (1, 0, 1)):
                        ins = s.activation(
                            qpad[0:C, k, bass.ds(g * GT + 1, GT), :].rearrange("p x (b h) -> p x b h", b=B)[:, :, :, o0:o0 + H - 1],
                            ps[half][0:C, 0:GT * C].bitcast(BF16).rearrange("p (t b h) -> p t b h", t=GT, b=B)[:, :, :, i0:i0 + H - 1],
                            ACT.Copy)
                    ins.then_inc(q_low, 1)
            layer_norm()
            turn_groups(T_L1F)
            exp_gates(1, 8)
            exp_gates(1, 8)
            exp_gates(1, 8)
            experts(1)
            layer_norm()
            layer_norm()
            asked()
            s.activation(SQ[:, 4, :], SQ[:, 4, :], ACT.Sigmoid).then_inc(act_done, 1)
            layer_norm()
            turn_groups(T_L2F)
            asked()
            s.activation(dtab, dtab, ACT.Exp).then_inc(act_step, 1)
            s.activation(stab[:, :, 0:8], stab[:, :, 0:8], ACT.Exp).then_inc(act_done, 1)
            def make_hots(b, pair, half, phase):
                s.wait_ge(places_cut, b + 1)
                s.wait_ge(block_added, b + 1)
                settle(s, carried)
                for c in range(BLK):
                    s.activation(offset[:, c], iotaP[:], ACT.Square, bias=ef[:, half, 0, c:c + 1]).then_inc(offset_made, 1)
                s.wait_ge(offset_made, b * BLK + BLK)
                s.activation(onehot[:, half], offset, ACT.Relu, bias=ones[:, 0:1], scale=-1.0).then_inc(hot_made, 1)
                s.wait_ge(hot_made, b + 3)
                settle(s, carried)

            total = s.value_load(plan[0:1, 0:1], min_val=0, max_val=NBLK)
            run_blocks(s, total, make_hots)
            asked()
            s.activation(lnsd[:], lnvar[:], ACT.Sqrt).then_inc(act_done, 1)
            exp_gates(NT, 4)
            experts(2)
            layer_norm()
            asked()
            for k in range(4):
                ins = s.activation(XC[:].rearrange("p t c -> p (t c)")[:, k * 512:(k + 1) * 512], ps[k][:, :], ACT.Copy)
            ins.then_inc(act_done, 1)
            turn_groups(T_WAV)
            layer_norm()
            turn_groups(T_L3F)
            exp_gates(NT, 8)
            experts3()

        @block.tensor
        def _(t):
            def turn_groups(stage, product):
                with t.Fori(0, NG // TURNS) as it:
                    def turn(k):
                        n = it * TURNS + (k + NG * stage)
                        made = k + NG * stage + 1 + (NG if stage >= T_L1F else 0)
                        t.wait_ge(group_made, it * TURNS + made)
                        t.wait_ge(turned_copied, n + 1)
                        settle(t, carried)
                        for j in range(GT):
                            ins = t.transpose(ps[k % 2][:, j * C:(j + 1) * C].bitcast(F16),
                                              yg[:, k % 2, j].rearrange("p d c -> p (d c)"), identh[:])
                        ins.then_inc(group_turned, 1)

                    turn(0)
                    for k in range(TURNS):
                        if k + 1 < TURNS:
                            turn(k + 1)
                        t.wait_ge(turned_copied, it * TURNS + (k + NG * stage + 3))
                        product(it * TURNS + k, k % 2)

            def logits(w, width, base):
                def product(g, half):
                    t.wait_ge(product_read, g + (base + 1))
                    settle(t, carried)
                    for j in range(GT):
                        for k in range(2):
                            ins = t.matmul(ps[2 + half][:, j * width:(j + 1) * width], yT[:, bass.ds(g * GN + j * P, P)],
                                           w[:, k], start=(k == 0), stop=(k == 1))
                    ins.then_inc(turned_used, 1)
                return product

            def experts3():
                E, KH, FC = L3F
                t.wait_ge(turned_copied, 2 + NG * (T_L3F + 1))
                t.wait_ge(product_read, 2 + READ0[T_L3F] + NG)
                t.wait_ge(piece_cut, PIECES)

                def project_up(g, k):
                    t.wait_ge(hid_made, g * (E * FC) + (k + 1))
                    settle(t, carried)
                    for q in range(2):
                        for part in range(2):
                            at = q * UP3H + k * KH
                            ins = t.matmul(ps[2 * q + k % 2][:, :], up3[:, part, at:at + P], yT[:, bass.ds(g * GN, GN)],
                                           start=(part == 0), stop=(part == 1))
                    ins.then_inc(hid_full, 1)

                def project_down(g, k):
                    e, f = k // FC, k % FC
                    t.wait_ge(low_done[k % 2], g * (E * FC // 2) + (k // 2 + 2))
                    if f == 0:
                        t.wait_ge(out_kept, g * E + (e + 1))
                    for part in range(2):
                        ins = t.matmul(ps[4 + e % 2][:, :], dn3[:, k], hidp[:, k % (2 * FC), part],
                                       start=(f == 0 and part == 0), stop=(f == FC - 1 and part == 1))
                    if f == FC - 1:
                        ins.then_inc(down_done, 1)

                def turn(g, e):
                    t.wait_ge(out_kept, g * E + (e + 3))
                    t.wait_ge(comb_done, g * E + (e + UNIT0[3] + 1))
                    for j in range(GT):
                        ins = t.matmul(ps[6 + e % 2][:, j * C:(j + 1) * C], outs[:, e % 2, j * P:(j + 1) * P], twoid[:],
                                       start=True, stop=True)
                    ins.then_inc(out_turned, 1)

                def rest_of_group(g, last):
                    for k in range(LAG, E * FC):
                        project_up(g, k)
                        project_down(g, k - LAG)
                        if k >= TURN_AT and (k - TURN_AT) % FC == 0:
                            turn(g, (k - TURN_AT) // FC)
                    for k in range(LAG):
                        if not last:
                            project_up(g + 1, k)
                        project_down(g, E * FC - LAG + k)
                    turn(g, E - 1)

                for k in range(LAG):
                    project_up(0, k)
                with t.Fori(0, NG - 1) as g:
                    rest_of_group(g, False)
                rest_of_group(NG - 1, True)

            def experts(m, stage, reads, ups):
                E, KH, FC = MOES[m]
                t.wait_ge(turned_copied, 2 + NG * (stage + 1))
                t.wait_ge(product_read, 2 + reads)
                with t.Fori(0, NG) as g:
                    x = yT[:, bass.ds(g * GN, GN)]

                    def project_up(e):
                        for f in range(FC):
                            k = e * FC + f
                            n = g * (E * FC) + (k + CHUNK0[m])
                            t.wait_ge(hid_act, n + 1)
                            settle(t, carried)
                            for q, w in enumerate(ups):
                                for part in range(2):
                                    ins = t.matmul(ps[2 * q + k % 2][0:KH, :], w[:, part, k * KH:(k + 1) * KH], x,
                                                   start=(part == 0), stop=(part == 1))
                            ins.then_inc(hid_full, 1)

                    def project_down(e):
                        u = g * E + (e + UNIT0[m])
                        t.wait_ge(hid_act, g * (E * FC) + ((e + 1) * FC + CHUNK0[m] + 2))
                        t.wait_ge(comb_done, u + 1)
                        for j in range(GT):
                            for f in range(FC):
                                ins = t.matmul(ps[4 + e % 2][:, j * C:(j + 1) * C],
                                               hS[0:KH, (e % 2) * FC + f, j * P:(j + 1) * P],
                                               dn[m][:, e * FC + f, :], start=(f == 0), stop=(f == FC - 1))
                        ins.then_inc(down_done, 1)

                    def turn_gates():
                        t.wait_ge(gate_staged, g + NG * m + 1)
                        t.wait_ge(gate_copied, g + NG * m + 1)
                        t.transpose(ps[6][0:GT * 8, 0:P], gst[:], ident[:]).then_inc(gate_turned, 1)

                    def bias():
                        t.wait_ge(gate_copied, g + NG * m + 2)
                        t.wait_ge(bias_read, g + NG * m + 1)
                        t.matmul(ps[7][:, 0:GT * C], gTs[:], db[m][:].rearrange("p t c -> p (t c)"), start=True,
                                 stop=True).then_inc(bias_done, 1)

                    for e in range(E):
                        project_up(e)
                        if e == 0:
                            turn_gates()
                        if e == 1:
                            bias()
                        if e:
                            project_down(e - 1)
                    project_down(E - 1)

            asked = [0]

            def ask():
                asked[0] += 1
                t.wait_ge(ask_pe, asked[0])

            t.wait_ge(pool_const, POOL_CONSTS)
            t.wait_ge(w0_in, 80)
            t.wait_ge(weights_cut, 1)

            def project_xz(g, half):
                t.wait_ge(xz_copied, g * 2 + 2)
                for bank in range(2):
                    for part in range(2):
                        ins = t.matmul(ps[4 + 2 * bank + half][:, :], w0in[:, part, bank * DI:(bank + 1) * DI],
                                       yT[:, bass.ds(g * GN, GN)], start=(part == 0), stop=(part == 1))
                ins.then_inc(turned_used, 1)

            turn_groups(T_L0C, project_xz)
            with t.Fori(0, NG // 2) as it:
                for half in range(2):
                    g = it * 2 + half
                    t.wait_ge(conv_gated, g + 3)
                    t.wait_ge(conv_added, g + 1)
                    for j in range(GT):
                        ins = t.matmul(ps[half][:, j * C:(j + 1) * C], cy[:, half, j * P:(j + 1) * P], w0out[:],
                                       start=True, stop=True)
                    ins.then_inc(conv_out, 1)
            t.wait_ge(w_in, W_LOADS * 16)
            t.wait_ge(weights_cut, 2)
            turn_groups(T_L0F, logits(gwp[0], 8, 0))
            experts(0, T_L0F, NG, [up[0]])

            def no_product(g, half):
                t.sem_inc(turned_used, 1)

            ask()
            wt = ps[6][:, 0:3 * C].bitcast(BF16).rearrange("p (k o) -> p k o", k=6)
            for dx in range(3):
                t.transpose(wt[:, 2 * dx], wqb[:, dx * 3 * C:dx * 3 * C + 2 * C], identb[0:C, 0:C])
                ins = t.transpose(wt[0:C, 2 * dx + 1], wqb[:, dx * 3 * C + 2 * C:(dx + 1) * 3 * C], identb[0:C, 0:C])
            ins.then_inc(pe_done, 1)
            ask()
            t.matmul(ps[7][:, 0:C], SQ[0:C, 0:2, :].rearrange("p a c -> p (a c)"), ident[0:C, 0:C], start=True, stop=True).then_inc(pe_done, 1)
            ask()
            t.transpose(ps[6][0:1, 0:P], small[:, 11:12], ident[:]).then_inc(pe_done, 1)
            ask()
            t.matmul(ps[7][:, 0:1], SQ[0:1, 0:2, :].rearrange("p a c -> p (a c)"), ones[0:1, 0:1], start=True, stop=True).then_inc(pe_done, 1)
            with t.Fori(0, NG // 2) as it:
                for half in range(2):
                    g = it * 2 + half
                    t.wait_ge(group_made, g + (2 * NG + 1))
                    t.wait_ge(q_low, g + 1)
                    t.wait_ge(q_high, g + 1)
                    for j in range(GT):
                        ins = t.transpose(ps[half][:, j * C:(j + 1) * C].bitcast(BF16),
                                          qg[:, half, j].rearrange("p d c -> p (d c)"), identb[:])
                    ins.then_inc(q_turned, 1)
            t.wait_ge(q_low, 2 + NG)
            t.wait_ge(q_high, 2 + NG)
            with t.Fori(0, NG // 2) as it:
                for half in range(2):
                    g = it * 2 + half
                    t.wait_ge(taps_read, g + 1)
                    for j in range(GT):
                        for k in range(6):
                            ins = t.matmul(ps[4 + half][:, j * C:(j + 1) * C],
                                           qpad[:, k % 2, bass.ds(g * GT + (j + k // 2), 1), :].rearrange("p x n -> p (x n)"),
                                           rhsq[:, k, :], start=(k == 0), stop=(k == 5))
                    ins.then_inc(taps_done, 1)
            turn_groups(T_L1F, no_product)
            ask()
            t.matmul(ps[6][0:C, 0:B], SQ[:, 0, :], blk32[:], start=True, stop=True).then_inc(pe_done, 1)
            ask()
            t.matmul(ps[7][:, 0:8], SQ[0:C, 1:3, :].rearrange("p a c -> p (a c)"), gw1[:], start=True, stop=True).then_inc(pe_done, 1)
            ask()
            t.matmul(ps[6][:, 0:8], ones[:], SQ[:, 3, 0:8], start=True, stop=True).then_inc(pe_done, 1)
            experts(1, T_L1F, READ0[T_L2F], [up[1]])
            ask()
            t.matmul(ps[6][0:C, 0:B], SQ[:, 0, :], blk32[:], start=True, stop=True).then_inc(pe_done, 1)
            ask()
            t.matmul(ps[7][0:4, 0:B], se1[:], SQ[0:C, 1, 0:B], start=True, stop=True).then_inc(pe_done, 1)
            ask()
            t.matmul(ps[6][:, 0:C], SQ[0:4, 2:4, :].rearrange("p a c -> p (a c)"), se2[:], start=True, stop=True).then_inc(pe_done, 1)
            turn_groups(T_L2F, logits(gwp[2], 16, READ0[T_L2F]))
            ask()
            t.matmul(ps[4][:, 0:SRCW], lastsel[:], stab[:, NT - 1, :], start=True, stop=True).then_inc(pe_done, 1)
            ask()
            flat = aggr.rearrange("p t k -> p (t k)")
            for k in range(2):
                ins = t.matmul(ps[6 + k][:, 0:16 * MSG], ident[:], flat[:, k * 16 * MSG:(k + 1) * 16 * MSG],
                               start=True, stop=False, skip_group_check=True)
            ins.then_inc(pe_done, 1)
            def count_far(i, n):
                t.wait_ge(far_made, i * 2 + 2 * (n + 1))
                settle(t, carried)
                for c in range(FARB):
                    ins = t.matmul(ps[5][0:FQ, 0:FQ], farhot[:, n % 2, 0, :, c], farhot[:, n % 2, 1, :, c],
                                   start=False, stop=False, skip_group_check=True)
                ins.then_inc(far_counted, 1)

            def add_block(b, pair, half, phase):
                t.wait_ge(hot_made, b + 3)
                for c in range(BLK):
                    t.wait_ge(spread_made, b * BLK + (c + 1))
                    for k in range(2):
                        ins = t.matmul(ps[6 + k][:, 0:16 * MSG], onehot[:, half, c],
                                       spread[:, half, c, k * 16:(k + 1) * 16, :].rearrange("p w m -> p (w m)"),
                                       start=False, stop=False, skip_group_check=True)
                    if c == BLK - 1:
                        ins.then_inc(block_added, 1)
                    if phase == 0 and c < FAR_PER_BLOCK:
                        count_far(b * FAR_PER_BLOCK, FAR_FIRST + c)

            t.matmul(ps[5][0:FQ, 0:FQ], zerob[:, 0:FQ], zerob[:, 0:FQ], start=True, stop=False, skip_group_check=True)
            for n in range(FAR_FIRST):
                count_far(0, n)
            total = t.value_load(plan[0:1, 0:1], min_val=0, max_val=NBLK)
            run_blocks(t, total, add_block)
            ask()
            t.drain().then_inc(pe_done, 1)
            ask()
            for k in range(2):
                ins = t.matmul(ps[4][:, 0:NT], halfsel[:, k], farcnt[:, k * NT:(k + 1) * NT], start=(k == 0), stop=(k == 1))
            ins.then_inc(pe_done, 1)
            assert asked[0] == PE_EDGES
            experts(2, T_L2F, READ0[T_WAV], [up[2]])
            ask()
            for k in range(4):
                ins = t.matmul(ps[k][:, :], rh[:], Y[:].rearrange("p t c -> p (t c)")[:, k * 512:(k + 1) * 512],
                               start=True, stop=True)
            ins.then_inc(pe_done, 1)
            turn_groups(T_WAV, logits(rcp, C, READ0[T_WAV]))
            turn_groups(T_L3F, logits(gwp[3], 8, READ0[T_L3F]))
            experts3()

        @block.gpsimd
        def _(q):
            for m in range(3):
                q.memset(db[m][:], 0.0)
            q.engine_nop().then_inc(pool_const, 1)
            cst = [1]

            def const(ins):
                ins.then_inc(pool_const, 1)
                cst[0] += 1
                q.wait_ge(pool_const, cst[0])
            const(q.memset(ident[:], 0.0))
            const(q.memset(ones[:], 1.0))
            const(q.affine_select(out=ident[:], in_=ident[:], compare_op=ALU.not_equal, fill=1.0, base=0,
                                  pattern=[[-1, P]], channel_multiplier=1))
            const(q.tensor_copy(identb[:], ident[:]))
            const(q.tensor_copy(identh[:], ident[:]))
            const(q.affine_select(out=twoid[:], in_=ident[:, 0:C], compare_op=ALU.not_equal, fill=1.0, base=-C,
                                  pattern=[[-1, C]], channel_multiplier=1))
            const(q.affine_select(out=blk32[:], in_=ones[:, 0:B], compare_op=ALU.is_ge, fill=0.0, base=0,
                                  pattern=[[-H, B]], channel_multiplier=1))
            const(q.affine_select(out=blk32[:], in_=blk32[:], compare_op=ALU.is_ge, fill=0.0, base=H - 1,
                                  pattern=[[H, B]], channel_multiplier=-1))
            const(q.iota(iotaP[:], [[1, P]], base=0, channel_multiplier=0, allow_small_or_imprecise_dtypes=True))
            const(q.iota(iotaQ[:], [[1, FQ], [0, FARB]], base=0, channel_multiplier=0, allow_small_or_imprecise_dtypes=True))
            const(q.memset(halfsel[:], 0.0))
            for k in range(2):
                const(q.affine_select(out=halfsel[:, k], in_=halfsel[:, k], compare_op=ALU.not_equal, fill=1.0, base=k,
                                      pattern=[[-1, P]], channel_multiplier=2))
            const(q.affine_select(out=lastsel[:], in_=ones[:], compare_op=ALU.is_ge, fill=0.0, base=1 - P,
                                  pattern=[[0, P]], channel_multiplier=1))
            const(q.memset(zerob[:], 0.0))
            const(q.iota(iotaW[:], [[1, W]], base=0, channel_multiplier=0, allow_small_or_imprecise_dtypes=True))
            assert cst[0] == POOL_CONSTS

            cuts = [0]

            def cut(parts, whole):
                for ins in (lambda: q.tensor_scalar(whole, whole, W_SCALE, None, ALU.mult),
                            lambda: q.tensor_copy(parts[:, 0], whole),
                            lambda: q.tensor_tensor(parts[:, 1], whole, parts[:, 0], ALU.subtract)):
                    ins().then_inc(pool_step, 1)
                    cuts[0] += 1
                    q.wait_ge(pool_step, cuts[0])

            q.wait_ge(w0_in, 80)
            cut(w0in, stage_w0)
            q.sem_inc(weights_cut, 1)
            q.wait_ge(ask_pool, 1)
            q.partition_all_reduce(counts[:, 1], counts[:, 0], P, RMAX).then_inc(pool_done, 1)
            q.wait_ge(w_in, W_LOADS * 16)
            for m in (0, 2, 3):
                cut(gwp[m], stage_gw[m])
            for m in range(3):
                cut(up[m], stage_up[m])
            q.sem_inc(weights_cut, 1)

            q.wait_ge(ask_pool, 2)
            q.partition_all_reduce(small[:, 28:32], small[:, 24:28], P, RMAX).then_inc(pool_done, 1)
            q.wait_ge(tables_out, 33)

            def gather_block(b, pair, half, phase):
                q.wait_ge(idx_ready, b + 1)
                q.wait_ge(rows_used, b + 1)
                settle(q, carried)
                for c in range(BLK):
                    q.indirect_dma_start(gsrc[:, half, c], None, src_rows,
                                         bass.IndirectOffsetOnAxis(ap=ei[:, half, 0, c:c + 1].bitcast(U32), axis=0)).then_inc(src_in[half], 16)
                    q.indirect_dma_start(gdst[:, half, c], None, dst_rows,
                                         bass.IndirectOffsetOnAxis(ap=ei[:, half, 1, c:c + 1].bitcast(U32), axis=0)).then_inc(dst_in[half], 16)

            total = q.value_load(plan[0:1, 0:1], min_val=0, max_val=NBLK)
            run_blocks(q, total, gather_block)
            for n in range(PIECES):
                q.wait_ge(piece_in[n % 2], 32 * (n // 2 + 1))
                if n < UP_PIECES:
                    cut(up3[:, :, n * PIECE:(n + 1) * PIECE], piece[:, n % 2])
                else:
                    k = n - UP_PIECES
                    per = DN_PIECE // C
                    cut(dn3[:, k * per:(k + 1) * per].rearrange("p a (k c) -> p k a c", k=2),
                        piece[:, n % 2, 0:DN_PIECE].rearrange("p (a c) -> p a c", c=C))
                q.sem_inc(piece_cut, 1)
            E, KH, FC = L3F
            with q.Fori(0, NG) as g:
                for k in range(1, E * FC, 2):
                    slot = hidp[:, k % (2 * FC)]
                    q.wait_ge(high_done, g * (E * FC) + (k + 3))
                    q.tensor_tensor(slot[:, 1], hid[:, k % 2], slot[:, 0], ALU.subtract).then_inc(low_done[1], 1)


def kernel(**inputs):
    import numpy as np
    import concourse.bacc as bacc
    from concourse.bass_utils import run_bass_kernel_spmd as run

    nc = bacc.Bacc("TRN2", target_bir_lowering=False, num_devices=1)
    arrays, aps = {}, {}

    def give(name, v):
        v = np.ascontiguousarray(v)
        arrays[f"in_{name}"] = v
        aps[name] = nc.dram_tensor(f"in_{name}", v.shape, mybir.dt.from_np(v.dtype), kind="ExternalInput").ap()

    i = {k: np.asarray(v) for k, v in inputs.items()}
    give("x", i["x"].reshape(P, NT, C))
    give("src", i["L2_ffn_edge_index"][0].reshape(P, EPP))
    give("dst", i["L2_ffn_edge_index"][1].reshape(P, EPP))
    give("w0in", i["L0_conv_W_in"].T)
    give("w0out", i["L0_conv_W_out"].T)
    give("c0w", i["L0_conv_conv_w"].reshape(DI, TAPS))
    give("c0b", i["L0_conv_conv_b"].reshape(DI, 1))

    def ups(w, k, f):
        e, c, h = w.shape
        r = np.zeros((c, e, k * f), w.dtype)
        r[:, :, 0:h] = w.transpose(1, 0, 2)
        return r.reshape(c, e * k * f)

    def downs(w, k, f):
        e, h, c = w.shape
        r = np.zeros((e, k * f, c), w.dtype)
        r[:, 0:h, :] = w
        return r.reshape(e * f, k, c).transpose(1, 0, 2)

    for m in range(3):
        e, k, f = MOES[m]
        give(f"up{m}", ups(i[f"L{m}_ffn_W1"], k, f))
        give(f"ub{m}", i[f"L{m}_ffn_b1"].reshape(e * f, k).T)
        give(f"dn{m}", downs(i[f"L{m}_ffn_W2"], k, f))
        give(f"db{m}", i[f"L{m}_ffn_b2"])
    e, k, f = L3F
    up3 = [ups(i[f"L3_ffn_{w}"].transpose(0, 2, 1), k, f) for w in ("w1", "w3")]
    give("up3", np.concatenate(up3 + [np.zeros((C, UP3 - 2 * UP3H), up3[0].dtype)], 1))
    dn3 = downs(i["L3_ffn_w2"].transpose(0, 2, 1), k, f).reshape(k, DN3)
    give("dn3", np.concatenate([dn3, np.zeros((P - k, DN3), dn3.dtype)]))
    give("gw0", i["L0_ffn_Wg"])
    give("gw1", i["L1_ffn_Wr"])
    give("gw2", i["L2_ffn_W_gat"])
    give("gw3", i["L3_ffn_router_w"].T)
    give("gb0", i["L0_ffn_bg"])
    give("gb1", i["L1_ffn_br"])
    give("rhs", i["L1_conv_rhs"].transpose(3, 1, 0, 2).reshape(C, 9 * C))
    give("gam1", i["L1_ffn_gamma"])
    give("bet1", i["L1_ffn_beta"])
    give("se1", i["L2_conv_w1"])
    give("se1b", i["L2_conv_b1"].reshape(4, 1))
    give("se2", i["L2_conv_w2"])
    give("se2b", i["L2_conv_b2"])
    give("att_src", i["L2_ffn_att_src"].reshape(16))
    give("att_dst", i["L2_ffn_att_dst"].reshape(16))
    give("b_gat", i["L2_ffn_b_gat"])
    give("gat_g", i["L2_ffn_ln_gamma"])
    give("gat_b", i["L2_ffn_ln_beta"])
    give("wavelet", i["L3_conv_h"])

    def masks(n, copies):
        half = n // 2
        m = np.zeros((n, FT, n), np.float32)
        for o in range(n):
            for k in range(FT):
                if (o + k) % 2:
                    at = ((o + k - 1) // 2 - (FT // 2 - 1)) % half
                    m[at, FT - 1 - k, o] = 1.0
                    m[half + at, k, o] = 1.0 if k % 2 else -1.0
        r = np.zeros((copies, n, FT, copies, n), np.float32)
        for c in range(copies):
            r[c, :, :, c, :] = m
        return r.reshape(copies * n, FT, copies * n)

    give("maskH", masks(H, B))
    give("maskC", masks(C, 1))
    out = nc.dram_tensor("out_x", (P, NT, C), F32, kind="ExternalOutput").ap()
    build_program(nc, aps, out)
    r = run(nc, [arrays], core_ids=[0])
    return np.asarray(r.results[0]["out_x"]).reshape(B, H, W, C)
```

```python
from contextlib import ExitStack

import concourse.bass as bass
from concourse import mybir

F32 = mybir.dt.float32
BF16 = mybir.dt.bfloat16
F16 = mybir.dt.float16
I32 = mybir.dt.int32
U32 = mybir.dt.uint32
ALU = mybir.AluOpType
ACT = mybir.ActivationFunctionType
AX = mybir.AxisListType
RMAX = bass.bass_isa.ReduceOp.max

P = 128
B, H, W, C = 4, 32, 32, 64
NT = W
GT = 4
NG = NT // GT
HALVES = (slice(0, NT // 2), slice(NT // 2, NT))
L = H * W
GN = GT * P

DI = 2 * C
TAPS = 4
XW = (NT + TAPS - 1) * P

L0F = (8, 128, 2)
L1F = (8, 128, 1)
L2F = (4, 128, 1)
L3F = (8, 114, 6)
MOES = [L0F, L1F, L2F, L3F]
CHUNK0 = [NG * sum(e * f for e, _, f in MOES[:m]) for m in range(5)]
UNIT0 = [NG * sum(e for e, _, _ in MOES[:m]) for m in range(5)]

HEADS, HK = 4, 4
N_EDGES = 262144
NODES = B * H * W
EPP = N_EDGES // P
TOP = 8
SEG = 256
NSEG = EPP // SEG
NEAR_ROUNDS = 5
NEAR_LIST = NSEG * NEAR_ROUNDS * TOP
BLK = TOP
NBLK = EPP // BLK
SHORT_BLOCKS = 24
SURE_BLOCKS = 20
SHORT_ROUNDS = SHORT_BLOCKS // NG
FQ = 64
FARB = 16
FAR_STEPS = EPP // FARB
FAR_PER_BLOCK = 2 * (FAR_STEPS // (2 * SURE_BLOCKS))
FAR_FIRST = FAR_STEPS - SURE_BLOCKS * FAR_PER_BLOCK
TABLE = (SHORT_BLOCKS + 2) * BLK
SRCW = 2 * HEADS + HEADS * HK
DSTW = 2 * HEADS
MSG = HEADS * HK + HEADS
PAD = W + 2
CAPACITY = -(-NODES * 5 // (4 * 8))
QMAX = 127.0
ROUND = 1.5 * 2.0 ** 23
FT = 8
X_SCALE, W_SCALE = 32.0, 64.0
UNSCALE = 1.0 / (X_SCALE * W_SCALE)
UP3H = 8 * 684
UP3 = 2 * UP3H + 36
DN3 = 8 * 6 * C
UP_PIECES, DN_PIECES = 6, 2
PIECE, DN_PIECE = UP3 // UP_PIECES, DN3 // DN_PIECES
PIECES = UP_PIECES + DN_PIECES
LAG = 4
ROT = 9
STAGE_AT = 9
SPREAD_AT, KEEP_AT, COMBINE_AT = 11, 11, 12
G_SCALE = 256.0
H_SCALE = 1.0 / 8
DN_UNSCALE = 1.0 / (H_SCALE * W_SCALE)


class Steps:

    def __init__(self, eng, sem):
        self.eng, self.sem, self.at, self.i, self.per, self.first = eng, sem, 0, None, 0, 0

    def __call__(self, ins):
        ins.then_inc(self.sem, 1)
        self.at += 1
        self.eng.wait_ge(self.sem, self.at if self.i is None else self.i * self.per + self.at)

    def enter(self, i, per):
        self.i, self.per, self.first = i, per, self.at

    def leave(self, times):
        assert self.at - self.first == self.per, (self.at - self.first, self.per)
        self.at = self.first + times * self.per
        self.i = None


def settle(eng, sem):
    eng.sem_inc(sem, 1)


def run_blocks(eng, total, block):
    with eng.Fori(0, SURE_BLOCKS // 2) as pair:
        for half in range(2):
            block(pair * 2 + half, pair, half, 0)
    for b in range(SURE_BLOCKS, SHORT_BLOCKS):
        with eng.If(total > b):
            block(b, b // 2, b % 2, 1)
    with eng.If(total > SHORT_BLOCKS):
        with eng.Fori(SHORT_BLOCKS // 2, NBLK // 2) as pair:
            for half in range(2):
                block(pair * 2 + half, pair, half, 2)


def build_program(nc, a, out):
    ctx = ExitStack()

    def sb(name, shape, dt=F32):
        return ctx.enter_context(nc.sbuf_tensor(name, shape, dt))

    def sem(name):
        return ctx.enter_context(nc.semaphore(name))

    with ctx:
        X = sb("X", [P, NT, C])
        XC = sb("XC", [P, NT, C])
        Y = sb("Y", [P, NT, C])
        SQ = sb("SQ", [P, NT, C])
        ACC = sb("ACC", [P, NT, C])
        yT = sb("yT", [P, NT * P], F16)
        yg = sb("yg", [P, 2, GT, 2, C], F16)
        ygf = sb("ygf", [P, 2, GT, C])
        hS = sb("hS", [P, 12, GN])
        arena = sb("arena", [P, 12288])
        keys = sb("keys", [P, EPP + 2 * BLK])
        sil = sb("sil", [P, 2, GN])
        comb = sb("comb", [P, 2, GT, C])
        ident = sb("ident", [P, P])
        identb = sb("identb", [P, P], BF16)
        identh = sb("identh", [P, P], F16)
        ones = sb("ones", [P, P])
        blk32 = sb("blk32", [P, B])
        iotaP = sb("iotaP", [P, P])
        iotaW = sb("iotaW", [P, W])
        lnsum = sb("lnsum", [P, NT])
        lnneg = sb("lnneg", [P, NT])
        lnvar = sb("lnvar", [P, NT])
        lnsd = sb("lnsd", [P, NT])
        rstd = sb("rstd", [P, NT])
        logit = sb("logit", [P, NT, 16])
        gate = sb("gate", [P, NT, 8])
        gex = sb("gex", [P, NT, 8])
        gsum = sb("gsum", [P, 4, NT])
        gst = sb("gst", [P, GT * 8])
        gTs = sb("gTs", [GT * 8, P])
        small = sb("small", [P, 256])
        w0in = sb("w0in", [P, 2, 2 * DI], F16)
        w0out = sb("w0out", [DI, C])
        c0w = sb("c0w", [DI, TAPS])
        c0b = sb("c0b", [DI, 1])
        gw1 = sb("gw1", [C, 8])
        gwp = {m: sb(f"gwp{m}", [P, 2, n], F16) for m, n in ((0, 8), (2, 16), (3, 8))}
        gb = [sb(f"gb{m}", [P, 16]) for m in range(4)]
        up = [sb(f"up{m}", [P, 2, e * f * k], F16) for m, (e, k, f) in enumerate(MOES[:3])]
        ub = [sb(f"ub{m}", [P, e * f]) for m, (e, k, f) in enumerate(MOES[:3])]
        dn = [sb(f"dn{m}", [k, e * f, C]) for m, (e, k, f) in enumerate(MOES[:3])]
        dn3 = sb("dn3", [P, DN3 // C, 2 * C], F16)
        db = [sb(f"db{m}", [GT * 8, GT, C]) for m in range(3)]
        rhsq = sb("rhsq", [P, 6, C], BF16)
        seg = sb("seg", [P, SEG])
        best = sb("best", [P, NEAR_ROUNDS * TOP])
        srow = sb("srow", [P, C])
        gam1 = sb("gam1", [P, C])
        bet1 = sb("bet1", [P, C])
        se1 = sb("se1", [C, 4])
        se1b = sb("se1b", [4, 1])
        se2 = sb("se2", [4, C])
        se2b = sb("se2b", [P, C])
        att = sb("att", [P, 2, 16])
        gatv = sb("gatv", [P, 3, 16])
        hb = sb("hb", [P, 2, FT])
        rc = sb("rc", [P, C])
        rcp = sb("rcp", [P, 2, C], F16)
        rh = sb("rh", [P, P])
        gatep = sb("gatep", [P, NT, 2, 8], F16)
        gst3 = sb("gst3", [P, GT, 16], F16)
        gT3 = sb("gT3", [16, GN], F16)
        expsel = sb("expsel", [16, 8, P], F16)
        twoid = sb("twoid", [P, C])
        lastsel = sb("lastsel", [P, P])
        halfsel = sb("halfsel", [FQ, 2, P])
        zerob = sb("zerob", [P, P], BF16)
        iotaQ = sb("iotaQ", [P, FQ, FARB], BF16)
        farhi = sb("farhi", [P, EPP], BF16)
        farlo = sb("farlo", [P, EPP], BF16)
        segcnt = sb("segcnt", [P, NSEG])
        counts = sb("counts", [P, 2, 2])
        plan = sb("plan", [P, 4], I32)
        fardst = sb("fardst", [P, NT])

        esrc = ACC[:].rearrange("p t c -> p (t c)").bitcast(I32)
        edst = Y[:].rearrange("p t c -> p (t c)").bitcast(I32)
        isnear = dn3[:].rearrange("p a c -> p (a c)").bitcast(F32)[:, 0:EPP]
        farhot = Y[:].rearrange("p t c -> p (t c)").bitcast(BF16).rearrange("p (s k q c) -> p s k q c", s=2, k=2, q=FQ)
        farcnt = Y[0:FQ].rearrange("p t c -> p (t c)")[:, 0:FQ]
        xbuf = arena[:, 0:XW]
        zs = arena[:, XW:XW + NT * P]
        spread = arena[:, 0:2 * BLK * W * MSG].rearrange("p (s c w m) -> p s c w m", s=2, c=BLK, w=W)
        onehot = arena[:, 10240:10240 + 2 * BLK * P].rearrange("p (s c q) -> p s c q", s=2, c=BLK)
        up3 = arena[:, 0:UP3].bitcast(F16).rearrange("p (k n) -> p k n", k=2)
        nearlist = sil[:].rearrange("p a n -> p (a n)")[:, 512:512 + NEAR_LIST]
        shortlist = sil[:].rearrange("p a n -> p (a n)")[:, 832:832 + SHORT_BLOCKS * BLK]
        outg = farlo[:].bitcast(F32).rearrange("p (s n) -> p s n", s=2)
        gated_out, out_sum = (farhi[:].bitcast(F32)[:, k * GN:(k + 1) * GN] for k in range(2))
        hid = keys[:, 0:4 * GN].rearrange("p (s n) -> p s n", s=4)
        hidp = hS[:].rearrange("p a n -> p (a n)").bitcast(F16).rearrange("p (a k n) -> p a k n", a=12, k=2)
        stage_up, at = [], XW + NT * P
        for e, k, f in MOES[:3]:
            stage_up.append(arena[:, at:at + e * k * f])
            at += e * k * f
        assert at <= 12288
        sil_flat = sil[:].rearrange("p a n -> p (a n)")
        stage_w0 = sil_flat[:, 0:2 * DI]
        stage_gw = {m: sil_flat[:, o:o + n] for m, o, n in ((0, 256, 8), (2, 264, 16), (3, 280, 8))}
        cu = hS[:, 0:2, :]
        csu = hS[:, 2:4, :]
        cy = hS[:, 4:6, :]
        qg = hS[:, 0:1, :].rearrange("p a n -> p (a n)").bitcast(BF16).rearrange("p (s t d c) -> p s t d c", s=2, t=GT, d=2)
        qf = hS[:, 1, :].rearrange("p (s t c) -> p s t c", s=2, t=GT)
        wqf = hS[0:C, 2:4, :].rearrange("p a n -> p (a n)")[:, 0:576]
        wqb = hS[0:C, 9:12, :].rearrange("p a n -> p (a n)")[:, 600:600 + 288].bitcast(BF16)
        qpad = hS[:, 2:11, :].rearrange("p a n -> p (a n)").bitcast(BF16)[:, 0:2 * PAD * P].rearrange(
            "p (k x n) -> p k x n", k=2, x=PAD)
        rq = hS[0:C, 9:12, :].rearrange("p a n -> p (a n)")
        maskH = hS[:, 0:2, :].rearrange("p a n -> p (a n)").rearrange("p (t q) -> p t q", t=FT)
        maskC = hS[:, 2:3, :].rearrange("p a n -> p (a n)").rearrange("p (t q) -> p t q", t=FT)
        piece = hS[:, 3:12, :].rearrange("p a n -> p (a n)")[:, 0:2 * PIECE].rearrange("p (s n) -> p s n", s=2)
        hn = hS[:, 0, :].rearrange("p (t k) -> p t k", t=NT)
        stab = hS[:, 1:3, :].rearrange("p a n -> p (a n)")[:, 0:NT * SRCW].rearrange("p (t k) -> p t k", t=NT)
        dtab = hS[:, 3, 0:NT * DSTW].rearrange("p (t k) -> p t k", t=NT)
        gsrc = hS[:, 4, 0:2 * BLK * SRCW].rearrange("p (s c k) -> p s c k", s=2, c=BLK)
        gdst = hS[:, 5, 0:2 * BLK * DSTW].rearrange("p (s c k) -> p s c k", s=2, c=BLK)
        em = hS[:, 6, 0:2 * BLK * MSG].rearrange("p (s c k) -> p s c k", s=2, c=BLK)
        ei = hS[:, 7, 0:2 * 2 * BLK].bitcast(I32).rearrange("p (s k c) -> p s k c", s=2, k=2)
        epart = hS[:, 7, 128:128 + 2 * BLK].bitcast(I32).rearrange("p (k c) -> p k c", k=2)
        ef = hS[:, 8, 0:2 * 2 * BLK].rearrange("p (s k c) -> p s k c", s=2, k=2)
        ew = hS[:, 8, 64:64 + BLK * 2 * HEADS].rearrange("p (c k) -> p c k", c=BLK)
        offset = XC[:].rearrange("p t c -> p (t c)")[:, 1024:1024 + BLK * P].rearrange("p (c q) -> p c q", c=BLK)
        nodes = XC[:].rearrange("p t c -> p (t c)")[:, 0:2 * TABLE].bitcast(I32).rearrange("p (k c) -> p k c", k=2)
        places = XC[:].rearrange("p t c -> p (t c)")[:, 2 * TABLE:4 * TABLE].rearrange("p (k c) -> p k c", k=2)
        spare = SQ[:].rearrange("p t c -> p (t c)")[:, 0:2 * TABLE].bitcast(I32).rearrange("p (k c) -> p k c", k=2)
        av = hS[:, 11, 0:4 * NT * HEADS].rearrange("p (k t h) -> p k t h", k=4, t=NT)
        aggr = hS[:, 9:11, :].rearrange("p a n -> p (a n)")[:, 0:NT * MSG].rearrange("p (t k) -> p t k", t=NT)

        ps = [ctx.enter_context(nc.psum_tensor(f"ps{n}", [P, 512], F32)) for n in range(8)]
        src_rows = nc.dram_tensor("src_rows", [NODES, SRCW], F32, kind="Internal").ap()
        dst_rows = nc.dram_tensor("dst_rows", [NODES, DSTW], F32, kind="Internal").ap()

        x_in = sem("x_in")
        edges_in = sem("edges_in")
        w0_in = sem("w0_in")
        w_in = sem("w_in")
        masks_in = sem("masks_in")
        piece_in = [sem(f"piece_in{h}") for h in range(2)]
        piece_cut = sem("piece_cut")
        weights_cut = sem("weights_cut")
        edges_left = sem("edges_left")
        tables_out = sem("tables_out")
        stored = sem("stored")
        pool_const = sem("pool_const")
        carried = sem("carried")
        dve_step = sem("dve_step")
        act_step = sem("act_step")
        pool_step = sem("pool_step")
        ask_act, act_done = sem("ask_act"), sem("act_done")
        ask_pe, pe_done = sem("ask_pe"), sem("pe_done")
        ask_pool, pool_done = sem("ask_pool"), sem("pool_done")
        group_made = sem("group_made")
        group_turned = sem("group_turned")
        turned_copied = sem("turned_copied")
        turned_used = sem("turned_used")
        product_read = sem("product_read")
        xz_copied = sem("xz_copied")
        conv_made = sem("conv_made")
        conv_silu = sem("conv_silu")
        conv_gated = sem("conv_gated")
        conv_out = sem("conv_out")
        conv_added = sem("conv_added")
        hid_full = sem("hid_full")
        hid_act = sem("hid_act")
        hid_made = sem("hid_made")
        high_done = sem("high_done")
        low_done = [sem(f"low_done{h}") for h in range(2)]
        out_kept = sem("out_kept")
        gates_spread = sem("gates_spread")
        sum_turned = sem("sum_turned")
        sil_done = sem("sil_done")
        down_done = sem("down_done")
        comb_done = sem("comb_done")
        gate_staged = sem("gate_staged")
        gate_turned = sem("gate_turned")
        gate_copied = sem("gate_copied")
        bias_done = sem("bias_done")
        bias_read = sem("bias_read")
        q_turned = sem("q_turned")
        q_low = sem("q_low")
        q_high = sem("q_high")
        taps_done = sem("taps_done")
        taps_read = sem("taps_read")
        list_kept = sem("list_kept")
        near_made = sem("near_made")
        far_made = sem("far_made")
        far_counted = sem("far_counted")
        idx_ready = sem("idx_ready")
        rows_used = sem("rows_used")
        src_in = [sem(f"src_in{h}") for h in range(2)]
        dst_in = [sem(f"dst_in{h}") for h in range(2)]
        edge_step = sem("edge_step")
        rest_step = sem("rest_step")
        places_cut = sem("places_cut")
        hot_made = sem("hot_made")
        offset_made = sem("offset_made")
        spread_made = sem("spread_made")
        block_added = sem("block_added")

        RING2 = [group_turned, turned_copied, turned_used, product_read, conv_silu,
                 conv_gated, conv_out, conv_added, hid_full, hid_act, hid_made, high_done, out_kept, gates_spread,
                 sil_done, down_done, comb_done,
                 q_turned, q_low, q_high, taps_done, taps_read, block_added, rows_used,
                 far_counted, hot_made] + low_done
        RING1 = [sum_turned, gate_turned, gate_copied, bias_done, bias_read]

        W_LOADS = 46
        POOL_CONSTS = 21
        PE_EDGES = 14

        block = ctx.enter_context(nc.Block())

        T_L0C, T_L0F, T_L1F, T_L2F, T_WAV, T_L3F = range(6)
        READ0 = {T_L0F: 0, T_L2F: NG, T_WAV: 2 * NG, T_L3F: 3 * NG}

        @block.sync
        def _(sp):
            sp.dma_start(X[:], a["x"]).then_inc(x_in, 16)
            for half in range(2):
                sp.dma_start(stage_w0[half * C:(half + 1) * C], a["w0in"]).then_inc(w0_in, 16)
            sp.dma_start(edst, a["dst"]).then_inc(edges_in, 16)
            sp.dma_start(esrc, a["src"]).then_inc(edges_in, 16)
            sp.dma_start(w0out[:], a["w0out"]).then_inc(w0_in, 16)
            sp.dma_start(c0w[:], a["c0w"]).then_inc(w0_in, 16)
            sp.dma_start(c0b[:], a["c0b"]).then_inc(w0_in, 16)
            n_w = [0]

            def load(dst, src):
                n_w[0] += 16
                sp.dma_start(dst, src).then_inc(w_in, 16)

            def rows(v):
                return v.partition_broadcast(P)

            def load_twice(dst, src):
                load(dst[0:C], src)
                load(dst[C:P], src)

            for m, (e, k, f) in enumerate(MOES):
                if m < 3:
                    load_twice(stage_up[m], a[f"up{m}"])
                    load(ub[m][0:k, :], a[f"ub{m}"])
                    load(dn[m][:], a[f"dn{m}"])
                if m == 1:
                    load(gw1[:], a["gw1"])
                else:
                    load_twice(stage_gw[m], a[f"gw{m}"])
            for m in range(2):
                load(gb[m][:, 0:8], rows(a[f"gb{m}"]))
            sp.wait_ge(pool_const, 1)
            for m in range(3):
                e = MOES[m][0]
                for j in range(GT):
                    load(db[m][j * 8:j * 8 + e, j, :], a[f"db{m}"])
            load(rq[:, 0:576], a["rhs"])
            load(gam1[:], rows(a["gam1"]))
            load(bet1[:], rows(a["bet1"]))
            load(se1[:], a["se1"])
            load(se1b[:], a["se1b"])
            load(se2[:], a["se2"])
            load(se2b[:], rows(a["se2b"]))
            load(att[:, 0, :], rows(a["att_src"]))
            load(att[:, 1, :], rows(a["att_dst"]))
            load(gatv[:, 0, :], rows(a["b_gat"]))
            load(gatv[:, 1, :], rows(a["gat_g"]))
            load(gatv[:, 2, :], rows(a["gat_b"]))
            load(hb[:, 0, :], rows(a["wavelet"]))
            assert n_w[0] == W_LOADS * 16, n_w[0] // 16
            sp.wait_ge(tables_out, 1)
            sp.dma_start(src_rows.rearrange("(p t) k -> p (t k)", p=P), stab.rearrange("p t k -> p (t k)")).then_inc(tables_out, 16)
            sp.dma_start(dst_rows.rearrange("(p t) k -> p (t k)", p=P), dtab.rearrange("p t k -> p (t k)")).then_inc(tables_out, 16)
            sp.wait_ge(pe_done, PE_EDGES)
            sp.wait_ge(edges_left, 1)
            for n in range(PIECES):
                if n >= 2:
                    sp.wait_ge(piece_cut, n - 1)
                if n < UP_PIECES:
                    for half in range(2):
                        sp.dma_start(piece[half * C:(half + 1) * C, n % 2], a["up3"][:, n * PIECE:(n + 1) * PIECE]).then_inc(piece_in[n % 2], 16)
                else:
                    k = n - UP_PIECES
                    sp.dma_start(piece[:, n % 2, 0:DN_PIECE], a["dn3"][:, k * DN_PIECE:(k + 1) * DN_PIECE]).then_inc(piece_in[n % 2], 32)
            sp.wait_ge(masks_in, 1)
            sp.dma_start(maskH, a["maskH"]).then_inc(masks_in, 16)
            for half in range(2):
                sp.dma_start(maskC[half * C:(half + 1) * C], a["maskC"]).then_inc(masks_in, 16)
            sp.wait_ge(stored, 1)
            sp.dma_start(out, X[:]).then_inc(stored, 16)
            sp.wait_ge(stored, 17)

        @block.vector
        def _(v):
            st = Steps(v, dve_step)
            asked = {"act": 0, "pe": 0, "pool": 0}
            asks = {"act": (ask_act, act_done), "pe": (ask_pe, pe_done), "pool": (ask_pool, pool_done)}

            def ask(who, ins):
                ins.then_inc(asks[who][0], 1)
                asked[who] += 1

            def answer(who, but=0):
                v.wait_ge(asks[who][1], asked[who] - but)

            def bc(ap, shape):
                return ap.to_broadcast(shape)

            for s in RING2:
                v.sem_inc(s, 2)
            for s in RING1:
                v.sem_inc(s, 1)
            v.sem_inc(xz_copied, 4)

            v.wait_ge(x_in, 16)

            def layer_norm(src, eps):
                st(v.tensor_reduce(lnsum[:], src[:], AX.X, ALU.add))
                st(v.tensor_scalar(lnneg[:], lnsum[:], -1.0 / C, None, ALU.mult))
                for ts in HALVES:
                    ask("act", v.tensor_tensor(XC[:, ts], src[:, ts], bc(lnneg[:, ts].unsqueeze(2), [P, NT // 2, C]), ALU.add))
                for n, ts in enumerate(HALVES):
                    answer("act", 1 - n)
                    st(v.tensor_reduce(lnvar[:, ts], SQ[:, ts], AX.X, ALU.add))
                ask("act", v.tensor_scalar(lnvar[:], lnvar[:], 1.0 / C, eps, ALU.mult, ALU.add))
                answer("act")
                st(v.reciprocal(rstd[:], lnsd[:]))

            def normalised(dst):
                st(v.tensor_tensor(dst[:], XC[:], bc(rstd[:].unsqueeze(2), [P, NT, C]), ALU.mult))

            def turn_groups(stage, made, read=None):

                def make(k):
                    v.wait_ge(group_turned, k + NG * stage + 1)
                    made(k, k % 2)

                def take(k):
                    v.wait_ge(turned_used, k + NG * stage + 3)
                    read(k, k % 2)
                for k in range(2):
                    make(k)
                for k in range(NG):
                    if k + 2 < NG:
                        make(k + 2)
                    if read:
                        take(k)

            def group_norm(g, half):
                st(v.scalar_tensor_tensor(ygf[:, half], XC[:, bass.ds(g * GT, GT), :], X_SCALE,
                                          bc(rstd[:, bass.ds(g * GT, GT)].unsqueeze(2), [P, GT, C]), ALU.mult, ALU.mult))
                cut_group(half)

            def cut_group(half):
                st(v.tensor_copy(yg[:, half, :, 0], ygf[:, half]))
                v.tensor_tensor(yg[:, half, :, 1], ygf[:, half], yg[:, half, :, 0], ALU.subtract).then_inc(group_made, 1)

            def read_logits(width, bias, dst):
                def read(g, half):
                    o = ps[2 + half][:, 0:GT * width].rearrange("p (t k) -> p t k", t=GT)
                    d = dst[:, bass.ds(g * GT, GT), 0:width]
                    if bias is None:
                        v.tensor_scalar(d, o, UNSCALE, None, ALU.mult).then_inc(product_read, 1)
                    else:
                        v.scalar_tensor_tensor(d, o, UNSCALE, bc(bias.unsqueeze(1), [P, GT, width]), ALU.mult, ALU.add).then_inc(product_read, 1)
                return read

            def top2_gates(n_tiles, E, eps=None):
                lg, gx, gt = (z[:, 0:n_tiles, 0:E] for z in (logit, gex, gate))
                beats = SQ[:].rearrange("p t c -> p (t c)")[:, 0:n_tiles * E * E].rearrange("p (t e f) -> p t e f", t=n_tiles, e=E)
                mx, sm, z, rec = (gsum[:, k, 0:n_tiles] for k in range(4))
                st(v.tensor_reduce(mx, lg, AX.X, ALU.max))
                ask("act", v.tensor_tensor(gx, lg, bc(mx.unsqueeze(2), [P, n_tiles, E]), ALU.subtract))
                for e in range(E):
                    if e:
                        st(v.tensor_tensor(beats[:, :, e, 0:e], lg[:, :, 0:e], bc(lg[:, :, e:e + 1], [P, n_tiles, e]), ALU.is_ge))
                    st(v.tensor_tensor(beats[:, :, e, e:E], lg[:, :, e:E], bc(lg[:, :, e:e + 1], [P, n_tiles, E - e]), ALU.is_gt))
                st(v.tensor_reduce(gt, beats, AX.X, ALU.add))
                st(v.tensor_scalar(gt, gt, 1.5, None, ALU.is_lt))
                answer("act")
                st(v.tensor_tensor(gt, gt, gx, ALU.mult))
                st(v.tensor_reduce(sm, gt, AX.X, ALU.add))
                if eps is not None:
                    st(v.tensor_reduce(z, gx, AX.X, ALU.add))
                    st(v.scalar_tensor_tensor(sm, z, eps, sm, ALU.mult, ALU.add))
                st(v.reciprocal(rec, sm))
                st(v.tensor_tensor(gt, gt, bc(rec.unsqueeze(2), [P, n_tiles, E]), ALU.mult))

            def softmax_row():
                lg, mx, sm, rec = logit[:, 0, 0:8], gsum[:, 0, 0:1], gsum[:, 1, 0:1], gsum[:, 2, 0:1]
                st(v.tensor_reduce(mx, lg, AX.X, ALU.max))
                ask("act", v.tensor_scalar(gex[:, 0, 0:8], lg, mx, None, ALU.subtract))
                answer("act")
                st(v.tensor_reduce(sm, gex[:, 0, 0:8], AX.X, ALU.add))
                st(v.reciprocal(rec, sm))
                st(v.tensor_scalar(lg, gex[:, 0, 0:8], rec, None, ALU.mult))

            def image_means():
                ask("pe", v.tensor_reduce(SQ[:, 0, :], Y[:].rearrange("p t c -> p c t"), AX.X, ALU.add))
                answer("pe")

            def round_clip(dst, src, scale, tmp):
                st(v.tensor_scalar(tmp, src, scale, ROUND, ALU.mult, ALU.add))
                st(v.tensor_scalar(tmp, tmp, ROUND, QMAX, ALU.subtract, ALU.min))
                return v.tensor_scalar(dst, tmp if len(dst.shape) == len(tmp.shape) else
                                       bc(tmp.unsqueeze(2), list(dst.shape)), -QMAX, None, ALU.max)

            def sort_round(source, r):
                b = best[:, r * TOP:(r + 1) * TOP]
                settle(v, carried)
                st(v.max(b, source))
                settle(v, carried)
                st(v.match_replace(source, b, source, 0.0))

            def sort_segment(g, e):
                if e == 0:
                    st(v.tensor_copy(seg[:], keys[:, bass.ds(g * SEG, SEG)]))
                if e < NEAR_ROUNDS:
                    sort_round(seg[:], e)
                if e == NEAR_ROUNDS:
                    st(v.tensor_copy(nearlist[:, bass.ds(g * (NEAR_ROUNDS * TOP), NEAR_ROUNDS * TOP)], best[:]))

            def sort_list(g, e):
                if e < SHORT_ROUNDS:
                    sort_round(nearlist, e)
                if e == SHORT_ROUNDS:
                    st(v.tensor_copy(shortlist[:, bass.ds(g * (SHORT_ROUNDS * TOP), SHORT_ROUNDS * TOP)],
                                     best[:, 0:SHORT_ROUNDS * TOP]))

            def experts(m, T, beside=None, beside_steps=0):
                E, KH, FC = MOES[m]

                def group(g):
                    v.wait_ge(gate_turned, g + (NG * m + 1))
                    st(v.tensor_copy(gst[:].rearrange("p (t e) -> p t e", t=GT), gate[:, bass.ds(g * GT, GT), :]))
                    tg = T[:, bass.ds(g * GT, GT), :]
                    v.sem_inc(gate_staged, 1)
                    v.wait_ge(bias_done, g + (NG * m + 2))
                    st(v.tensor_tensor(tg, tg, ps[7][:, 0:GT * C].rearrange("p (t c) -> p t c", t=GT), ALU.add))
                    v.sem_inc(bias_read, 1)

                    def combine(e):
                        u = g * E + (e + UNIT0[m])
                        v.wait_ge(down_done, u + 3)
                        v.tensor_tensor(comb[:, e % 2], ps[4 + e % 2][:, 0:GT * C].rearrange("p (t c) -> p t c", t=GT),
                                        bc(gst[:].rearrange("p (t e) -> p t e", t=GT)[:, :, e:e + 1], [P, GT, C]),
                                        ALU.mult).then_inc(comb_done, 1)
                        v.wait_ge(comb_done, u + 3)
                        st(v.tensor_tensor(tg, tg, comb[:, e % 2], ALU.add))

                    for e in range(E):
                        if beside:
                            beside(g, e)
                        combine(e)

                with v.Fori(0, NG // 2) as it:
                    st.enter(it, 2 * (E + 2 + beside_steps))
                    for half in range(2):
                        group(it * 2 + half)
                    st.leave(NG // 2)

            def experts3():
                E, KH, FC = L3F
                st(v.tensor_scalar(gate[:], gate[:], G_SCALE, None, ALU.mult))
                st(v.tensor_copy(gatep[:, :, 0], gate[:]))
                st(v.tensor_tensor(gatep[:, :, 1], gate[:], gatep[:, :, 0], ALU.subtract))

                def whole(g, k):
                    v.wait_ge(sil_done, g * (E * FC) + (k + 3))
                    v.wait_ge(low_done[k % 2], g * (E * FC // 2) + (k // 2 + 1))
                    v.scalar_tensor_tensor(hid[:, k % 4], ps[2 + k % 2][:, :], UNSCALE * H_SCALE,
                                           sil[:, k % 2, :], ALU.mult, ALU.mult).then_inc(hid_made, 1)
                    if k % 2:
                        slot = hidp[:, (k - 1) % (2 * FC)]
                        v.wait_ge(high_done, g * (E * FC) + (k + 2))
                        v.tensor_tensor(slot[:, 1], hid[:, (k - 1) % 4], slot[:, 0], ALU.subtract).then_inc(low_done[0], 1)

                def gate_output(g, e):
                    u = g * E + e
                    v.wait_ge(down_done, u + (UNIT0[3] + 3))
                    v.wait_ge(out_kept, u + 3)
                    if e == 0:
                        v.wait_ge(sum_turned, g + 1)
                    st(v.tensor_tensor(gated_out if e else out_sum, ps[4 + e % 2][:, :], outg[:, e % 2], ALU.mult))
                    if e == 0:
                        v.sem_inc(comb_done, 1)

                def sum_output(g, e):
                    v.tensor_tensor(out_sum, out_sum, gated_out, ALU.add).then_inc(comb_done, 1)
                    v.wait_ge(comb_done, g * E + (e + UNIT0[3] + 3))

                def add_sum(g):
                    xg = X[:, bass.ds(g * GT, GT), :]
                    v.wait_ge(sum_turned, g + 2)
                    st(v.scalar_tensor_tensor(xg, ps[6][:, 0:GT * C].rearrange("p (t c) -> p t c", t=GT),
                                              DN_UNSCALE / G_SCALE, xg, ALU.mult, ALU.add))

                def rest_of_group(g, last):
                    v.wait_ge(gate_turned, g + (NG * 3 + 1))
                    st(v.tensor_copy(gst3[:], gatep[:, bass.ds(g * GT, GT)].rearrange("p t k e -> p t (k e)")))
                    v.sem_inc(gate_staged, 1)
                    for k in range(ROT, E * FC + ROT):
                        if k < E * FC:
                            whole(g, k)
                        elif not last:
                            whole(g + 1, k - E * FC)
                        e, at = divmod(k - COMBINE_AT, FC)
                        if e >= 0 and at == 0:
                            gate_output(g, e)
                        if e > 0 and at == (2 if e < E - 1 else 1):
                            sum_output(g, e)
                    add_sum(g)

                for k in range(ROT):
                    whole(0, k)
                with v.Fori(0, NG - 1) as g:
                    st.enter(g, 1 + E + 1)
                    rest_of_group(g, False)
                    st.leave(NG - 1)
                rest_of_group(NG - 1, True)

            layer_norm(X, 1e-6)

            v.wait_ge(w0_in, 80)
            v.wait_ge(pool_const, POOL_CONSTS)
            v.wait_ge(weights_cut, 1)

            turn_groups(T_L0C, group_norm)
            v.wait_ge(w_in, W_LOADS * 16)
            amax, scale, inv = small[0:C, 8:9], small[0:C, 9:10], small[0:C, 10:11]
            st(v.tensor_reduce(amax, rq[:, 0:576], AX.X, ALU.max, apply_absolute_value=True))
            st(v.tensor_scalar(scale, amax, 1e-6, 1.0 / QMAX, ALU.max, ALU.mult))
            st(v.reciprocal(inv, scale))
            ask("pe", round_clip(wqb, rq[:, 0:576], inv, wqf))
            answer("pe")
            st(v.memset(rhsq[:], 0.0))
            wt = ps[2][:, 0:3 * C].bitcast(BF16).rearrange("p (k o) -> p k o", k=6)
            st(v.tensor_copy(rhsq[:, 0:6:2, :], wt[:, 0:6:2, :]))
            st(v.tensor_copy(rhsq[0:C, 1:6:2, :], wt[0:C, 1:6:2, :]))
            ask("pe", v.tensor_copy(SQ[0:C, 0:2, :].rearrange("p a c -> p (a c)"), bc(scale, [C, P])))
            answer("pe")
            st(v.tensor_copy(srow[:], ps[3][:, 0:C]))
            v.wait_ge(xz_copied, 4 + 2 * NG)
            st(v.memset(xbuf[:, 0:(TAPS - 1) * P], 0.0))
            prev = xbuf[:, NT * P:XW].rearrange("p (t b h) -> p t b h", t=TAPS - 1, b=B)
            head = xbuf[:, 0:(TAPS - 1) * P].rearrange("p (t b h) -> p t b h", t=TAPS - 1, b=B)
            for t in range(TAPS - 1):
                st(v.tensor_copy(head[:, t, :, 1:H], prev[:, t, :, 0:H - 1]))

            def convolve(k):
                g, half = k, k % 2
                v.wait_ge(conv_silu, (k + 1))
                st(v.tensor_scalar(cu[:, half], xbuf[:, bass.ds(g * GN, GN)], c0w[:, 0:1], None, ALU.mult))
                for tap in range(1, TAPS):
                    ins = v.scalar_tensor_tensor(cu[:, half], xbuf[:, bass.ds(g * GN + tap * P, GN)], c0w[:, tap:tap + 1],
                                                 cu[:, half], ALU.mult, ALU.add)
                    if tap == TAPS - 1:
                        ins.then_inc(conv_made, 1)
                    else:
                        st(ins)

            def gated(k):
                v.wait_ge(conv_silu, (k + 3))
                v.wait_ge(conv_out, (k + 1))
                v.scalar_tensor_tensor(cy[:, k % 2], csu[:, k % 2], 4.0, zs[:, bass.ds(k * GN, GN)],
                                       ALU.mult, ALU.mult).then_inc(conv_gated, 1)

            def add_out(k):
                v.wait_ge(conv_out, (k + 3))
                xg = X[:, bass.ds(k * GT, GT), :]
                st(v.tensor_tensor(xg, xg, ps[k % 2][:, 0:GT * C].rearrange("p (t c) -> p t c", t=GT), ALU.add))
                v.sem_inc(conv_added, 1)

            for k in range(NG + 2):
                if k < NG:
                    convolve(k)
                if 1 <= k <= NG:
                    gated(k - 1)
                if k >= 2:
                    add_out(k - 2)

            layer_norm(X, 1e-5)
            turn_groups(T_L0F, group_norm, read_logits(8, gb[0][:, 0:8], logit))
            v.wait_ge(product_read, 2 + NG)
            top2_gates(NT, 8)
            v.wait_ge(near_made, 1)
            experts(0, X, sort_segment, 2 * NEAR_ROUNDS + 2)
            st(v.tensor_reduce(segcnt[:], isnear.rearrange("p (s c) -> p s c", s=NSEG), AX.X, ALU.add))
            st(v.tensor_reduce(counts[:, 0, 0:1], segcnt[:], AX.X, ALU.max))
            ask("pool", v.tensor_reduce(counts[:, 0, 1:2], segcnt[:], AX.X, ALU.add))
            answer("pool")
            st(v.tensor_scalar(segcnt[:, 0:1], counts[:, 1, 0:1], float(NEAR_ROUNDS * TOP), None, ALU.is_gt))
            st(v.tensor_scalar(segcnt[:, 1:2], counts[:, 1, 1:2], float(SHORT_BLOCKS * BLK), None, ALU.is_gt))
            st(v.tensor_tensor(plan[:, 1:2], segcnt[:, 0:1], segcnt[:, 1:2], ALU.max))
            st(v.tensor_scalar(plan[:, 0:1], counts[:, 1, 1:2], float(BLK - 1), None, ALU.add))
            st(v.tensor_scalar(plan[:, 0:1], plan[:, 0:1], 3, None, ALU.logical_shift_right))
            st(v.tensor_scalar(plan[:, 2:3], plan[:, 1:2], NBLK, None, ALU.mult))
            st(v.tensor_tensor(plan[:, 0:1], plan[:, 0:1], plan[:, 2:3], ALU.max))

            ask("pool", v.drain())
            layer_norm(X, 1e-6)
            normalised(Y)
            answer("pool")
            ask("pe", v.tensor_reduce(small[:, 11:12], Y[:].rearrange("p t c -> p (t c)"), AX.X, ALU.max,
                                      apply_absolute_value=True))
            answer("pe")
            st(v.tensor_reduce(small[0:1, 12:16], ps[6][0:1, 0:P].rearrange("p (b h) -> p b h", b=B), AX.X, ALU.max))
            ask("pe", v.tensor_copy(SQ[0:1, 0:2, :].rearrange("p a c -> p (a c)").rearrange("p (b h) -> p b h", b=B),
                                    bc(small[0:1, 12:16].unsqueeze(2), [1, B, H])))
            answer("pe")
            st(v.tensor_scalar(small[:, 16:17], ps[7][:, 0:1], 1e-6, 1.0 / QMAX, ALU.max, ALU.mult))
            st(v.reciprocal(small[:, 17:18], small[:, 16:17]))
            with v.Fori(0, NG // 2) as it:
                st.enter(it, 4)
                for half in range(2):
                    g = it * 2 + half
                    v.wait_ge(q_turned, g + 1)
                    round_clip(qg[:, half], Y[:, bass.ds(g * GT, GT), :], small[:, 17:18], qf[:, half]).then_inc(group_made, 1)
                for half in range(2):
                    g = it * 2 + half
                    v.wait_ge(q_turned, g + 3)
                    v.tensor_copy(qpad[C:P, 0, bass.ds(g * GT + 1, GT), :].rearrange("p x n -> p (x n)"),
                                  ps[half][C:P, 0:GT * C].bitcast(BF16)).then_inc(q_high, 1)
                st.leave(NG // 2)
            with v.Fori(0, NG // 2) as it:
                st.enter(it, 4)
                for half in range(2):
                    g = it * 2 + half
                    v.wait_ge(taps_done, g + 3)
                    xg = X[:, bass.ds(g * GT, GT), :]
                    st(v.scalar_tensor_tensor(comb[:, half], ps[4 + half][:, 0:GT * C].rearrange("p (t c) -> p t c", t=GT),
                                              small[:, 16:17], bc(srow[:].unsqueeze(1), [P, GT, C]), ALU.mult, ALU.mult))
                    v.sem_inc(taps_read, 1)
                    st(v.tensor_tensor(xg, xg, comb[:, half], ALU.add))
                st.leave(NG // 2)

            layer_norm(X, 1e-5)
            turn_groups(T_L1F, group_norm)
            normalised(Y)
            image_means()
            ask("pe", v.tensor_scalar(SQ[0:C, 1:3, :].rearrange("p a c -> p (a c)").rearrange("p (b h) -> p b h", b=B),
                                      bc(ps[6][0:C, 0:B].unsqueeze(2), [C, B, H]), 1.0 / L, None, ALU.mult))
            answer("pe")
            st(v.tensor_tensor(logit[:, 0, 0:8], ps[7][:, 0:8], gb[1][:, 0:8], ALU.add))
            softmax_row()
            ask("pe", v.tensor_copy(SQ[:, 3, 0:8], logit[:, 0, 0:8]))
            answer("pe")
            load = SQ[:, 4, 0:8]
            st(v.tensor_scalar(load, ps[6][:, 0:8], float(L // H), None, ALU.mult))
            st(v.reciprocal(load, load))
            st(v.tensor_scalar(load, load, float(CAPACITY), 1.0, ALU.mult, ALU.min))
            st(v.tensor_tensor(logit[:, 0, 0:8], logit[:, 0, 0:8], load, ALU.mult))
            softmax_row()
            top2_gates(1, 8)
            st(v.tensor_copy(gate[:, 1:NT, :], bc(gate[:, 0:1, :], [P, NT - 1, 8])))
            experts(1, Y, sort_list, 2 * SHORT_ROUNDS + 1)
            unsorted = v.value_load(plan[0:1, 1:2], min_val=0, max_val=1)
            with v.If(unsorted < 1):
                v.tensor_copy(keys[:, 0:SHORT_BLOCKS * BLK], shortlist).then_inc(list_kept, 1)
                v.wait_ge(list_kept, 1)
                settle(v, carried)
            ask("pool", v.drain())
            layer_norm(Y, 1e-5)
            normalised(Y)
            st(v.tensor_tensor(Y[:], Y[:], bc(gam1[:].unsqueeze(1), [P, NT, C]), ALU.mult))
            answer("pool")
            st(v.tensor_tensor(X[:], X[:], Y[:], ALU.add))

            layer_norm(X, 1e-6)
            normalised(Y)
            image_means()
            ask("pe", v.tensor_scalar(SQ[0:C, 1, 0:B], ps[6][0:C, 0:B], 1.0 / L, None, ALU.mult))
            answer("pe")
            st(v.tensor_scalar(small[0:4, 20:24], ps[7][0:4, 0:B], se1b[:, 0:1], 0.0, ALU.add, ALU.max))
            ask("pe", v.tensor_copy(SQ[0:4, 2:4, :].rearrange("p a c -> p (a c)").rearrange("p (b h) -> p b h", b=B),
                                    bc(small[0:4, 20:24].unsqueeze(2), [4, B, H])))
            answer("pe")
            ask("act", v.tensor_tensor(SQ[:, 4, :], ps[6][:, 0:C], se2b[:], ALU.add))
            answer("act")
            st(v.tensor_tensor(Y[:], Y[:], bc(SQ[:, 4:5, :], [P, NT, C]), ALU.mult))
            st(v.tensor_tensor(X[:], X[:], Y[:], ALU.add))

            layer_norm(X, 1e-5)
            turn_groups(T_L2F, group_norm, read_logits(16, None, hn))
            v.wait_ge(product_read, 2 + READ0[T_WAV])
            hk = SQ[:].rearrange("p t c -> p (t c)")[:, 0:NT * 16].rearrange("p (t k) -> p t k", t=NT)
            hk4 = hk.rearrange("p t (h k) -> p t h k", h=HEADS)
            sa, da, sw, sv = (av[:, k] for k in range(4))
            for k, dst in ((0, sa), (1, da)):
                st(v.tensor_tensor(hk, hn, bc(att[:, k:k + 1, :], [P, NT, 16]), ALU.mult))
                st(v.tensor_reduce(dst, hk4, AX.X, ALU.add))
            ask("pool", v.tensor_reduce(small[:, 24:28], sa.rearrange("p t h -> p h t"), AX.X, ALU.max))
            answer("pool")
            top = bc(small[:, 28:32].unsqueeze(1), [P, NT, HEADS])
            sp_, sq_, sh_ = stab[:, :, 0:4], stab[:, :, 4:8], stab[:, :, 8:SRCW]
            du_, dv_ = dtab[:, :, 0:4], dtab[:, :, 4:8]
            st(v.tensor_tensor(sp_, sa, top, ALU.subtract))
            st(v.tensor_scalar(sq_, sp_, 0.2, None, ALU.mult))
            st(v.tensor_tensor(da, da, top, ALU.add))
            st(v.scalar_tensor_tensor(sw, da, 0.2, da, ALU.mult, ALU.max))
            st(v.tensor_tensor(du_, da, sw, ALU.subtract))
            ask("act", v.scalar_tensor_tensor(dv_, da, 0.2, sw, ALU.mult, ALU.subtract))
            st(v.tensor_copy(sh_, hn))
            answer("act")
            v.sem_inc(tables_out, 1)
            st(v.tensor_tensor(sw, sp_, du_, ALU.mult))
            st(v.tensor_tensor(sv, sq_, dv_, ALU.mult))
            st(v.tensor_tensor(aggr[:, :, 16:MSG], sw, sv, ALU.max))
            ask("pe", v.drain())
            answer("pe")
            last = av[:, 1].rearrange("p t h -> p (t h)")[:, 0:SRCW].unsqueeze(1)
            st(v.tensor_copy(last, ps[4][:, 0:SRCW].unsqueeze(1)))
            a4 = aggr[:, :, 0:16].rearrange("p t (h k) -> p t h k", h=HEADS)
            for h in range(HEADS):
                ins = v.tensor_tensor(a4[:, :, h, :], hn[:, :, h * HK:(h + 1) * HK],
                                      bc(aggr[:, :, 16 + h:17 + h], [P, NT, HK]), ALU.mult)
                if h < HEADS - 1:
                    st(ins)
                else:
                    ask("pe", ins)
            answer("pe")

            def cut_nodes(kb, t, to, sc):
                sc(v.tensor_scalar(t, kb, -1.0, 0.0, ALU.add, ALU.max))
                sc(v.tensor_scalar(to[:, 0], t, NODES - 1, None, ALU.bitwise_and))
                return v.tensor_scalar(to[:, 1], t, 12, None, ALU.logical_shift_right)

            def cut_places(kb, t, part, to, sc):
                sc(v.tensor_scalar(t, kb, -1.0, 0.0, ALU.add, ALU.max))
                sc(v.tensor_scalar(part, t, 12, W - 1, ALU.logical_shift_right, ALU.bitwise_and))
                sc(v.tensor_copy(to[:, 1], part))
                sc(v.tensor_scalar(part, t, 17, None, ALU.logical_shift_right))
                sc(v.tensor_scalar(to[:, 0], kb, 0.5, 1000.0, ALU.is_lt, ALU.mult))
                return v.tensor_tensor(to[:, 0], to[:, 0], part, ALU.subtract)

            def count_far(i, n):
                v.wait_ge(far_counted, i + (n + 1))
                for k, part in enumerate((farhi, farlo)):
                    v.tensor_tensor(farhot[:, n % 2, k], iotaQ[:],
                                    bc(part[:, bass.ds(i * FARB + n * FARB, FARB)].unsqueeze(1), [P, FQ, FARB]),
                                    ALU.is_equal).then_inc(far_made, 1)

            table_keys = keys[:, 0:TABLE]
            st(cut_nodes(table_keys, spare[:, 0], nodes, st))
            for half in range(2):
                v.tensor_copy(ei[:, half], nodes[:, :, half * BLK:(half + 1) * BLK]).then_inc(idx_ready, 1)
            st(cut_places(table_keys, spare[:, 0], spare[:, 1], places, st))
            for n in range(FAR_FIRST):
                count_far(0, n)

            def add_block(b, pair, half, phase):
                es = Steps(v, edge_step)
                es.i, es.per = b, 2
                gs, gd, m, kb = gsrc[:, half], gdst[:, half], em[:, half], keys[:, bass.ds(b * BLK, BLK)]
                v.wait_ge(hot_made, b + 1)
                if phase < 2:
                    v.tensor_copy(ef[:, half], places[:, :, bass.ds(b * BLK, BLK)]).then_inc(places_cut, 1)
                else:
                    rs = Steps(v, rest_step)
                    rs.i, rs.per = b - SHORT_BLOCKS, 7
                    cut_places(kb, epart[:, 0], epart[:, 1], ef[:, half], rs).then_inc(places_cut, 1)
                v.wait_ge(src_in[half], pair * (16 * BLK) + 16 * BLK)
                v.wait_ge(dst_in[half], pair * (16 * BLK) + 16 * BLK)
                if phase < 2:
                    v.tensor_copy(ei[:, half], nodes[:, :, bass.ds((b + 2) * BLK, BLK)]).then_inc(idx_ready, 1)
                else:
                    cut_nodes(keys[:, bass.ds((b + 2) * BLK, BLK)], epart[:, 0], ei[:, half], rs).then_inc(idx_ready, 1)
                es(v.tensor_tensor(ew, gs[:, :, 0:8], gd, ALU.mult))
                es(v.tensor_tensor(m[:, :, 16:MSG], ew[:, :, 0:4], ew[:, :, 4:8], ALU.max))
                v.tensor_tensor(m[:, :, 0:16].rearrange("p c (h k) -> p c h k", h=HEADS),
                                gs[:, :, 8:SRCW].rearrange("p c (h k) -> p c h k", h=HEADS),
                                bc(m[:, :, 16:MSG].unsqueeze(3), [P, BLK, HEADS, HK]), ALU.mult).then_inc(rows_used, 1)
                v.wait_ge(rows_used, b + 3)
                v.wait_ge(places_cut, b + 1)
                v.wait_ge(block_added, b + 1)
                for c in range(BLK):
                    v.scalar_tensor_tensor(spread[:, half, c], bc(iotaW[:].unsqueeze(2), [P, W, MSG]),
                                           ef[:, half, 1, c:c + 1], bc(m[:, c:c + 1, :], [P, W, MSG]),
                                           ALU.is_equal, ALU.mult).then_inc(spread_made, 1)
                    if phase == 0 and c < FAR_PER_BLOCK:
                        count_far(b * FAR_PER_BLOCK, FAR_FIRST + c)
                v.wait_ge(spread_made, (b + 1) * BLK)
                settle(v, carried)

            total = v.value_load(plan[0:1, 0:1], min_val=0, max_val=NBLK)
            run_blocks(v, total, add_block)
            ask("pe", v.drain())
            answer("pe")
            for k in range(2):
                st(v.tensor_copy(aggr[:, k * 16:(k + 1) * 16, :].rearrange("p t k -> p (t k)"), ps[6 + k][:, 0:16 * MSG]))
            st(v.tensor_copy(farcnt, ps[5][0:FQ, 0:FQ]))
            ask("pe", v.drain())
            answer("pe")
            st(v.tensor_copy(fardst[:], ps[4][:, 0:NT]))
            farw = av[:, 0]
            st(v.tensor_tensor(sw, du_, bc(last[:, :, 0:4], [P, NT, HEADS]), ALU.mult))
            st(v.tensor_tensor(sv, dv_, bc(last[:, :, 4:8], [P, NT, HEADS]), ALU.mult))
            st(v.tensor_tensor(farw, sw, sv, ALU.max))
            st(v.tensor_tensor(farw, farw, bc(fardst[:].unsqueeze(2), [P, NT, HEADS]), ALU.mult))
            for h in range(HEADS):
                st(v.tensor_tensor(hk4[:, :, h, :], bc(last[:, :, 8 + h * HK:8 + (h + 1) * HK], [P, NT, HK]),
                                   bc(farw[:, :, h:h + 1], [P, NT, HK]), ALU.mult))
            st(v.tensor_tensor(aggr[:, :, 0:16], aggr[:, :, 0:16], hk, ALU.add))
            st(v.tensor_tensor(aggr[:, :, 16:MSG], aggr[:, :, 16:MSG], farw, ALU.add))
            den = av[:, 0]
            st(v.tensor_scalar(den, aggr[:, :, 16:MSG], 1e-16, None, ALU.add))
            st(v.reciprocal(den, den))
            for h in range(HEADS):
                st(v.tensor_tensor(hk4[:, :, h, :], aggr[:, :, h * HK:(h + 1) * HK], bc(den[:, :, h:h + 1], [P, NT, HK]), ALU.mult))
            v.sem_inc(edges_left, 1)
            vec = lambda k: bc(gatv[:, k:k + 1, :], [P, NT, 16])
            st(v.tensor_tensor(hk, hk, vec(0), ALU.add))
            st(v.tensor_reduce(lnsum[:], hk, AX.X, ALU.add))
            st(v.tensor_scalar(lnneg[:], lnsum[:], -1.0 / 16, None, ALU.mult))
            st(v.tensor_tensor(hk, hk, bc(lnneg[:].unsqueeze(2), [P, NT, 16]), ALU.add))
            sq16 = SQ[:].rearrange("p t c -> p (t c)")[:, NT * 16:NT * 32].rearrange("p (t k) -> p t k", t=NT)
            st(v.tensor_tensor(sq16, hk, hk, ALU.mult))
            st(v.tensor_reduce(lnvar[:], sq16, AX.X, ALU.add))
            ask("act", v.tensor_scalar(lnvar[:], lnvar[:], 1.0 / 16, 1e-5, ALU.mult, ALU.add))
            answer("act")
            st(v.reciprocal(rstd[:], lnsd[:]))
            st(v.tensor_tensor(hk, hk, bc(rstd[:].unsqueeze(2), [P, NT, 16]), ALU.mult))
            st(v.tensor_tensor(hk, hk, vec(1), ALU.mult))
            st(v.tensor_tensor(hk, hk, vec(2), ALU.add))
            st(v.tensor_reduce(logit[:, :, 0:4], hk.rearrange("p t (h k) -> p t k h", h=HEADS), AX.X, ALU.add))
            st(v.tensor_scalar(logit[:, :, 0:4], logit[:, :, 0:4], 1.0 / HEADS, None, ALU.mult))
            st(v.memset(gate[:], 0.0))
            top2_gates(NT, 4)
            experts(2, X)

            v.sem_inc(masks_in, 1)
            layer_norm(X, 1e-6)
            normalised(Y)
            v.wait_ge(masks_in, 49)
            st(v.tensor_copy(hb[:, 1, 1:FT:2], hb[:, 0, 1:FT:2]))
            st(v.tensor_scalar(hb[:, 1, 0:FT:2], hb[:, 0, 0:FT:2], -1.0, None, ALU.mult))
            for mat, mask in ((rc, maskC), (rh, maskH)):
                st(v.tensor_scalar(mat[:], mask[:, 0], hb[:, 0, 0:1], None, ALU.mult))
                for k in range(1, FT):
                    ins = v.scalar_tensor_tensor(mat[:], mask[:, k], hb[:, 0, k:k + 1], mat[:], ALU.mult, ALU.add)
                    if k == FT - 1 and mat is rh:
                        ask("pe", ins)
                    else:
                        st(ins)
            st(v.tensor_scalar(rc[:], rc[:], W_SCALE, None, ALU.mult))
            st(v.tensor_copy(rcp[:, 0], rc[:]))
            st(v.tensor_tensor(rcp[:, 1], rc[:], rcp[:, 0], ALU.subtract))
            answer("pe")
            ask("act", v.drain())
            answer("act")
            for par in range(2):
                rows_out = ACC[:].rearrange("p (m two) c -> p m two c", two=2)[:, :, par]
                first = True
                for k in range(1 - par, FT, 2):
                    off = ((par + k - 1) // 2 - (FT // 2 - 1)) % (W // 2)
                    for wide, filt in ((0, hb[:, 0, FT - 1 - k:FT - k]), (1, hb[:, 1, k:k + 1])):
                        for m0, m1, s0 in ((0, W // 2 - off, off), (W // 2 - off, W // 2, 0)):
                            if m0 == m1:
                                continue
                            srcs = XC[:, wide * (W // 2) + s0:wide * (W // 2) + s0 + m1 - m0, :]
                            o = rows_out[:, m0:m1, :]
                            if first:
                                st(v.tensor_scalar(o, srcs, filt, None, ALU.mult))
                            else:
                                st(v.scalar_tensor_tensor(o, srcs, filt, o, ALU.mult, ALU.add))
                        first = False

            def copy_group(g, half):
                st(v.tensor_scalar(ygf[:, half], ACC[:, bass.ds(g * GT, GT), :], X_SCALE, None, ALU.mult))
                cut_group(half)

            def add_group(g, half):
                xg = X[:, bass.ds(g * GT, GT), :]
                v.scalar_tensor_tensor(xg, ps[2 + half][:, 0:GT * C].rearrange("p (t c) -> p t c", t=GT), UNSCALE, xg,
                                       ALU.mult, ALU.add).then_inc(product_read, 1)
            turn_groups(T_WAV, copy_group, add_group)
            v.wait_ge(product_read, 2 + READ0[T_L3F])

            layer_norm(X, 1e-5)
            turn_groups(T_L3F, group_norm, read_logits(8, None, logit))
            v.wait_ge(product_read, 2 + READ0[T_L3F] + NG)
            top2_gates(NT, 8, 1e-9)
            experts3()
            v.drain().then_inc(stored, 1)

        @block.scalar
        def _(s):
            done = [0]

            def asked():
                done[0] += 1
                s.wait_ge(ask_act, done[0])

            def layer_norm():
                for ts in HALVES:
                    asked()
                    s.activation(SQ[:, ts], XC[:, ts], ACT.Square).then_inc(act_done, 1)
                asked()
                s.activation(lnsd[:], lnvar[:], ACT.Sqrt).then_inc(act_done, 1)

            def exp_gates(n_tiles, E):
                asked()
                s.activation(gex[:, 0:n_tiles, 0:E], gex[:, 0:n_tiles, 0:E], ACT.Exp).then_inc(act_done, 1)

            def turn_groups(stage, after=None):
                for k in range(NG + 1):
                    if k < NG:
                        s.wait_ge(group_turned, (k + NG * stage + 3))
                        s.activation(yT[:, bass.ds(k * GN, GN)], ps[k % 2][:, 0:GN // 2].bitcast(F16),
                                     ACT.Copy).then_inc(turned_copied, 1)
                    if after and k:
                        after(k - 1, (k - 1) % 2)

            def experts(m):
                E, KH, FC = MOES[m]

                def group(g):
                    for e in range(E):
                        for f in range(FC):
                            k = e * FC + f
                            n = g * (E * FC) + (k + CHUNK0[m])
                            s.wait_ge(hid_full, n + 3)
                            if f == 0:
                                s.wait_ge(down_done, g * E + (e + UNIT0[m] + 1))
                            s.activation(hS[0:KH, (e % 2) * FC + f, :], ps[k % 2][0:KH, :], ACT.Gelu,
                                         bias=ub[m][0:KH, k:k + 1], scale=UNSCALE).then_inc(hid_act, 1)
                        if e == 0:
                            s.wait_ge(gate_turned, g + (NG * m + 2))
                            s.wait_ge(bias_done, g + (NG * m + 1))
                            s.activation(gTs[:], ps[6][0:GT * 8, 0:P], ACT.Copy).then_inc(gate_copied, 1)

                with s.Fori(0, NG // 2) as it:
                    for half in range(2):
                        group(it * 2 + half)

            def experts3():
                E, KH, FC = L3F

                def high(g, k):
                    e = k // FC
                    s.wait_ge(hid_made, g * (E * FC) + (k + 3))
                    if k % FC == 0:
                        s.wait_ge(down_done, g * E + (e + UNIT0[3] + 1))
                    s.activation(hidp[:, k % (2 * FC), 0], hid[:, k % 4], ACT.Copy).then_inc(high_done, 1)

                def copy_gates(g):
                    s.wait_ge(gate_turned, g + (NG * 3 + 2))
                    s.wait_ge(gates_spread, g * E + 2)
                    s.activation(gT3[:], ps[6][0:16, 0:GN // 2].bitcast(F16), ACT.Copy).then_inc(gate_copied, 1)

                def keep(g, e):
                    s.wait_ge(gates_spread, g * E + (e + 3))
                    s.wait_ge(comb_done, g * E + (e + UNIT0[3] + 1))
                    s.activation(outg[:, e % 2], ps[7][:, :], ACT.Copy).then_inc(out_kept, 1)

                def gated(g, k):
                    n = g * (E * FC) + k
                    s.wait_ge(hid_full, n + (CHUNK0[3] + 3))
                    s.wait_ge(hid_made, n + 1)
                    s.activation(sil[:, k % 2], ps[k % 2][:, :], ACT.Silu, scale=UNSCALE).then_inc(sil_done, 1)

                def rest_of_group(g, last):
                    for k in range(ROT, E * FC + ROT):
                        if k < E * FC:
                            gated(g, k)
                            high(g, k - 1)
                        elif not last:
                            gated(g + 1, k - E * FC)
                            high(*((g + 1, k - E * FC - 1) if k > E * FC else (g, E * FC - 1)))
                        elif k == E * FC:
                            high(g, E * FC - 1)
                        if k == STAGE_AT + 1:
                            copy_gates(g)
                        if k >= KEEP_AT and (k - KEEP_AT) % FC == 0 and k < KEEP_AT + E * FC:
                            keep(g, (k - KEEP_AT) // FC)

                for k in range(ROT):
                    gated(0, k)
                    if k:
                        high(0, k - 1)
                with s.Fori(0, NG - 1) as g:
                    rest_of_group(g, False)
                rest_of_group(NG - 1, True)

            layer_norm()
            s.wait_ge(w0_in, 80)

            def copy_xz(g, half):
                s.wait_ge(turned_used, g + 3)
                s.activation(xbuf[:, bass.ds(g * GN + (TAPS - 1) * P, GN)], ps[4 + half][:, :], ACT.Copy, scale=UNSCALE).then_inc(xz_copied, 1)
                s.activation(zs[:, bass.ds(g * GN, GN)], ps[6 + half][:, :], ACT.Silu, scale=UNSCALE).then_inc(xz_copied, 1)
            turn_groups(T_L0C, copy_xz)
            with s.Fori(0, NG // 2) as it:
                for half in range(2):
                    g = it * 2 + half
                    s.wait_ge(conv_made, g + 1)
                    s.wait_ge(conv_gated, g + 1)
                    s.activation(csu[:, half], cu[:, half], ACT.Silu, bias=c0b[:, 0:1]).then_inc(conv_silu, 1)
            layer_norm()
            s.wait_ge(w_in, W_LOADS * 16)
            turn_groups(T_L0F)
            exp_gates(NT, 8)
            experts(0)
            layer_norm()
            with s.Fori(0, NG // 2) as it:
                for half in range(2):
                    g = it * 2 + half
                    s.wait_ge(q_turned, g + 3)
                    for k, o0, i0 in ((0, 1, 0), (1, 0, 1)):
                        ins = s.activation(
                            qpad[0:C, k, bass.ds(g * GT + 1, GT), :].rearrange("p x (b h) -> p x b h", b=B)[:, :, :, o0:o0 + H - 1],
                            ps[half][0:C, 0:GT * C].bitcast(BF16).rearrange("p (t b h) -> p t b h", t=GT, b=B)[:, :, :, i0:i0 + H - 1],
                            ACT.Copy)
                    ins.then_inc(q_low, 1)
            layer_norm()
            turn_groups(T_L1F)
            exp_gates(1, 8)
            exp_gates(1, 8)
            exp_gates(1, 8)
            experts(1)
            layer_norm()
            layer_norm()
            asked()
            s.activation(SQ[:, 4, :], SQ[:, 4, :], ACT.Sigmoid).then_inc(act_done, 1)
            layer_norm()
            turn_groups(T_L2F)
            asked()
            s.activation(dtab, dtab, ACT.Exp).then_inc(act_step, 1)
            s.activation(stab[:, :, 0:8], stab[:, :, 0:8], ACT.Exp).then_inc(act_done, 1)
            def make_hots(b, pair, half, phase):
                s.wait_ge(places_cut, b + 1)
                s.wait_ge(block_added, b + 1)
                settle(s, carried)
                for c in range(BLK):
                    s.activation(offset[:, c], iotaP[:], ACT.Square, bias=ef[:, half, 0, c:c + 1]).then_inc(offset_made, 1)
                s.wait_ge(offset_made, b * BLK + BLK)
                s.activation(onehot[:, half], offset, ACT.Relu, bias=ones[:, 0:1], scale=-1.0).then_inc(hot_made, 1)
                s.wait_ge(hot_made, b + 3)
                settle(s, carried)

            total = s.value_load(plan[0:1, 0:1], min_val=0, max_val=NBLK)
            run_blocks(s, total, make_hots)
            asked()
            s.activation(lnsd[:], lnvar[:], ACT.Sqrt).then_inc(act_done, 1)
            exp_gates(NT, 4)
            experts(2)
            layer_norm()
            asked()
            for k in range(4):
                ins = s.activation(XC[:].rearrange("p t c -> p (t c)")[:, k * 512:(k + 1) * 512], ps[k][:, :], ACT.Copy)
            ins.then_inc(act_done, 1)
            turn_groups(T_WAV)
            layer_norm()
            turn_groups(T_L3F)
            exp_gates(NT, 8)
            experts3()

        @block.tensor
        def _(t):
            def turn_groups(stage, product):
                def turn(k):
                    n = (k + NG * stage)
                    made = k + NG * stage + 1 + (NG if stage >= T_L1F else 0)
                    t.wait_ge(group_made, made)
                    t.wait_ge(turned_copied, n + 1)
                    settle(t, carried)
                    for j in range(GT):
                        ins = t.transpose(ps[k % 2][:, j * C:(j + 1) * C].bitcast(F16),
                                          yg[:, k % 2, j].rearrange("p d c -> p (d c)"), identh[:])
                    ins.then_inc(group_turned, 1)

                turn(0)
                for k in range(NG):
                    if k + 1 < NG:
                        turn(k + 1)
                    t.wait_ge(turned_copied, (k + NG * stage + 3))
                    product(k, k % 2)

            def logits(w, width, base):
                def product(g, half):
                    t.wait_ge(product_read, g + (base + 1))
                    settle(t, carried)
                    for j in range(GT):
                        for k in range(2):
                            ins = t.matmul(ps[2 + half][:, j * width:(j + 1) * width], yT[:, bass.ds(g * GN + j * P, P)],
                                           w[:, k], start=(k == 0), stop=(k == 1))
                    ins.then_inc(turned_used, 1)
                return product

            def experts3():
                E, KH, FC = L3F
                t.wait_ge(turned_copied, 2 + NG * (T_L3F + 1))
                t.wait_ge(product_read, 2 + READ0[T_L3F] + NG)
                t.wait_ge(piece_cut, PIECES)

                def project_up(g, k):
                    t.wait_ge(hid_made, g * (E * FC) + (k + 1))
                    settle(t, carried)
                    for q in range(2):
                        for part in range(2):
                            at = q * UP3H + k * KH
                            ins = t.matmul(ps[2 * q + k % 2][:, :], up3[:, part, at:at + P], yT[:, bass.ds(g * GN, GN)],
                                           start=(part == 0), stop=(part == 1))
                    ins.then_inc(hid_full, 1)

                def project_down(g, k):
                    e, f = k // FC, k % FC
                    t.wait_ge(low_done[k % 2], g * (E * FC // 2) + (k // 2 + 3))
                    if f == 0:
                        t.wait_ge(comb_done, g * E + (e + UNIT0[3] + 1))
                    for part in range(2):
                        ins = t.matmul(ps[4 + e % 2][:, :], dn3[:, k], hidp[:, k % (2 * FC), part],
                                       start=(f == 0 and part == 0), stop=(f == FC - 1 and part == 1))
                    if f == FC - 1:
                        ins.then_inc(down_done, 1)

                def turn_gates(g):
                    t.wait_ge(gate_staged, g + (NG * 3 + 1))
                    t.wait_ge(gate_copied, g + (NG * 3 + 1))
                    settle(t, carried)
                    for j in range(GT):
                        ins = t.transpose(ps[6][0:16, j * C:(j + 1) * C].bitcast(F16), gst3[:, j], identh[:])
                    ins.then_inc(gate_turned, 1)

                def spread_gates(g, e):
                    if e == 0:
                        t.wait_ge(gate_copied, g + (NG * 3 + 2))
                    t.wait_ge(out_kept, g * E + (e + 2))
                    t.matmul(ps[7][:, :], expsel[:, e], gT3[:], start=True, stop=True).then_inc(gates_spread, 1)

                def turn_sum(g):
                    t.wait_ge(comb_done, g * E + (E + UNIT0[3] + 2))
                    for j in range(GT):
                        ins = t.matmul(ps[6][:, j * C:(j + 1) * C], out_sum[:, j * P:(j + 1) * P], twoid[:],
                                       start=True, stop=True)
                    ins.then_inc(sum_turned, 1)

                def rest_of_group(g, last):
                    for k in range(ROT, E * FC + ROT):
                        over = k - E * FC
                        if k < E * FC:
                            project_up(g, k)
                        elif not last:
                            project_up(g + 1, over)
                        if over < LAG:
                            project_down(g, k - LAG)
                        elif not last:
                            project_down(g + 1, over - LAG)
                        if k == STAGE_AT:
                            turn_gates(g)
                        if k >= SPREAD_AT and (k - SPREAD_AT) % FC == 0 and k < SPREAD_AT + E * FC:
                            spread_gates(g, (k - SPREAD_AT) // FC)
                    turn_sum(g)

                for k in range(ROT):
                    project_up(0, k)
                    if k >= LAG:
                        project_down(0, k - LAG)
                with t.Fori(0, NG - 1) as g:
                    rest_of_group(g, False)
                rest_of_group(NG - 1, True)

            def experts(m, stage, reads, ups):
                E, KH, FC = MOES[m]
                t.wait_ge(turned_copied, 2 + NG * (stage + 1))
                t.wait_ge(product_read, 2 + reads)

                def group(g):
                    x = yT[:, bass.ds(g * GN, GN)]

                    def project_up(e):
                        for f in range(FC):
                            k = e * FC + f
                            n = g * (E * FC) + (k + CHUNK0[m])
                            t.wait_ge(hid_act, n + 1)
                            settle(t, carried)
                            for q, w in enumerate(ups):
                                for part in range(2):
                                    ins = t.matmul(ps[2 * q + k % 2][0:KH, :], w[:, part, k * KH:(k + 1) * KH], x,
                                                   start=(part == 0), stop=(part == 1))
                            ins.then_inc(hid_full, 1)

                    def project_down(e):
                        u = g * E + (e + UNIT0[m])
                        t.wait_ge(hid_act, g * (E * FC) + ((e + 1) * FC + CHUNK0[m] + 2))
                        t.wait_ge(comb_done, u + 1)
                        for j in range(GT):
                            for f in range(FC):
                                ins = t.matmul(ps[4 + e % 2][:, j * C:(j + 1) * C],
                                               hS[0:KH, (e % 2) * FC + f, j * P:(j + 1) * P],
                                               dn[m][:, e * FC + f, :], start=(f == 0), stop=(f == FC - 1))
                        ins.then_inc(down_done, 1)

                    def turn_gates():
                        t.wait_ge(gate_staged, g + NG * m + 1)
                        t.wait_ge(gate_copied, g + NG * m + 1)
                        t.transpose(ps[6][0:GT * 8, 0:P], gst[:], ident[:]).then_inc(gate_turned, 1)

                    def bias():
                        t.wait_ge(gate_copied, g + NG * m + 2)
                        t.wait_ge(bias_read, g + NG * m + 1)
                        t.matmul(ps[7][:, 0:GT * C], gTs[:], db[m][:].rearrange("p t c -> p (t c)"), start=True,
                                 stop=True).then_inc(bias_done, 1)

                    for e in range(E):
                        project_up(e)
                        if e == 0:
                            turn_gates()
                        if e == 1:
                            bias()
                        if e:
                            project_down(e - 1)
                    project_down(E - 1)

                with t.Fori(0, NG // 2) as it:
                    for half in range(2):
                        group(it * 2 + half)

            asked = [0]

            def ask():
                asked[0] += 1
                t.wait_ge(ask_pe, asked[0])

            t.wait_ge(pool_const, POOL_CONSTS)
            t.wait_ge(w0_in, 80)
            t.wait_ge(weights_cut, 1)

            def project_xz(g, half):
                t.wait_ge(xz_copied, g * 2 + 2)
                for bank in range(2):
                    for part in range(2):
                        ins = t.matmul(ps[4 + 2 * bank + half][:, :], w0in[:, part, bank * DI:(bank + 1) * DI],
                                       yT[:, bass.ds(g * GN, GN)], start=(part == 0), stop=(part == 1))
                ins.then_inc(turned_used, 1)

            turn_groups(T_L0C, project_xz)
            t.wait_ge(w_in, W_LOADS * 16)
            ask()
            wt = ps[2][:, 0:3 * C].bitcast(BF16).rearrange("p (k o) -> p k o", k=6)
            for dx in range(3):
                t.transpose(wt[:, 2 * dx], wqb[:, dx * 3 * C:dx * 3 * C + 2 * C], identb[0:C, 0:C])
                ins = t.transpose(wt[0:C, 2 * dx + 1], wqb[:, dx * 3 * C + 2 * C:(dx + 1) * 3 * C], identb[0:C, 0:C])
            ins.then_inc(pe_done, 1)
            ask()
            t.matmul(ps[3][:, 0:C], SQ[0:C, 0:2, :].rearrange("p a c -> p (a c)"), ident[0:C, 0:C], start=True, stop=True).then_inc(pe_done, 1)
            with t.Fori(0, NG // 2) as it:
                for half in range(2):
                    g = it * 2 + half
                    t.wait_ge(conv_gated, g + 3)
                    t.wait_ge(conv_added, g + 1)
                    for j in range(GT):
                        ins = t.matmul(ps[half][:, j * C:(j + 1) * C], cy[:, half, j * P:(j + 1) * P], w0out[:],
                                       start=True, stop=True)
                    ins.then_inc(conv_out, 1)
            t.wait_ge(weights_cut, 2)
            turn_groups(T_L0F, logits(gwp[0], 8, 0))
            experts(0, T_L0F, NG, [up[0]])

            def no_product(g, half):
                t.sem_inc(turned_used, 1)

            ask()
            t.transpose(ps[6][0:1, 0:P], small[:, 11:12], ident[:]).then_inc(pe_done, 1)
            ask()
            t.matmul(ps[7][:, 0:1], SQ[0:1, 0:2, :].rearrange("p a c -> p (a c)"), ones[0:1, 0:1], start=True, stop=True).then_inc(pe_done, 1)
            with t.Fori(0, NG // 2) as it:
                for half in range(2):
                    g = it * 2 + half
                    t.wait_ge(group_made, g + (2 * NG + 1))
                    t.wait_ge(q_low, g + 1)
                    t.wait_ge(q_high, g + 1)
                    for j in range(GT):
                        ins = t.transpose(ps[half][:, j * C:(j + 1) * C].bitcast(BF16),
                                          qg[:, half, j].rearrange("p d c -> p (d c)"), identb[:])
                    ins.then_inc(q_turned, 1)
            t.wait_ge(q_low, 2 + NG)
            t.wait_ge(q_high, 2 + NG)
            with t.Fori(0, NG // 2) as it:
                for half in range(2):
                    g = it * 2 + half
                    t.wait_ge(taps_read, g + 1)
                    for j in range(GT):
                        for k in range(6):
                            ins = t.matmul(ps[4 + half][:, j * C:(j + 1) * C],
                                           qpad[:, k % 2, bass.ds(g * GT + (j + k // 2), 1), :].rearrange("p x n -> p (x n)"),
                                           rhsq[:, k, :], start=(k == 0), stop=(k == 5))
                    ins.then_inc(taps_done, 1)
            turn_groups(T_L1F, no_product)
            ask()
            t.matmul(ps[6][0:C, 0:B], SQ[:, 0, :], blk32[:], start=True, stop=True).then_inc(pe_done, 1)
            ask()
            t.matmul(ps[7][:, 0:8], SQ[0:C, 1:3, :].rearrange("p a c -> p (a c)"), gw1[:], start=True, stop=True).then_inc(pe_done, 1)
            ask()
            t.matmul(ps[6][:, 0:8], ones[:], SQ[:, 3, 0:8], start=True, stop=True).then_inc(pe_done, 1)
            experts(1, T_L1F, READ0[T_L2F], [up[1]])
            ask()
            t.matmul(ps[6][0:C, 0:B], SQ[:, 0, :], blk32[:], start=True, stop=True).then_inc(pe_done, 1)
            ask()
            t.matmul(ps[7][0:4, 0:B], se1[:], SQ[0:C, 1, 0:B], start=True, stop=True).then_inc(pe_done, 1)
            ask()
            t.matmul(ps[6][:, 0:C], SQ[0:4, 2:4, :].rearrange("p a c -> p (a c)"), se2[:], start=True, stop=True).then_inc(pe_done, 1)
            turn_groups(T_L2F, logits(gwp[2], 16, READ0[T_L2F]))
            ask()
            t.matmul(ps[4][:, 0:SRCW], lastsel[:], stab[:, NT - 1, :], start=True, stop=True).then_inc(pe_done, 1)
            ask()
            flat = aggr.rearrange("p t k -> p (t k)")
            for k in range(2):
                ins = t.matmul(ps[6 + k][:, 0:16 * MSG], ident[:], flat[:, k * 16 * MSG:(k + 1) * 16 * MSG],
                               start=True, stop=False, skip_group_check=True)
            ins.then_inc(pe_done, 1)
            def count_far(i, n):
                t.wait_ge(far_made, i * 2 + 2 * (n + 1))
                settle(t, carried)
                for c in range(FARB):
                    ins = t.matmul(ps[5][0:FQ, 0:FQ], farhot[:, n % 2, 0, :, c], farhot[:, n % 2, 1, :, c],
                                   start=False, stop=False, skip_group_check=True)
                ins.then_inc(far_counted, 1)

            def add_block(b, pair, half, phase):
                t.wait_ge(hot_made, b + 3)
                for c in range(BLK):
                    t.wait_ge(spread_made, b * BLK + (c + 1))
                    for k in range(2):
                        ins = t.matmul(ps[6 + k][:, 0:16 * MSG], onehot[:, half, c],
                                       spread[:, half, c, k * 16:(k + 1) * 16, :].rearrange("p w m -> p (w m)"),
                                       start=False, stop=False, skip_group_check=True)
                    if c == BLK - 1:
                        ins.then_inc(block_added, 1)
                    if phase == 0 and c < FAR_PER_BLOCK:
                        count_far(b * FAR_PER_BLOCK, FAR_FIRST + c)

            t.matmul(ps[5][0:FQ, 0:FQ], zerob[:, 0:FQ], zerob[:, 0:FQ], start=True, stop=False, skip_group_check=True)
            for n in range(FAR_FIRST):
                count_far(0, n)
            total = t.value_load(plan[0:1, 0:1], min_val=0, max_val=NBLK)
            run_blocks(t, total, add_block)
            ask()
            t.drain().then_inc(pe_done, 1)
            ask()
            for k in range(2):
                ins = t.matmul(ps[4][:, 0:NT], halfsel[:, k], farcnt[:, k * NT:(k + 1) * NT], start=(k == 0), stop=(k == 1))
            ins.then_inc(pe_done, 1)
            assert asked[0] == PE_EDGES
            experts(2, T_L2F, READ0[T_WAV], [up[2]])
            ask()
            for k in range(4):
                ins = t.matmul(ps[k][:, :], rh[:], Y[:].rearrange("p t c -> p (t c)")[:, k * 512:(k + 1) * 512],
                               start=True, stop=True)
            ins.then_inc(pe_done, 1)
            turn_groups(T_WAV, logits(rcp, C, READ0[T_WAV]))
            turn_groups(T_L3F, logits(gwp[3], 8, READ0[T_L3F]))
            experts3()

        @block.gpsimd
        def _(q):
            for m in range(3):
                q.memset(db[m][:], 0.0)
            q.engine_nop().then_inc(pool_const, 1)
            cst = [1]

            def const(ins):
                ins.then_inc(pool_const, 1)
                cst[0] += 1
                q.wait_ge(pool_const, cst[0])
            const(q.memset(ident[:], 0.0))
            const(q.memset(ones[:], 1.0))
            const(q.affine_select(out=ident[:], in_=ident[:], compare_op=ALU.not_equal, fill=1.0, base=0,
                                  pattern=[[-1, P]], channel_multiplier=1))
            const(q.tensor_copy(identb[:], ident[:]))
            const(q.tensor_copy(identh[:], ident[:]))
            each = arena[0:16, 0:8 * P].rearrange("p (e q) -> p e q", e=8)
            const(q.memset(each, 0.0))
            for k in range(2):
                const(q.affine_select(out=each, in_=each, compare_op=ALU.not_equal, fill=1.0, base=-8 * k,
                                      pattern=[[-1, 8], [0, P]], channel_multiplier=1))
            const(q.tensor_copy(expsel[:], each))
            const(q.affine_select(out=twoid[:], in_=ident[:, 0:C], compare_op=ALU.not_equal, fill=1.0, base=-C,
                                  pattern=[[-1, C]], channel_multiplier=1))
            const(q.affine_select(out=blk32[:], in_=ones[:, 0:B], compare_op=ALU.is_ge, fill=0.0, base=0,
                                  pattern=[[-H, B]], channel_multiplier=1))
            const(q.affine_select(out=blk32[:], in_=blk32[:], compare_op=ALU.is_ge, fill=0.0, base=H - 1,
                                  pattern=[[H, B]], channel_multiplier=-1))
            const(q.iota(iotaP[:], [[1, P]], base=0, channel_multiplier=0, allow_small_or_imprecise_dtypes=True))
            const(q.iota(iotaQ[:], [[1, FQ], [0, FARB]], base=0, channel_multiplier=0, allow_small_or_imprecise_dtypes=True))
            const(q.memset(halfsel[:], 0.0))
            for k in range(2):
                const(q.affine_select(out=halfsel[:, k], in_=halfsel[:, k], compare_op=ALU.not_equal, fill=1.0, base=k,
                                      pattern=[[-1, P]], channel_multiplier=2))
            const(q.affine_select(out=lastsel[:], in_=ones[:], compare_op=ALU.is_ge, fill=0.0, base=1 - P,
                                  pattern=[[0, P]], channel_multiplier=1))
            const(q.memset(zerob[:], 0.0))
            const(q.iota(iotaW[:], [[1, W]], base=0, channel_multiplier=0, allow_small_or_imprecise_dtypes=True))
            assert cst[0] == POOL_CONSTS

            cuts = [0]

            def cut(parts, whole):
                for ins in (lambda: q.tensor_scalar(whole, whole, W_SCALE, None, ALU.mult),
                            lambda: q.tensor_copy(parts[:, 0], whole),
                            lambda: q.tensor_tensor(parts[:, 1], whole, parts[:, 0], ALU.subtract)):
                    ins().then_inc(pool_step, 1)
                    cuts[0] += 1
                    q.wait_ge(pool_step, cuts[0])

            q.wait_ge(w0_in, 80)
            cut(w0in, stage_w0)
            q.sem_inc(weights_cut, 1)
            q.wait_ge(w_in, W_LOADS * 16)
            for m in (0, 2, 3):
                cut(gwp[m], stage_gw[m])
            for m in range(3):
                cut(up[m], stage_up[m])
            q.sem_inc(weights_cut, 1)
            near = keys[:, 0:EPP]

            def step(ins):
                ins.then_inc(pool_step, 1)
                cuts[0] += 1
                q.wait_ge(pool_step, cuts[0])
            q.wait_ge(edges_in, 32)
            src, dst = esrc.bitcast(F32), edst.bitcast(F32)
            step(q.tensor_copy(src, esrc))
            step(q.tensor_copy(dst, edst))
            step(q.tensor_scalar(isnear, src, float(NODES - 1), None, ALU.is_lt))
            step(q.tensor_scalar(near, dst, float(NODES), None, ALU.is_lt))
            step(q.tensor_tensor(isnear, isnear, near, ALU.mult))
            step(q.tensor_scalar(near, dst, float(NODES), 1.0, ALU.mult, ALU.add))
            step(q.tensor_tensor(near, near, src, ALU.add))
            step(q.tensor_tensor(near, near, isnear, ALU.mult))
            q.memset(keys[:, EPP:EPP + 2 * BLK], 0.0).then_inc(near_made, 1)
            step(q.tensor_scalar(farhi[:], isnear, 1024.0, None, ALU.mult))
            high = src
            step(q.tensor_scalar(high, dst, 1.0 / FQ, -(FQ - 1.0) / (2 * FQ), ALU.mult, ALU.add))
            step(q.tensor_scalar(high, high, ROUND, None, ALU.add))
            step(q.tensor_scalar(high, high, ROUND, None, ALU.subtract))
            step(q.tensor_tensor(farhi[:], farhi[:], high, ALU.add))
            step(q.tensor_scalar(high, high, -float(FQ), None, ALU.mult))
            step(q.tensor_tensor(farlo[:], high, dst, ALU.add))
            q.wait_ge(ask_pool, 1)
            q.partition_all_reduce(counts[:, 1], counts[:, 0], P, RMAX).then_inc(pool_done, 1)
            q.wait_ge(ask_pool, 2)
            q.memset(qpad, 0.0).then_inc(pool_done, 1)
            q.wait_ge(ask_pool, 3)
            q.tensor_tensor(X[:], X[:], bet1[:].unsqueeze(1).to_broadcast([P, NT, C]), ALU.add).then_inc(pool_done, 1)

            q.wait_ge(ask_pool, 4)
            q.partition_all_reduce(small[:, 28:32], small[:, 24:28], P, RMAX).then_inc(pool_done, 1)
            q.wait_ge(tables_out, 33)

            def gather_block(b, pair, half, phase):
                q.wait_ge(idx_ready, b + 1)
                q.wait_ge(rows_used, b + 1)
                settle(q, carried)
                for c in range(BLK):
                    q.indirect_dma_start(gsrc[:, half, c], None, src_rows,
                                         bass.IndirectOffsetOnAxis(ap=ei[:, half, 0, c:c + 1].bitcast(U32), axis=0)).then_inc(src_in[half], 16)
                    q.indirect_dma_start(gdst[:, half, c], None, dst_rows,
                                         bass.IndirectOffsetOnAxis(ap=ei[:, half, 1, c:c + 1].bitcast(U32), axis=0)).then_inc(dst_in[half], 16)

            total = q.value_load(plan[0:1, 0:1], min_val=0, max_val=NBLK)
            run_blocks(q, total, gather_block)
            for n in range(PIECES):
                q.wait_ge(piece_in[n % 2], 32 * (n // 2 + 1))
                if n < UP_PIECES:
                    cut(up3[:, :, n * PIECE:(n + 1) * PIECE], piece[:, n % 2])
                else:
                    k = n - UP_PIECES
                    per = DN_PIECE // C
                    cut(dn3[:, k * per:(k + 1) * per].rearrange("p a (k c) -> p k a c", k=2),
                        piece[:, n % 2, 0:DN_PIECE].rearrange("p (a c) -> p a c", c=C))
                q.sem_inc(piece_cut, 1)
            E, KH, FC = L3F
            with q.Fori(0, NG) as g:
                for k in range(1, E * FC, 2):
                    slot = hidp[:, k % (2 * FC)]
                    q.wait_ge(high_done, g * (E * FC) + (k + 3))
                    q.tensor_tensor(slot[:, 1], hid[:, k % 4], slot[:, 0], ALU.subtract).then_inc(low_done[1], 1)


def kernel(**inputs):
    import numpy as np
    import concourse.bacc as bacc
    from concourse.bass_utils import run_bass_kernel_spmd as run

    nc = bacc.Bacc("TRN2", target_bir_lowering=False, num_devices=1)
    arrays, aps = {}, {}

    def give(name, v):
        v = np.ascontiguousarray(v)
        arrays[f"in_{name}"] = v
        aps[name] = nc.dram_tensor(f"in_{name}", v.shape, mybir.dt.from_np(v.dtype), kind="ExternalInput").ap()

    i = {k: np.asarray(v) for k, v in inputs.items()}
    give("x", i["x"].reshape(P, NT, C))
    give("src", i["L2_ffn_edge_index"][0].reshape(P, EPP))
    give("dst", i["L2_ffn_edge_index"][1].reshape(P, EPP))
    give("w0in", i["L0_conv_W_in"].T)
    give("w0out", i["L0_conv_W_out"].T)
    give("c0w", i["L0_conv_conv_w"].reshape(DI, TAPS))
    give("c0b", i["L0_conv_conv_b"].reshape(DI, 1))

    def ups(w, k, f):
        e, c, h = w.shape
        r = np.zeros((c, e, k * f), w.dtype)
        r[:, :, 0:h] = w.transpose(1, 0, 2)
        return r.reshape(c, e * k * f)

    def downs(w, k, f):
        e, h, c = w.shape
        r = np.zeros((e, k * f, c), w.dtype)
        r[:, 0:h, :] = w
        return r.reshape(e * f, k, c).transpose(1, 0, 2)

    for m in range(3):
        e, k, f = MOES[m]
        give(f"up{m}", ups(i[f"L{m}_ffn_W1"], k, f))
        give(f"ub{m}", i[f"L{m}_ffn_b1"].reshape(e * f, k).T)
        give(f"dn{m}", downs(i[f"L{m}_ffn_W2"], k, f))
        give(f"db{m}", i[f"L{m}_ffn_b2"])
    e, k, f = L3F
    up3 = [ups(i[f"L3_ffn_{w}"].transpose(0, 2, 1), k, f) for w in ("w1", "w3")]
    give("up3", np.concatenate(up3 + [np.zeros((C, UP3 - 2 * UP3H), up3[0].dtype)], 1))
    dn3 = downs(i["L3_ffn_w2"].transpose(0, 2, 1), k, f).reshape(k, DN3)
    give("dn3", np.concatenate([dn3, np.zeros((P - k, DN3), dn3.dtype)]))
    give("gw0", i["L0_ffn_Wg"])
    give("gw1", i["L1_ffn_Wr"])
    give("gw2", i["L2_ffn_W_gat"])
    give("gw3", i["L3_ffn_router_w"].T)
    give("gb0", i["L0_ffn_bg"])
    give("gb1", i["L1_ffn_br"])
    give("rhs", i["L1_conv_rhs"].transpose(3, 1, 0, 2).reshape(C, 9 * C))
    give("gam1", i["L1_ffn_gamma"])
    give("bet1", i["L1_ffn_beta"])
    give("se1", i["L2_conv_w1"])
    give("se1b", i["L2_conv_b1"].reshape(4, 1))
    give("se2", i["L2_conv_w2"])
    give("se2b", i["L2_conv_b2"])
    give("att_src", i["L2_ffn_att_src"].reshape(16))
    give("att_dst", i["L2_ffn_att_dst"].reshape(16))
    give("b_gat", i["L2_ffn_b_gat"])
    give("gat_g", i["L2_ffn_ln_gamma"])
    give("gat_b", i["L2_ffn_ln_beta"])
    give("wavelet", i["L3_conv_h"])

    def masks(n, copies):
        half = n // 2
        m = np.zeros((n, FT, n), np.float32)
        for o in range(n):
            for k in range(FT):
                if (o + k) % 2:
                    at = ((o + k - 1) // 2 - (FT // 2 - 1)) % half
                    m[at, FT - 1 - k, o] = 1.0
                    m[half + at, k, o] = 1.0 if k % 2 else -1.0
        r = np.zeros((copies, n, FT, copies, n), np.float32)
        for c in range(copies):
            r[c, :, :, c, :] = m
        return r.reshape(copies * n, FT, copies * n)

    give("maskH", masks(H, B))
    give("maskC", masks(C, 1))
    out = nc.dram_tensor("out_x", (P, NT, C), F32, kind="ExternalOutput").ap()
    build_program(nc, aps, out)
    r = run(nc, [arrays], core_ids=[0])
    return np.asarray(r.results[0]["out_x"]).reshape(B, H, W, C)
```
